# Optimizing a Trainium2 kernel written in Bass

```python
import numpy as np
import jax
import jax.numpy as jnp

def _softmax(x, axis=-1):
    return jax.nn.softmax(x, axis=axis)

def _gelu(x):
    return jax.nn.gelu(x, approximate=True)

def _silu(x):
    return jax.nn.silu(x)

def _sigmoid(x):
    return jax.nn.sigmoid(x)

def _layernorm(x, axis=-1, eps=1e-05):
    m = jnp.mean(x, axis=axis, keepdims=True)
    v = jnp.var(x, axis=axis, keepdims=True)
    return (x - m) / jnp.sqrt(v + eps)

def _scatter_add(tgt, idx, src, axis=0):
    return tgt.at[idx].add(src)

def _segment_sum(src, seg, n):
    return jax.ops.segment_sum(src, seg, n)
kernel_name = 'mk_cond_seq_d4_seqx_r8_4a6dd3'

def setup_inputs(seed: int=0):
    np.random.seed(seed)
    _w = jnp.asarray

    def _rec_inputs():
        import jax
        import jax.numpy as jnp
        _rk = jax.random.key(seed)
        x = -9.26e-05 + 0.9999 * jax.random.normal(jax.random.fold_in(_rk, 1), (32, 32, 144), jnp.float32)
        _lenS = 32 - jax.random.randint(jax.random.fold_in(_rk, 7), (32,), 0, max(1, 32 // 4) + 1, jnp.int32)
        _lenS2 = 32 - jax.random.randint(jax.random.fold_in(_rk, 8), (32,), 0, max(1, 32 // 4) + 1, jnp.int32)
        cond_1152 = 0.00338249 + 1.00093 * jax.random.normal(jax.random.fold_in(_rk, 11), (32, 144), jnp.float32)
        return (x, cond_1152)
    x, cond_1152 = _rec_inputs()

    def _L0_cond_setup():
        import jax, jax.numpy as jnp
        import numpy as np
        N, T, D, H = (32, 128, 144, 16)
        DH = D // H
        MLP = int(D * 4.0)
        EPS = 1e-06

        def _layernorm(x):
            m = jnp.mean(x, axis=-1, keepdims=True)
            v = jnp.var(x, axis=-1, keepdims=True)
            return (x - m) * jax.lax.rsqrt(v + EPS)

        def _modulate(x, shift, scale):
            return x * (1.0 + scale[:, None, :]) + shift[:, None, :]

        def _attention(x, qkv_w, qkv_b, proj_w, proj_b):
            n, t, d = x.shape
            scale = DH ** (-0.5)
            qkv = x @ qkv_w + qkv_b
            qkv = qkv.reshape(n, t, 3, H, DH)
            q, k, v = (qkv[:, :, 0], qkv[:, :, 1], qkv[:, :, 2])
            attn = jnp.einsum('nthd,ntkd->nthk', q * scale, k)
            attn = jax.nn.softmax(attn, axis=-1)
            out = jnp.einsum('nthk,ntkd->nthd', attn, v)
            out = out.transpose(0, 2, 1, 3).reshape(n, t, d)
            return out @ proj_w + proj_b

        def _mlp(x, fc1_w, fc1_b, fc2_w, fc2_b):
            h = jax.nn.gelu(x @ fc1_w + fc1_b, approximate=False)
            return h @ fc2_w + fc2_b
        key = jax.random.key(seed)
        ks = jax.random.split(key, 14)
        s = 0.02
        return {'x': jax.random.normal(ks[0], (N, T, D), jnp.float32), 'c': jax.random.normal(ks[1], (N, D), jnp.float32), 'qkv_w': jax.random.normal(ks[2], (D, 3 * D), jnp.float32) * s, 'qkv_b': jax.random.normal(ks[3], (3 * D,), jnp.float32) * s, 'proj_w': jax.random.normal(ks[4], (D, D), jnp.float32) * s, 'proj_b': jax.random.normal(ks[5], (D,), jnp.float32) * s, 'fc1_w': jax.random.normal(ks[6], (D, MLP), jnp.float32) * s, 'fc1_b': jax.random.normal(ks[7], (MLP,), jnp.float32) * s, 'fc2_w': jax.random.normal(ks[8], (MLP, D), jnp.float32) * s, 'fc2_b': jax.random.normal(ks[9], (D,), jnp.float32) * s, 'ada_w': jax.random.normal(ks[10], (D, 6 * D), jnp.float32) * s, 'ada_b': jax.random.normal(ks[11], (6 * D,), jnp.float32) * s}
    _L0_cond_all = _L0_cond_setup()
    _L0_cond_in = {k: v for k, v in _L0_cond_all.items() if k in ('qkv_w', 'qkv_b', 'proj_w', 'proj_b', 'fc1_w', 'fc1_b', 'fc2_w', 'fc2_b', 'ada_w', 'ada_b')}
    del _L0_cond_all

    def _L1_cond_setup():
        import jax, jax.numpy as jnp
        import numpy as np
        HID = 144
        HEADS = 16
        HD = HID // HEADS
        MLP = int(HID * 4.0)

        def _ln(x, eps, gamma=None, beta=None):
            mu = jnp.mean(x, axis=-1, keepdims=True)
            var = jnp.mean(jnp.square(x - mu), axis=-1, keepdims=True)
            y = (x - mu) / jnp.sqrt(var + eps)
            if gamma is not None:
                y = y * gamma + beta
            return y
        key = jax.random.key(seed)
        ks = jax.random.split(key, 12)
        B, N, C = (8, 128, HID)
        s = lambda k, *sh: jax.random.normal(k, sh, dtype=jnp.float32) * 0.02
        return {'x': jax.random.normal(ks[0], (B, N, C), dtype=jnp.float32), 'c': jax.random.normal(ks[1], (B, C), dtype=jnp.float32), 'w_qkv': s(ks[2], C, 3 * C), 'b_qkv': jnp.zeros((3 * C,), jnp.float32), 'w_proj': s(ks[3], C, C), 'b_proj': jnp.zeros((C,), jnp.float32), 'qn_g': jnp.ones((HD,), jnp.float32), 'qn_b': jnp.zeros((HD,), jnp.float32), 'kn_g': jnp.ones((HD,), jnp.float32), 'kn_b': jnp.zeros((HD,), jnp.float32), 'w1': s(ks[4], C, MLP), 'b1': jnp.zeros((MLP,), jnp.float32), 'w2': s(ks[5], MLP, C), 'b2': jnp.zeros((C,), jnp.float32), 'w_ada': s(ks[6], C, 6 * C), 'b_ada': jnp.zeros((6 * C,), jnp.float32)}
    _L1_cond_all = _L1_cond_setup()
    _L1_cond_in = {k: v for k, v in _L1_cond_all.items() if k in ('w_qkv', 'b_qkv', 'w_proj', 'b_proj', 'qn_g', 'qn_b', 'kn_g', 'kn_b', 'w1', 'b1', 'w2', 'b2', 'w_ada', 'b_ada')}
    del _L1_cond_all

    def _L2_cond_setup():
        import jax, jax.numpy as jnp
        import numpy as np
        from jax.scipy.linalg import expm
        N, D, COND_DIM = (144, 64, 144)
        B, T = (16, 128)

        def _rotation(cond, W, b):
            v = jax.nn.silu(cond) @ W.T + b
            iu, ju = jnp.triu_indices(D, k=1)
            A = jnp.zeros((cond.shape[0], D, D), dtype=v.dtype)
            A = A.at[:, iu, ju].set(v).at[:, ju, iu].set(-v)
            return expm(A)
        key = jax.random.key(seed)
        k1, k2, k3, k4, k5 = jax.random.split(key, 5)
        x = jax.random.normal(k1, (B, T, N), dtype=jnp.float32)
        cond = jax.random.normal(k2, (B, COND_DIM), dtype=jnp.float32)
        P = jax.random.normal(k3, (N, D), dtype=jnp.float32)
        n_skew = D * (D - 1) // 2
        bound = 1.0 / np.sqrt(COND_DIM)
        W = jax.random.uniform(k4, (n_skew, COND_DIM), minval=-bound, maxval=bound, dtype=jnp.float32)
        b = jax.random.uniform(k5, (n_skew,), minval=-bound, maxval=bound, dtype=jnp.float32)
        return {'x': x, 'cond': cond, 'P': P, 'W': W, 'b': b}
    _L2_cond_all = _L2_cond_setup()
    _L2_cond_in = {k: v for k, v in _L2_cond_all.items() if k in ('P', 'W', 'b')}
    del _L2_cond_all

    def _L3_cond_setup():
        import jax, jax.numpy as jnp
        import numpy as np
        B, L, C = (8, 128, 144)
        H = 16
        D = C // H
        FF = int(C * 4.0)
        EPS = 1e-06

        def _layernorm(x):
            mu = jnp.mean(x, axis=-1, keepdims=True)
            var = jnp.mean(jnp.square(x - mu), axis=-1, keepdims=True)
            return (x - mu) * jax.lax.rsqrt(var + EPS)

        def _modulate(x, shift, scale):
            return x * (1.0 + scale) + shift

        def _attention(h, W_qkv, b_qkv, W_proj, b_proj):
            b, l, c = h.shape
            qkv = h @ W_qkv + b_qkv
            qkv = qkv.reshape(b, l, 3, H, D)
            q, k, v = (qkv[:, :, 0], qkv[:, :, 1], qkv[:, :, 2])
            scale = D ** (-0.5)
            scores = jnp.einsum('blhd,bmhd->bhlm', q * scale, k)
            attn = jax.nn.softmax(scores, axis=-1)
            o = jnp.einsum('bhlm,bmhd->blhd', attn, v).reshape(b, l, c)
            return o @ W_proj + b_proj
        key = jax.random.key(seed)
        ks = jax.random.split(key, 12)
        s = 0.02
        return {'x': jax.random.normal(ks[0], (B, L, C), jnp.float32), 'c': jax.random.normal(ks[1], (B, 1, C), jnp.float32), 'W_qkv': jax.random.normal(ks[2], (C, 3 * C), jnp.float32) * s, 'b_qkv': jnp.zeros((3 * C,), jnp.float32), 'W_proj': jax.random.normal(ks[3], (C, C), jnp.float32) * s, 'b_proj': jnp.zeros((C,), jnp.float32), 'W_fc1': jax.random.normal(ks[4], (C, FF), jnp.float32) * s, 'b_fc1': jnp.zeros((FF,), jnp.float32), 'W_fc2': jax.random.normal(ks[5], (FF, C), jnp.float32) * s, 'b_fc2': jnp.zeros((C,), jnp.float32), 'W_ada': jax.random.normal(ks[6], (C, 6 * C), jnp.float32) * s, 'b_ada': jnp.zeros((6 * C,), jnp.float32)}
    _L3_cond_all = _L3_cond_setup()
    _L3_cond_in = {k: v for k, v in _L3_cond_all.items() if k in ('W_qkv', 'b_qkv', 'W_proj', 'b_proj', 'W_fc1', 'b_fc1', 'W_fc2', 'b_fc2', 'W_ada', 'b_ada')}
    del _L3_cond_all
    return {'x': x, 'cond_1152': cond_1152, 'L0_cond_qkv_w': _L0_cond_in['qkv_w'], 'L0_cond_qkv_b': _L0_cond_in['qkv_b'], 'L0_cond_proj_w': _L0_cond_in['proj_w'], 'L0_cond_proj_b': _L0_cond_in['proj_b'], 'L0_cond_fc1_w': _L0_cond_in['fc1_w'], 'L0_cond_fc1_b': _L0_cond_in['fc1_b'], 'L0_cond_fc2_w': _L0_cond_in['fc2_w'], 'L0_cond_fc2_b': _L0_cond_in['fc2_b'], 'L0_cond_ada_w': _L0_cond_in['ada_w'], 'L0_cond_ada_b': _L0_cond_in['ada_b'], 'L1_cond_w_qkv': _L1_cond_in['w_qkv'], 'L1_cond_b_qkv': _L1_cond_in['b_qkv'], 'L1_cond_w_proj': _L1_cond_in['w_proj'], 'L1_cond_b_proj': _L1_cond_in['b_proj'], 'L1_cond_qn_g': _L1_cond_in['qn_g'], 'L1_cond_qn_b': _L1_cond_in['qn_b'], 'L1_cond_kn_g': _L1_cond_in['kn_g'], 'L1_cond_kn_b': _L1_cond_in['kn_b'], 'L1_cond_w1': _L1_cond_in['w1'], 'L1_cond_b1': _L1_cond_in['b1'], 'L1_cond_w2': _L1_cond_in['w2'], 'L1_cond_b2': _L1_cond_in['b2'], 'L1_cond_w_ada': _L1_cond_in['w_ada'], 'L1_cond_b_ada': _L1_cond_in['b_ada'], 'L2_cond_P': _L2_cond_in['P'], 'L2_cond_W': _L2_cond_in['W'], 'L2_cond_b': _L2_cond_in['b'], 'L3_cond_W_qkv': _L3_cond_in['W_qkv'], 'L3_cond_b_qkv': _L3_cond_in['b_qkv'], 'L3_cond_W_proj': _L3_cond_in['W_proj'], 'L3_cond_b_proj': _L3_cond_in['b_proj'], 'L3_cond_W_fc1': _L3_cond_in['W_fc1'], 'L3_cond_b_fc1': _L3_cond_in['b_fc1'], 'L3_cond_W_fc2': _L3_cond_in['W_fc2'], 'L3_cond_b_fc2': _L3_cond_in['b_fc2'], 'L3_cond_W_ada': _L3_cond_in['W_ada'], 'L3_cond_b_ada': _L3_cond_in['b_ada']}

def reference(x, cond_1152, L0_cond_qkv_w, L0_cond_qkv_b, L0_cond_proj_w, L0_cond_proj_b, L0_cond_fc1_w, L0_cond_fc1_b, L0_cond_fc2_w, L0_cond_fc2_b, L0_cond_ada_w, L0_cond_ada_b, L1_cond_w_qkv, L1_cond_b_qkv, L1_cond_w_proj, L1_cond_b_proj, L1_cond_qn_g, L1_cond_qn_b, L1_cond_kn_g, L1_cond_kn_b, L1_cond_w1, L1_cond_b1, L1_cond_w2, L1_cond_b2, L1_cond_w_ada, L1_cond_b_ada, L2_cond_P, L2_cond_W, L2_cond_b, L3_cond_W_qkv, L3_cond_b_qkv, L3_cond_W_proj, L3_cond_b_proj, L3_cond_W_fc1, L3_cond_b_fc1, L3_cond_W_fc2, L3_cond_b_fc2, L3_cond_W_ada, L3_cond_b_ada):
    import jax
    import jax.numpy as jnp

    def _L0_cond_ref(x, c, qkv_w, qkv_b, proj_w, proj_b, fc1_w, fc1_b, fc2_w, fc2_b, ada_w, ada_b):
        import jax, jax.numpy as jnp
        import numpy as np
        N, T, D, H = (32, 128, 144, 16)
        DH = D // H
        MLP = int(D * 4.0)
        EPS = 1e-06

        def _layernorm(x):
            m = jnp.mean(x, axis=-1, keepdims=True)
            v = jnp.var(x, axis=-1, keepdims=True)
            return (x - m) * jax.lax.rsqrt(v + EPS)

        def _modulate(x, shift, scale):
            return x * (1.0 + scale[:, None, :]) + shift[:, None, :]

        def _attention(x, qkv_w, qkv_b, proj_w, proj_b):
            n, t, d = x.shape
            scale = DH ** (-0.5)
            qkv = x @ qkv_w + qkv_b
            qkv = qkv.reshape(n, t, 3, H, DH)
            q, k, v = (qkv[:, :, 0], qkv[:, :, 1], qkv[:, :, 2])
            attn = jnp.einsum('nthd,ntkd->nthk', q * scale, k)
            attn = jax.nn.softmax(attn, axis=-1)
            out = jnp.einsum('nthk,ntkd->nthd', attn, v)
            out = out.transpose(0, 2, 1, 3).reshape(n, t, d)
            return out @ proj_w + proj_b

        def _mlp(x, fc1_w, fc1_b, fc2_w, fc2_b):
            h = jax.nn.gelu(x @ fc1_w + fc1_b, approximate=False)
            return h @ fc2_w + fc2_b
        ada = jax.nn.silu(c) @ ada_w + ada_b
        shift_msa, scale_msa, gate_msa, shift_mlp, scale_mlp, gate_mlp = jnp.split(ada, 6, axis=1)
        x = x + gate_msa[:, None, :] * _attention(_modulate(_layernorm(x), shift_msa, scale_msa), qkv_w, qkv_b, proj_w, proj_b)
        x = x + gate_mlp[:, None, :] * _mlp(_modulate(_layernorm(x), shift_mlp, scale_mlp), fc1_w, fc1_b, fc2_w, fc2_b)
        return x

    def _L1_cond_ref(x, c, w_qkv, b_qkv, w_proj, b_proj, qn_g, qn_b, kn_g, kn_b, w1, b1, w2, b2, w_ada, b_ada):
        import jax, jax.numpy as jnp
        import numpy as np
        HID = 144
        HEADS = 16
        HD = HID // HEADS
        MLP = int(HID * 4.0)

        def _ln(x, eps, gamma=None, beta=None):
            mu = jnp.mean(x, axis=-1, keepdims=True)
            var = jnp.mean(jnp.square(x - mu), axis=-1, keepdims=True)
            y = (x - mu) / jnp.sqrt(var + eps)
            if gamma is not None:
                y = y * gamma + beta
            return y
        B, N, C = x.shape
        H, hd = (HEADS, HD)
        scale = hd ** (-0.5)
        mod = jax.nn.silu(c) @ w_ada + b_ada
        sh_msa, sc_msa, g_msa, sh_mlp, sc_mlp, g_mlp = jnp.split(mod, 6, axis=1)
        xn = _ln(x, 1e-06)
        xn = xn * (1 + sc_msa[:, None, :]) + sh_msa[:, None, :]
        qkv = (xn @ w_qkv + b_qkv).reshape(B, N, 3, H, hd)
        q, k, v = (qkv[:, :, 0], qkv[:, :, 1], qkv[:, :, 2])
        q = _ln(q, 1e-05, qn_g, qn_b)
        k = _ln(k, 1e-05, kn_g, kn_b)
        attn = jnp.einsum('bqhd,bkhd->bhqk', q, k) * scale
        attn = jax.nn.softmax(attn, axis=-1)
        o = jnp.einsum('bhqk,bkhd->bqhd', attn, v).reshape(B, N, C)
        o = o @ w_proj + b_proj
        x = x + g_msa[:, None, :] * o
        xn2 = _ln(x, 1e-06)
        xn2 = xn2 * (1 + sc_mlp[:, None, :]) + sh_mlp[:, None, :]
        h = jax.nn.gelu(xn2 @ w1 + b1, approximate=False)
        m = h @ w2 + b2
        x = x + g_mlp[:, None, :] * m
        return x

    def _L2_cond_ref(x, cond, P, W, b):
        import jax, jax.numpy as jnp
        import numpy as np
        from jax.scipy.linalg import expm
        N, D, COND_DIM = (144, 64, 144)
        B, T = (16, 128)

        def _rotation(cond, W, b):
            v = jax.nn.silu(cond) @ W.T + b
            iu, ju = jnp.triu_indices(D, k=1)
            A = jnp.zeros((cond.shape[0], D, D), dtype=v.dtype)
            A = A.at[:, iu, ju].set(v).at[:, ju, iu].set(-v)
            return expm(A)
        U, _ = jnp.linalg.qr(P)
        R = _rotation(cond, W, b)
        z = jnp.einsum('btn,nd->btd', x, U)
        z_rot = jnp.einsum('btd,bde->bte', z, R)
        x_rot = x + jnp.einsum('btd,nd->btn', z_rot - z, U)
        return x_rot

    def _L3_cond_ref(x, c, W_qkv, b_qkv, W_proj, b_proj, W_fc1, b_fc1, W_fc2, b_fc2, W_ada, b_ada):
        import jax, jax.numpy as jnp
        import numpy as np
        B, L, C = (8, 128, 144)
        H = 16
        D = C // H
        FF = int(C * 4.0)
        EPS = 1e-06

        def _layernorm(x):
            mu = jnp.mean(x, axis=-1, keepdims=True)
            var = jnp.mean(jnp.square(x - mu), axis=-1, keepdims=True)
            return (x - mu) * jax.lax.rsqrt(var + EPS)

        def _modulate(x, shift, scale):
            return x * (1.0 + scale) + shift

        def _attention(h, W_qkv, b_qkv, W_proj, b_proj):
            b, l, c = h.shape
            qkv = h @ W_qkv + b_qkv
            qkv = qkv.reshape(b, l, 3, H, D)
            q, k, v = (qkv[:, :, 0], qkv[:, :, 1], qkv[:, :, 2])
            scale = D ** (-0.5)
            scores = jnp.einsum('blhd,bmhd->bhlm', q * scale, k)
            attn = jax.nn.softmax(scores, axis=-1)
            o = jnp.einsum('bhlm,bmhd->blhd', attn, v).reshape(b, l, c)
            return o @ W_proj + b_proj
        ada = jax.nn.silu(c) @ W_ada + b_ada
        shift_msa, scale_msa, gate_msa, shift_mlp, scale_mlp, gate_mlp = jnp.split(ada, 6, axis=-1)
        h = _modulate(_layernorm(x), shift_msa, scale_msa)
        x = x + gate_msa * _attention(h, W_qkv, b_qkv, W_proj, b_proj)
        h = _modulate(_layernorm(x), shift_mlp, scale_mlp)
        mlp = jax.nn.gelu(h @ W_fc1 + b_fc1, approximate=True) @ W_fc2 + b_fc2
        x = x + gate_mlp * mlp
        return x
    x = _L0_cond_ref(x, cond_1152, L0_cond_qkv_w, L0_cond_qkv_b, L0_cond_proj_w, L0_cond_proj_b, L0_cond_fc1_w, L0_cond_fc1_b, L0_cond_fc2_w, L0_cond_fc2_b, L0_cond_ada_w, L0_cond_ada_b)
    x = _L1_cond_ref(x, cond_1152, L1_cond_w_qkv, L1_cond_b_qkv, L1_cond_w_proj, L1_cond_b_proj, L1_cond_qn_g, L1_cond_qn_b, L1_cond_kn_g, L1_cond_kn_b, L1_cond_w1, L1_cond_b1, L1_cond_w2, L1_cond_b2, L1_cond_w_ada, L1_cond_b_ada)
    x = _L2_cond_ref(x, cond_1152, L2_cond_P, L2_cond_W, L2_cond_b)
    x = _L3_cond_ref(x, cond_1152[:, None, :], L3_cond_W_qkv, L3_cond_b_qkv, L3_cond_W_proj, L3_cond_b_proj, L3_cond_W_fc1, L3_cond_b_fc1, L3_cond_W_fc2, L3_cond_b_fc2, L3_cond_W_ada, L3_cond_b_ada)
    return x

_drawn_inputs = setup_inputs


def setup_inputs(seed=0):
    import zlib

    import numpy as np

    out = dict(_drawn_inputs(seed))
    spreads = {'L1_cond_b_qkv': (0.0, 0.8),
     'L1_cond_b_proj': (0.0, 0.497),
     'L1_cond_qn_g': (1.0, 0.6),
     'L1_cond_qn_b': (0.0, 0.8),
     'L1_cond_kn_g': (1.0, 0.6),
     'L1_cond_kn_b': (0.0, 2.0),
     'L1_cond_b1': (0.0, 0.8),
     'L1_cond_b2': (0.0, 0.478),
     'L1_cond_b_ada': (0.0, 0.554),
     'L3_cond_b_qkv': (0.0, 0.8),
     'L3_cond_b_proj': (0.0, 0.438),
     'L3_cond_b_fc1': (0.0, 0.8),
     'L3_cond_b_fc2': (0.0, 0.466),
     'L3_cond_b_ada': (0.0, 0.491)}
    factors = {'L0_cond_qkv_w': 8.0,
     'L0_cond_qkv_b': 8.0,
     'L0_cond_proj_w': 8.0,
     'L0_cond_proj_b': 8.0,
     'L0_cond_fc1_w': 6.696,
     'L0_cond_fc1_b': 8.0,
     'L0_cond_fc2_w': 6.576,
     'L0_cond_fc2_b': 22.512,
     'L0_cond_ada_w': 5.799,
     'L0_cond_ada_b': 8.0,
     'L1_cond_w_qkv': 8.0,
     'L1_cond_w_proj': 8.0,
     'L1_cond_w1': 5.355,
     'L1_cond_w2': 4.858,
     'L3_cond_W_qkv': 8.0,
     'L3_cond_W_proj': 8.0,
     'L3_cond_W_fc1': 5.289,
     'L3_cond_W_fc2': 4.729}
    for name, (base, spread) in spreads.items():
        noise = np.random.default_rng([zlib.crc32(name.encode()), seed]).standard_normal(out[name].shape)
        drawn = base * np.exp(spread * noise) if base else spread * noise
        out[name] = jnp.asarray(drawn.astype(out[name].dtype))
    for name, factor in factors.items():
        out[name] = (out[name] * factor).astype(out[name].dtype)
    return out
```

```python
from contextlib import ExitStack
from math import factorial

import numpy as np

import concourse.bass as bass
from concourse import mybir

F32 = mybir.dt.float32
ALU = mybir.AluOpType
ACT = mybir.ActivationFunctionType
AX = mybir.AxisListType

P = 128
SEQ, TOK, D = 32, 32, 144
T = SEQ * TOK // P
B = P // TOK
C = D // 2
HEADS, DH = 16, 9
HC = HEADS // 2
QKV = 3 * D
VW = DH + 1
G4 = 4
MLP = 4 * D
MC = 5
HT = T // 2
HTOK = HT * P
R = 64
PAIRS = SEQ // 2
SQUARINGS = 5
EPS, QK_EPS = 1e-6, 1e-5
NB = 3


def fused_blocks(nc, x_in, cond_t, ada_w, qkv_w, proj_w, fc1_w, fc2_w, qk_gb, rot_w, p_in, pt_in,
                 eye, head_mask, below, seq_mask, skew, out):
    with ExitStack() as ctx:
        def sb(name, shape):
            return ctx.enter_context(nc.sbuf_tensor(name, shape, F32))

        def sem(name):
            return ctx.enter_context(nc.semaphore(name))

        ps = ctx.enter_context(nc.psum_tensor("ps", [P, 8, 512], F32))

        x = sb("x", [P, T, D])
        xn = sb("xn", [P, T, D])
        xmT = sb("xmT", [P, 2, T * P])
        qkv = sb("qkv", [P, T, QKV])
        qT = sb("qT", [C, 2, T * P])
        kT = sb("kT", [C, 4 * P])
        kexp = sb("kexp", [P, 2, 2, 2 * B, HC, TOK])
        vexp = sb("vexp", [P, SEQ, 4, G4 * VW])
        probs = sb("probs", [P, 2, HEADS * TOK])
        probsT = sb("probsT", [P, 2, HEADS * TOK])
        rowmax = sb("rowmax", [P, 2, HEADS])
        rinv = sb("rinv", [P, 2, HEADS])
        o = sb("o", [P, 2, D])
        oT = sb("oT", [P, 2, 2, P])
        delta = sb("delta", [P, 4, D])
        hT = sb("hT", [P, MC, T * P])
        gates = sb("gates", [P, NB, T, 2, D])
        mod = sb("mod", [C, NB, 4, 2, SEQ])
        bn = sb("bn", [P, T, 6])
        mv = sb("mv", [P, T, 2])
        rstd = sb("rstd", [P, T])
        veps = sb("veps", [P, T])
        qk_sum = sb("qk_sum", [P, 4 * 2 * HEADS])
        qk_mean = sb("qk_mean", [P, 4 * 2 * HEADS])
        qk_rs = sb("qk_rs", [P, 4 * 2 * HEADS])
        wq = sb("wq", [C + 1, 2, 2, QKV])
        wp = sb("wp", [C + 1, 2, 2, D])
        w1 = sb("w1", [C + 1, 2, 2, MLP])
        w2 = sb("w2", [P, 2, MC, D])
        ident = sb("ident", [P, P])
        kmask = sb("kmask", [C, HC])
        kscale = sb("kscale", [C, HC])
        kbias = sb("kbias", [C, HC])
        gb = sb("gb", [C, 4])
        half_neg = sb("half_neg", [P, 1])
        cT = sb("cT", [C, 2, SEQ])
        sT = sb("sT", [P, 2, SEQ])
        neg_below = sb("neg_below", [R, R])
        W = sb("W", [R, R])
        M = sb("M", [R, R])
        fcol = sb("fcol", [R, R])
        RD = sb("RD", [R, R])
        SG = sb("SG", [R, R])
        piv = sb("piv", [R, 4])
        dg = sb("dg", [R, 4])
        LiT = sb("LiT", [R, R])
        PT = sb("PT", [R, D])
        Pm = sb("Pm", [C, 2, R])
        UT = sb("UT", [R, D])
        U = sb("U", [C, 2, 2, R])
        sgn = sb("sgn", [P, R])
        EG = sb("EG", [P, 2, PAIRS, R])
        A, A2 = EG[:, 0], EG[:, 1]
        A3 = sb("A3", [P, PAIRS, R])
        EF = sb("EF", [P, 2, PAIRS, R])
        pol = EF[:, 1]
        kexp_flat = kexp[:].rearrange("p a c b h k -> p (a c b h k)")
        rotw = kexp_flat[0:C + 1].rearrange("p (c n) -> p c n", c=2)
        NP = HEADS * HEADS * DH
        prod_qk = kexp_flat[:, 0:NP]
        prod_pv = kexp_flat[:, NP:2 * NP]
        o_heads = kexp_flat[:, 2 * NP:2 * NP + 2 * D].rearrange("p (i f) -> p i f", i=2)
        vsb = vexp[:].rearrange("p a b c -> p (a b c)")[:, 0:1024].rearrange("p (r n) -> p r n", r=2)
        spread_seq = vexp[:].rearrange("p a b c -> p (a b c)")[0:SEQ, 1024:1024 + T * P]
        gsb = vexp[:].rearrange("p a b c -> p (a b c)")[0:SEQ, 2048:2048 + 4 * D].rearrange("p (l n) -> p l n", l=2)
        adaw = hT[:].rearrange("p a b -> p (a b)")[0:C + 1, 0:2 * 2 * 6 * D].rearrange(
            "p (l c n) -> p l c n", l=2, c=2)
        xn_flat = xn[:].rearrange("p a b -> p (a b)")
        xn_z = xn_flat[:, 0:HTOK]
        xn_y = xn_flat[:, HTOK:2 * HTOK]
        o_dram = nc.dram_tensor("o_scratch", (SEQ, HEADS, TOK, DH), F32, kind="Internal").ap()
        v_dram = nc.dram_tensor("v_scratch", (R, SEQ, R), F32, kind="Internal").ap()

        ld_const, ld_cond, ld_x, ld_p = sem("ld_const"), sem("ld_cond"), sem("ld_x"), sem("ld_p")
        ld_ada = [sem(f"ld_ada{n}") for n in range(NB)]
        ld_rot, ld_v, st_v = sem("ld_rot"), sem("ld_v"), sem("st_v")
        ld_w = [sem(f"ld_w{n}") for n in range(NB)]
        silu_done, ones_set, ada_ps, ada_sb = sem("silu_done"), sem("ones_set"), sem("ada_ps"), sem("ada_sb")
        gate_ps, gate_sb = sem("gate_ps"), sem("gate_sb")
        v_ps, v_sb = sem("v_ps"), sem("v_sb")
        dve = sem("dve")
        act_own = sem("act_own")
        pool_own = sem("pool_own")
        gram_ps, w_ready, bc_ps, m_ready = sem("gram_ps"), sem("w_ready"), sem("bc_ps"), sem("m_ready")
        lit_in, lit_ps, lit_sb, ut_ps, ut_ready, u_ps, u_sb = (
            sem(s) for s in ("lit_in", "lit_ps", "lit_sb", "ut_ps", "ut_ready", "u_ps", "u_sb"))
        diag_ready, isd_ready = sem("diag_ready"), sem("isd_ready")
        a_ready, ex_ps, ex_act, ex_dve = sem("a_ready"), sem("ex_ps"), sem("ex_act"), sem("ex_dve")
        stats_ready, rstd_ready, xn_ready = sem("stats_ready"), sem("rstd_ready"), sem("xn_ready")
        xnT_ps, mod_done = sem("xnT_ps"), sem("mod_done")
        qkv_ps, qkv_sb = sem("qkv_ps"), sem("qkv_sb")
        qk_xc, qk_sq, qk_ss, qk_rstd, qk_norm = (sem(s) for s in ("qk_xc", "qk_sq", "qk_ss", "qk_rstd", "qk_norm"))
        v_spread = sem("v_spread")
        qkT_ps, q_sb, k_sb, k_act, k_dve = sem("qkT_ps"), sem("q_sb"), sem("k_sb"), sem("k_act"), sem("k_dve")
        s_ps, max_done, sub_done, exp_done = sem("s_ps"), sem("max_done"), sem("sub_done"), sem("exp_done")
        pT_ps, pT_sb, o_ps, o_sb = sem("pT_ps"), sem("pT_sb"), sem("o_ps"), sem("o_sb")
        oT_ps, oT_sb, pr_ps, gated1, x_mid = sem("oT_ps"), sem("oT_sb"), sem("pr_ps"), sem("gated1"), sem("x_mid")
        qk_prod, heads_out, o_stored = sem("qk_prod"), sem("heads_out"), sem("o_stored")
        o_back = [sem("o_back0"), sem("o_back1")]
        h_ps, gelu_done, m_ps, gated2, x_end = sem("h_ps"), sem("gelu_done"), sem("m_ps"), sem("gated2"), sem("x_end")
        xT_ps, xT_sb, z_ps, z_sb, y_ps, y_sb, d_ps, x_rot = (
            sem(s) for s in ("xT_ps", "xT_sb", "z_ps", "z_sb", "y_ps", "y_sb", "d_ps", "x_rot"))
        stored = sem("stored")

        LNS = 2 * NB
        ATT = T + 4
        K_ACT = 3

        def x_updates(n):
            return T * n

        block = ctx.enter_context(nc.Block())

        @block.sync
        def _(sp):
            sp.dma_start(ident[:], eye).then_inc(ld_const, 16)
            sp.dma_start(kmask[:], head_mask).then_inc(ld_const, 16)
            sp.dma_start(neg_below[:], below).then_inc(ld_const, 16)
            sp.dma_start(sgn[:], skew).then_inc(ld_const, 16)
            sp.dma_start(spread_seq, seq_mask).then_inc(ld_const, 16)
            sp.dma_start(gb[:], qk_gb).then_inc(ld_const, 16)
            sp.dma_start(cT[:], cond_t).then_inc(ld_cond, 16)
            for n in range(2):
                sp.dma_start(adaw[:, n], ada_w[n]).then_inc(ld_ada[n], 16)
            sp.dma_start(x[:], x_in.rearrange("(t p) f -> p t f", p=P)).then_inc(ld_x, 16)
            sp.dma_start(rotw[:], rot_w).then_inc(ld_rot, 16)
            sp.wait_ge(ada_ps, 1)
            sp.wait_ge(gate_ps, 1)
            sp.dma_start(adaw[:, 0], ada_w[2]).then_inc(ld_ada[2], 16)
            for r in range(2):
                sp.wait_ge(v_sb, r + 1)
                for q in range(B):
                    i0 = (r * B + q) * 8
                    sp.dma_start(v_dram[i0:i0 + 8].rearrange("i b j -> b i j"),
                                 vsb[32 * q:32 * q + 32, r].rearrange("b (i j) -> b i j", i=8)).then_inc(st_v, 16)
            sp.wait_ge(st_v, 16 * 2 * B)
            for p in range(2):
                sp.dma_start(EG[R * p:R * p + R, 1], v_dram[:, p:SEQ:2, :]).then_inc(ld_v, 16)
            for t in range(T):
                sp.wait_ge(heads_out, t + 1)
                for b in range(B):
                    sp.dma_start(o_dram[B * t + b].rearrange("h t d -> t h d"),
                                 o_heads[TOK * b:TOK * b + TOK, t % 2].rearrange("p (h d) -> p h d", h=HEADS)
                                 ).then_inc(o_stored, 16)
                sp.wait_ge(o_stored, 16 * B * (t + 1))
                if t >= 2:
                    sp.wait_ge(oT_ps, t - 1)
                sp.dma_start(o[:, t % 2, :], o_dram.rearrange("n h t d -> (n h t d)").rearrange(
                    "(i p f) -> i p f", p=P, f=D)[t]).then_inc(o_back[t % 2], 16)
            sp.wait_ge(m_ps, T)
            for w, src in ((wq, qkv_w), (wp, proj_w), (w1, fc1_w), (w2, fc2_w)):
                sp.dma_start(w[:, 0], src[2]).then_inc(ld_w[2], 16)
            for h in range(2):
                sp.wait_ge(x_end, T * (NB - 1) + HT * (h + 1))
                sp.dma_start(out.rearrange("(t p) f -> p t f", p=P)[:, HT * h:HT * h + HT],
                             x[:, HT * h:HT * h + HT]).then_inc(stored, 16)
            sp.wait_ge(stored, 32)

        @block.tensor
        def _(pe):
            def chunked(dst, lhs, rhs, bias=True):
                k = C + 1 if bias else C
                pe.matmul(dst, lhs(0, k), rhs(0, k), start=True, stop=False)
                return pe.matmul(dst, lhs(1, C), rhs(1, C), start=False, stop=True)

            pe.wait_ge(silu_done, 1)
            pe.wait_ge(ld_const, 16 * 6)
            for n in range(NB):
                pe.wait_ge(ld_ada[n], 16)
                if n >= 1:
                    pe.wait_ge(ada_sb, n)
                w = adaw[:, n % 2]
                for i, kind in enumerate((0, 1, 3, 4)):
                    for c in range(2):
                        col = kind * D + c * C
                        mm = chunked(ps[0:C, 0, (2 * i + c) * SEQ:(2 * i + c + 1) * SEQ],
                                     lambda kc, k: w[0:k, kc, col:col + C], lambda kc, k: sT[0:k, kc, :])
                mm.then_inc(ada_ps, 1)
                if n >= 2:
                    pe.wait_ge(gate_sb, 9 * (n - 1))
                for i, kind in enumerate((2, 5)):
                    mm = chunked(ps[0:SEQ, 1, i * D:(i + 1) * D], lambda kc, k: sT[0:k, kc, :],
                                 lambda kc, k: w[0:k, kc, kind * D:(kind + 1) * D])
                mm.then_inc(gate_ps, 1)
                for t in range(T):
                    if t == 0:
                        pe.wait_ge(gate_sb, 9 * n + 1)
                    if t >= 2:
                        pe.wait_ge(gate_sb, 9 * n + t)
                    elif n >= 1:
                        pe.wait_ge(gate_sb, 9 * n)
                    pe.matmul(ps[:, 2 + t % 2, 0:2 * D],
                              spread_seq[:, t * P:(t + 1) * P],
                              gsb[:, n % 2, :], start=True, stop=True).then_inc(gate_ps, 1)

            pe.wait_ge(ld_rot, 16)
            for r in range(2):
                for kc in range(2):
                    k = C + 1 - kc
                    for q in range(B):
                        col = (r * B + q) * 512
                        mm = pe.matmul(ps[32 * q:32 * q + 32, 4 + r, :], sT[0:k, kc, :], rotw[0:k, kc, col:col + 512],
                                       start=kc == 0, stop=kc == 1)
                mm.then_inc(v_ps, 1)

            pe.wait_ge(ld_p, 32)
            for kc in range(2):
                mm = pe.matmul(ps[0:R, 6, 0:R], Pm[:, kc, :], Pm[:, kc, :], start=kc == 0, stop=kc == 1)
            mm.then_inc(gram_ps, 1)

            def bcast_row(src, k):
                pe.matmul(ps[0:R, 7, 0:R], ident[0:R, k:k + 1].to_broadcast([R, R]), src[:, :],
                          start=True, stop=True).then_inc(bc_ps, 1)

            for k in range(R):
                pe.wait_ge(w_ready, k + 1)
                bcast_row(W, k)
            pe.wait_ge(lit_in, 1)
            pe.transpose(ps[0:R, 6, 0:R], W[:, :], ident[0:R, 0:R]).then_inc(lit_ps, 1)
            pe.wait_ge(lit_sb, 1)
            pe.matmul(ps[0:R, 6, 0:D], LiT[:, :], PT[:, :], start=True, stop=True).then_inc(ut_ps, 1)
            for k in range(R):
                pe.wait_ge(m_ready, k + 1)
                bcast_row(M, k)
            pe.wait_ge(ut_ready, 1)
            for c in range(2):
                mm = pe.transpose(ps[0:C, 6, c * R:(c + 1) * R], UT[:, c * C:(c + 1) * C], ident[0:R, 0:R])
            mm.then_inc(u_ps, 1)

            def pair_products(bank, lhs, rhs):
                for first in range(2):
                    for i in range(8):
                        for p in range(2):
                            m = (first ^ p) * 8 + i
                            row = slice(R * p, R * p + R)
                            mm = pe.matmul(ps[row, bank + m // 8, (m % 8) * R:(m % 8 + 1) * R],
                                           lhs(row, m), rhs(row, m), start=True, stop=True)
                return mm

            def mat(buf):
                return lambda row, m: buf[row, m, :]

            def half_of(buf, i):
                return lambda row, m: buf[row, i, m, :]

            pe.wait_ge(a_ready, 1)
            pair_products(0, mat(A), mat(A)).then_inc(ex_ps, 1)
            pe.wait_ge(ex_act, 1)
            pair_products(2, mat(A2), mat(A)).then_inc(ex_ps, 1)
            pe.wait_ge(ex_act, 2)
            pe.wait_ge(ex_dve, 1)
            pair_products(0, mat(A3), mat(pol)).then_inc(ex_ps, 1)
            pe.wait_ge(ex_dve, 2)
            pair_products(2, mat(A3), mat(pol)).then_inc(ex_ps, 1)
            pe.wait_ge(ex_dve, 3)
            pair_products(0, half_of(EF, 0),
                          lambda row, m: ident[row, row]).then_inc(ex_ps, 1)
            for i in range(SQUARINGS):
                src = EF if i % 2 == 0 else EG
                pe.wait_ge(ex_act, 3 + i)
                b = 2 if i % 2 == 0 else 0
                pair_products(b, half_of(src, 1), half_of(src, 0)).then_inc(ex_ps, 1)
                if i < SQUARINGS - 1:
                    pair_products(4 if i % 2 == 0 else 6, half_of(src, 0), half_of(src, 1)).then_inc(ex_ps, 1)

            def ln_transpose(i, h):
                pe.wait_ge(xn_ready, 2 * i + h + 1)
                if i >= 1:
                    pe.wait_ge(mod_done, 2 * i + h - 1)
                for t in range(HT * h, HT * h + HT):
                    for c in range(2):
                        mm = pe.transpose(ps[0:C, 2 * h + c, (t % HT) * P:(t % HT + 1) * P],
                                          xn[:, t, c * C:(c + 1) * C], ident[:, :])
                mm.then_inc(xnT_ps, 1)

            def rotate():
                pe.wait_ge(u_sb, 1)
                for h in range(2):
                    pe.wait_ge(x_end, T * 2)
                    if h == 1:
                        pe.wait_ge(xT_sb, 1)
                    for t in range(HT * h, HT * h + HT):
                        for c in range(2):
                            mm = pe.transpose(ps[0:C, c, (t % HT) * P:(t % HT + 1) * P], x[:, t, c * C:(c + 1) * C],
                                              ident[:, :])
                    mm.then_inc(xT_ps, 1)
                    pe.wait_ge(xT_sb, h + 1)
                    for c in range(2):
                        mm = pe.matmul(ps[:, 2, :], U[:, c].rearrange("p i r -> p (i r)"),
                                       xmT[0:C, c, HTOK * h:HTOK * (h + 1)], start=c == 0, stop=c == 1)
                    mm.then_inc(z_ps, 1)
                    pe.wait_ge(z_sb, h + 1)
                    for i in range(HT * B // 2):
                        for p in range(2):
                            b = HT * B * h + 2 * i + p
                            row = slice(R * p, R * p + R)
                            mm = pe.matmul(ps[0:R, 4 + p, i * TOK:(i + 1) * TOK], A3[row, b // 2, :],
                                           xn_z[row, (b % (HT * B)) * TOK:(b % (HT * B) + 1) * TOK],
                                           start=True, stop=True)
                    mm.then_inc(y_ps, 1)
                    pe.wait_ge(y_sb, h + 1)
                    for t in range(HT * h, HT * h + HT):
                        if t >= 2:
                            pe.wait_ge(x_rot, t - 1)
                        pe.matmul(ps[:, 6 + t % 2, 0:D], xn_y[0:R, (t % HT) * P:(t % HT + 1) * P], UT[:, :],
                                  start=True, stop=True).then_inc(d_ps, 1)

            for n in range(NB):
                s = n % 2
                if n == 0:
                    pe.wait_ge(ex_dve, 4)
                    pe.wait_ge(ones_set, 1)
                    pe.wait_ge(ex_act, 2 + SQUARINGS)
                if n == 2:
                    rotate()
                for h in range(2):
                    ln_transpose(2 * n, h)
                pe.wait_ge(ld_w[n], 16 * 4)
                for t in range(T):
                    pe.wait_ge(mod_done, 4 * n + t // HT + 1)
                    if t >= 4:
                        pe.wait_ge(qkv_sb, T * n + t - 3)
                    elif n >= 1:
                        pe.wait_ge(gelu_done, 2 * MC * n)
                        pe.wait_ge(gated2, T * n)
                        if n == 2:
                            pe.wait_ge(x_rot, T)
                    chunked(ps[:, 4 + t % 4, 0:QKV], lambda kc, k: xmT[0:k, kc, t * P:(t + 1) * P],
                            lambda kc, k: wq[0:k, s, kc, :]).then_inc(qkv_ps, 1)

                na = n - 1

                def sum_products(t):
                    pe.wait_ge(qk_prod, t + 1)
                    if t >= 2:
                        pe.wait_ge(sub_done, t - 1)
                    for d in range(DH):
                        mm = pe.matmul(ps[:, t % 2, 0:HEADS * HEADS], ident[:, :],
                                       prod_qk[:, d * HEADS * HEADS:(d + 1) * HEADS * HEADS],
                                       start=d == 0, stop=d == DH - 1)
                    mm.then_inc(s_ps, 1)

                def qk_transpose(p):
                    pe.wait_ge(qkv_sb, T * n + (T if p == 0 else 2 * p + 2))
                    if n == 1:
                        pe.wait_ge(qk_norm, p // 2 + 1)
                    if p >= 1:
                        pe.wait_ge(k_sb, 4 * na + p)
                    for i in range(2):
                        for c in range(2):
                            for j in range(2):
                                mm = pe.transpose(ps[0:C, 4 + i, (2 * c + j) * P:(2 * c + j + 1) * P],
                                                  qkv[:, 2 * p + j, i * D + c * C:i * D + (c + 1) * C], ident[:, :])
                    mm.then_inc(qkT_ps, 1)

                def scores(t):
                    p = t // 2
                    pe.wait_ge(q_sb, 4 * na + p + 1)
                    pe.wait_ge(k_act, 4 * na + p + 1)
                    pe.wait_ge(k_dve, 4 * na + p + 1)
                    if t >= 2:
                        pe.wait_ge(sub_done, T * n + t - 1)
                    for c in range(2):
                        for b in range(B):
                            mm = pe.matmul(ps[TOK * b:TOK * b + TOK, t % 2, c * 256:(c + 1) * 256],
                                           qT[:, c, t * P + b * TOK:t * P + (b + 1) * TOK],
                                           kexp[0:C, p % 2, c, (t % 2) * B + b, :, :],
                                           start=True, stop=True)
                    mm.then_inc(s_ps, 1)

                def probs_transpose(t):
                    pe.wait_ge(exp_done, T * n + t + 1)
                    if na or t:
                        pe.wait_ge(pT_sb, T * na + t)
                    for g in range(4):
                        mm = pe.transpose(ps[:, 2, g * P:(g + 1) * P], probs[:, t % 2, g * P:(g + 1) * P], ident[:, :])
                    mm.then_inc(pT_ps, 1)

                def values(t):
                    pe.wait_ge(pT_sb, T * na + t + 1)
                    pe.wait_ge(v_spread, 2 * na + t // HT + 1)
                    if na or t:
                        pe.wait_ge(o_sb, T * na + t)
                    if t == 0:
                        pe.wait_ge(qkv_sb, T * (n + 1))
                    for g in range(4):
                        for b in range(B):
                            mm = pe.matmul(ps[TOK * b:TOK * b + TOK, 6, g * G4 * VW:(g + 1) * G4 * VW],
                                           probsT[:, t % 2, g * P + TOK * b:g * P + TOK * b + TOK],
                                           vexp[:, B * t + b, g, :], start=True, stop=True)
                    mm.then_inc(o_ps, 1)

                def o_transpose(t):
                    if n == 0:
                        pe.wait_ge(o_back[t % 2], 16 * (t // 2 + 1))
                    else:
                        pe.wait_ge(o_sb, T * na + t + 1)
                    if n or t:
                        pe.wait_ge(oT_sb, T * n + t)
                    for c in range(2):
                        mm = pe.transpose(ps[0:C, 3, c * P:(c + 1) * P], o[:, t % 2, c * C:(c + 1) * C], ident[:, :])
                    mm.then_inc(oT_ps, 1)

                def project(t):
                    pe.wait_ge(oT_sb, T * n + t + 1)
                    if t >= 1:
                        pe.wait_ge(gated1, T * n + t)
                    chunked(ps[:, 7, 0:D], lambda kc, k: oT[0:k, t % 2, kc, :],
                            lambda kc, k: wp[0:k, s, kc, :]).then_inc(pr_ps, 1)

                if n == 0:
                    for st in range(ATT):
                        if st < T:
                            sum_products(st)
                        if 0 <= st - 3 < T:
                            o_transpose(st - 3)
                        if 0 <= st - 4 < T:
                            project(st - 4)
                else:
                    qk_transpose(0)
                for st in range(ATT if n else 0):
                    if st < T and st % 2 == 0 and st // 2 + 1 < T // 2:
                        qk_transpose(st // 2 + 1)
                    if st < T:
                        scores(st)
                    if 0 <= st - 1 < T:
                        probs_transpose(st - 1)
                    if 0 <= st - 2 < T:
                        values(st - 2)
                    if 0 <= st - 3 < T:
                        o_transpose(st - 3)
                    if 0 <= st - 4 < T:
                        project(st - 4)

                def fc1(h):
                    pe.wait_ge(mod_done, 4 * n + 2 + h + 1)
                    for m in range(MC):
                        i = MC * h + m
                        if i >= 2:
                            pe.wait_ge(gelu_done, 2 * MC * n + i - 1)
                        rows = min(P, MLP - P * m)
                        chunked(ps[0:rows, 4 + i % 2, :], lambda kc, k: w1[0:k, s, kc, m * P:m * P + rows],
                                lambda kc, k: xmT[0:k, kc, HTOK * h:HTOK * (h + 1)]).then_inc(h_ps, 1)

                def fc2(t):
                    pe.wait_ge(gelu_done, 2 * MC * n + MC * (t // HT + 1))
                    if t >= 2:
                        pe.wait_ge(gated2, T * n + t - 1)
                    else:
                        pe.wait_ge(gated1, T * (n + 1))
                    for m in range(MC):
                        rows = P if m < MC - 1 else R + 1
                        mm = pe.matmul(ps[:, 6 + t % 2, 0:D], hT[0:rows, m, t * P:(t + 1) * P], w2[0:rows, s, m, :],
                                       start=m == 0, stop=m == MC - 1)
                    mm.then_inc(m_ps, 1)

                ln_transpose(2 * n + 1, 0)
                ln_transpose(2 * n + 1, 1)
                fc1(0)
                fc1(1)
                for t in range(T):
                    fc2(t)

        @block.vector
        def _(v):
            own = [0]

            def link(ins):
                own[0] += 1
                ins.then_inc(dve, 1)
                v.wait_ge(dve, own[0])

            v.memset(xmT[64:P, :, :], 1.0)
            v.memset(oT[64:P, :, :, :], 1.0)
            link(v.memset(sT[64:P, :, :], 1.0))
            v.memset(half_neg[:], -0.5).then_inc(ones_set, 1)

            for n in range(NB):
                v.wait_ge(ada_ps, n + 1)
                src = ps[0:C, 0, 0:8 * SEQ].rearrange("p (k m) -> p k m", k=4)
                dst = mod[:, n].rearrange("p k c b -> p k (c b)")
                v.tensor_copy(dst[:, 0:4:2], src[:, 0:4:2])
                v.tensor_scalar(dst[:, 1:4:2], src[:, 1:4:2], 1.0, None, ALU.add).then_inc(ada_sb, 1)

            v.wait_ge(ld_const, 16 * 6)
            v.tensor_scalar(kscale[:], kmask[:], gb[:, 2:3], None, ALU.mult)
            v.tensor_scalar(kbias[:], kmask[:], gb[:, 3:4], None, ALU.mult)

            v.wait_ge(gram_ps, 1)
            v.tensor_copy(W[:], ps[0:R, 6, 0:R]).then_inc(w_ready, 1)
            for k in range(R):
                v.wait_ge(bc_ps, k + 1)
                link(v.reciprocal(RD[:, k:k + 1], ps[0:R, 7, k:k + 1]))
                link(v.scalar_tensor_tensor(out=fcol[:, k:k + 1], in0=W[:, k:k + 1], scalar=RD[:, k:k + 1],
                                            in1=neg_below[:, k:k + 1], op0=ALU.mult, op1=ALU.mult))
                link(v.scalar_tensor_tensor(out=W[:], in0=ps[0:R, 7, 0:R], scalar=fcol[:, k:k + 1], in1=W[:],
                                            op0=ALU.mult, op1=ALU.add))
                v.tensor_copy(W[:, k:k + 1], fcol[:, k:k + 1]).then_inc(w_ready, 1)
            v.wait_ge(w_ready, R + 1)
            v.tensor_tensor(W[:], W[:], ident[0:R, 0:R], ALU.add).then_inc(lit_in, 1)
            link(v.tensor_tensor(SG[:], RD[:], ident[0:R, 0:R], ALU.mult))
            v.tensor_reduce(dg[:, 0:1], SG[:], AX.X, ALU.add).then_inc(diag_ready, 1)
            v.wait_ge(lit_ps, 1)
            v.tensor_copy(LiT[:], ps[0:R, 6, 0:R]).then_inc(lit_sb, 1)
            v.wait_ge(ut_ps, 1)
            v.wait_ge(isd_ready, 1)
            link(v.tensor_scalar(UT[:], ps[0:R, 6, 0:D], dg[:, 1:2], None, ALU.mult))
            v.tensor_copy(M[:], UT[:, 0:R]).then_inc(m_ready, 1)
            for k in range(R):
                v.wait_ge(bc_ps, R + k + 1)
                alpha = ps[0:R, 7, k:k + 1]
                link(v.tensor_scalar(SG[:, k:k + 1], alpha, 0.0, 2.0, ALU.is_ge, ALU.mult))
                link(v.scalar_tensor_tensor(out=piv[:, 0:1], in0=SG[:, k:k + 1], scalar=-1.0, in1=alpha,
                                            op0=ALU.add, op1=ALU.add))
                link(v.reciprocal(piv[:, 1:2], piv[:, 0:1]))
                link(v.scalar_tensor_tensor(out=piv[:, 2:3], in0=M[:, k:k + 1], scalar=piv[:, 1:2],
                                            in1=neg_below[:, k:k + 1], op0=ALU.mult, op1=ALU.mult))
                v.scalar_tensor_tensor(out=M[:], in0=ps[0:R, 7, 0:R], scalar=piv[:, 2:3], in1=M[:],
                                       op0=ALU.mult, op1=ALU.add).then_inc(m_ready, 1)
                v.wait_ge(m_ready, k + 2)
            link(v.tensor_tensor(RD[:], SG[:], ident[0:R, 0:R], ALU.mult))
            link(v.tensor_reduce(dg[:, 2:3], RD[:], AX.X, ALU.add))
            link(v.tensor_scalar(dg[:, 3:4], dg[:, 2:3], -1.0, 1.0, ALU.mult, ALU.add))
            v.tensor_scalar(UT[:], UT[:], dg[:, 3:4], None, ALU.mult).then_inc(ut_ready, 1)
            v.wait_ge(u_ps, 1)
            for i in range(2):
                ins = v.tensor_copy(U[:, :, i, :], ps[0:C, 6, 0:2 * R].rearrange("p (c r) -> p c r", c=2))
            ins.then_inc(u_sb, 1)

            cf = [1.0 / factorial(i) for i in range(9)]

            def two_banks(b):
                return ps[:, b:b + 2, :].rearrange("p a (m r) -> p (a m) r", r=R)

            eye_p = [ident[R * p:R * p + R, R * p:R * p + R].unsqueeze(1).to_broadcast([R, PAIRS, R]) for p in range(2)]

            def add_eye(buf, c):
                for p in range(2):
                    ins = v.scalar_tensor_tensor(out=buf[R * p:R * p + R], in0=eye_p[p], scalar=c,
                                                 in1=buf[R * p:R * p + R], op0=ALU.mult, op1=ALU.add)
                return ins

            v.wait_ge(ld_v, 32)
            v.tensor_tensor(A, A2, sgn[:].unsqueeze(1).to_broadcast([P, PAIRS, R]), ALU.mult).then_inc(a_ready, 1)
            v.wait_ge(a_ready, 1)
            v.wait_ge(ex_act, 1)
            link(v.tensor_scalar(pol, A2, cf[8], None, ALU.mult))
            link(v.scalar_tensor_tensor(out=pol, in0=A, scalar=cf[7], in1=pol, op0=ALU.mult, op1=ALU.add))
            add_eye(pol, cf[6]).then_inc(ex_dve, 1)
            link(v.tensor_scalar(EF[:, 0], A2, cf[5], None, ALU.mult))
            link(v.scalar_tensor_tensor(out=EF[:, 0], in0=A, scalar=cf[4], in1=EF[:, 0], op0=ALU.mult, op1=ALU.add))
            link(add_eye(EF[:, 0], cf[3]))
            v.wait_ge(ex_ps, 3)
            v.scalar_tensor_tensor(out=pol, in0=two_banks(0), scalar=-1.0, in1=EF[:, 0],
                                   op0=ALU.mult, op1=ALU.add).then_inc(ex_dve, 1)
            v.wait_ge(ex_dve, 2)
            link(v.scalar_tensor_tensor(out=EF[:, 0], in0=A2, scalar=cf[2], in1=A, op0=ALU.mult, op1=ALU.add))
            link(add_eye(EF[:, 0], 1.0))
            v.wait_ge(ex_ps, 4)
            v.scalar_tensor_tensor(out=EF[:, 0], in0=two_banks(2), scalar=-1.0, in1=EF[:, 0],
                                   op0=ALU.mult, op1=ALU.add).then_inc(ex_dve, 1)
            v.wait_ge(ex_ps, 5 + 2 * SQUARINGS - 1)
            link(v.tensor_copy(A3[:], two_banks(2 if SQUARINGS % 2 else 0)))
            add_eye(A3, -1.0).then_inc(ex_dve, 1)

            def ln_stats(i, h):
                if i == 0:
                    v.wait_ge(ld_x, 16)
                elif i == 4:
                    v.wait_ge(x_rot, HT * (h + 1))
                elif i % 2 == 0:
                    v.wait_ge(x_end, x_updates(i // 2) - HT * (1 - h))
                else:
                    v.wait_ge(x_mid, T * (i // 2) + HT * (h + 1))
                for t in range(HT * h, HT * h + HT):
                    ins = v.bn_stats(bn[:, t, :], x[:, t, :])
                link(ins)
                for t in range(HT * h, HT * h + HT):
                    ins = v.bn_aggr(mv[:, t, :], bn[:, t, :])
                ins.then_inc(stats_ready, 1)

            def ln_apply(i, h):
                v.wait_ge(rstd_ready, 2 * i + h + 1)
                if i >= 1:
                    v.wait_ge(xnT_ps, 2 * i + h - 1)
                for t in range(HT * h, HT * h + HT):
                    ins = v.tensor_scalar(xn[:, t, :], x[:, t, :], mv[:, t, 0:1], rstd[:, t:t + 1],
                                          ALU.subtract, ALU.mult)
                ins.then_inc(xn_ready, 1)

            def modulate(i, h):
                n, k = i // 2, 2 * (i % 2)
                if i == 0:
                    v.wait_ge(ada_sb, NB)
                v.wait_ge(xnT_ps, 2 * i + h + 1)
                b0 = HT * B * h
                dst = xmT[0:C, :, HTOK * h:HTOK * (h + 1)].rearrange("p c (b t) -> p c b t", t=TOK)
                scale = mod[:, n, k + 1, :, b0:b0 + HT * B].unsqueeze(3).to_broadcast([C, 2, HT * B, TOK])
                shift = mod[:, n, k, :, b0:b0 + HT * B].unsqueeze(3).to_broadcast([C, 2, HT * B, TOK])
                link(v.tensor_tensor(dst, ps[0:C, 2 * h:2 * h + 2, :].rearrange("p c (b t) -> p c b t", t=TOK),
                                     scale, ALU.mult))
                v.tensor_tensor(dst, dst, shift, ALU.add).then_inc(mod_done, 1)

            for n in range(NB):
                if n == 2:
                    for t in range(T):
                        v.wait_ge(d_ps, t + 1)
                        v.tensor_tensor(x[:, t, :], x[:, t, :], ps[:, 6 + t % 2, 0:D], ALU.add).then_inc(x_rot, 1)
                for h in range(2):
                    ln_stats(2 * n, h)
                for h in range(2):
                    ln_apply(2 * n, h)
                for h in range(2):
                    modulate(2 * n, h)

                if n == 1:
                    for h in range(2):
                        qk = qkv[:, HT * h:HT * h + HT, 0:2 * D].rearrange("p t (g d) -> p t g d", d=DH)

                        def by_head(stat):
                            return stat[:].rearrange("p (t g) -> p t g", t=HT)

                        def over_head(stat):
                            return by_head(stat).unsqueeze(3).to_broadcast([P, HT, 2 * HEADS, DH])

                        v.wait_ge(qkv_sb, T * n + HT * (h + 1))
                        link(v.tensor_reduce(by_head(qk_sum), qk, AX.X, ALU.add))
                        link(v.tensor_scalar(qk_mean[:], qk_sum[:], 1.0 / DH, None, ALU.mult))
                        v.tensor_tensor(qk, qk, over_head(qk_mean), ALU.subtract).then_inc(qk_xc, 1)
                        v.wait_ge(qk_sq, h + 1)
                        v.tensor_reduce(by_head(qk_sum), xn[:].rearrange("p a (g d) -> p (a g) d", d=DH).rearrange(
                            "p (t g) d -> p t g d", t=HT), AX.X, ALU.add).then_inc(qk_ss, 1)
                        v.wait_ge(qk_rstd, h + 1)
                        v.tensor_tensor(qk, qk, over_head(qk_rs), ALU.mult).then_inc(qk_norm, 1)

                na = n - 1

                def spread_keys(p):
                    v.wait_ge(k_sb, 4 * na + p + 1)
                    if na or p >= 2:
                        v.wait_ge(s_ps, T * n + 2 * p - 2)
                    for j in range(K_ACT, HC):
                        dst = kexp[0:C, p % 2, :, :, j, :]
                        src = kT[:].rearrange("p (c b t) -> p c b t", c=2, t=TOK)
                        if n == 1:
                            ins = v.tensor_scalar(dst, src, kscale[:, j:j + 1], kbias[:, j:j + 1], ALU.mult, ALU.add)
                        else:
                            ins = v.tensor_scalar(dst, src, kmask[:, j:j + 1], None, ALU.mult)
                    ins.then_inc(k_dve, 1)

                keys = TOK if n else HEADS

                def by_head(buf):
                    return buf[:, 0:HEADS * keys].rearrange("p (h k) -> p h k", h=HEADS)

                def shift_scores(t):
                    v.wait_ge(s_ps, T * n + t + 1)
                    s = by_head(ps[:, t % 2, :])
                    v.tensor_reduce(rowmax[:, t % 2, :], s, AX.X, ALU.max).then_inc(max_done, 1)
                    v.wait_ge(max_done, T * n + t + 1)
                    if na >= 0 and (na or t >= 2):
                        v.wait_ge(pT_ps, T * na + t - 1)
                    v.tensor_tensor(by_head(probs[:, t % 2, :]), s,
                                    rowmax[:, t % 2, :].unsqueeze(2).to_broadcast([P, HEADS, keys]),
                                    ALU.subtract).then_inc(sub_done, 1)

                def normalise(t):
                    v.wait_ge(o_ps, T * na + t + 1)
                    acc = ps[:, 6, 0:HEADS * VW].rearrange("p (h d) -> p h d", h=HEADS)
                    link(v.reciprocal(rinv[:, t % 2, :], acc[:, :, DH]))
                    if n or t >= 2:
                        v.wait_ge(oT_ps, T * n + t - 1)
                    v.tensor_tensor(o[:, t % 2, :].rearrange("p (h d) -> p h d", h=HEADS), acc[:, :, 0:DH],
                                    rinv[:, t % 2, :].unsqueeze(2).to_broadcast([P, HEADS, DH]),
                                    ALU.mult).then_inc(o_sb, 1)

                def weigh_heads(t):
                    pr = by_head(probs[:, t % 2, :])
                    values = qkv[:, t, 2 * D:].rearrange("p (k d) -> p d k", k=HEADS)
                    v.wait_ge(exp_done, t + 1)
                    link(v.tensor_reduce(rowmax[:, t % 2, :], pr, AX.X, ALU.add))
                    link(v.reciprocal(rinv[:, t % 2, :], rowmax[:, t % 2, :]))
                    prod = prod_pv.rearrange("p (h d k) -> p h d k", h=HEADS, d=DH)
                    link(v.tensor_tensor(prod, pr.unsqueeze(2).to_broadcast([P, HEADS, DH, HEADS]),
                                         values.unsqueeze(1).to_broadcast([P, HEADS, DH, HEADS]), ALU.mult))
                    if t >= 2:
                        v.wait_ge(o_stored, 16 * B * (t - 1))
                    dst = o_heads[:, t % 2].rearrange("p (h d) -> p h d", h=HEADS)
                    link(v.tensor_reduce(dst, prod, AX.X, ALU.add))
                    v.tensor_tensor(dst, dst, rinv[:, t % 2, :].unsqueeze(2).to_broadcast([P, HEADS, DH]),
                                    ALU.mult).then_inc(heads_out, 1)

                def gate1(t):
                    v.wait_ge(pr_ps, T * n + t + 1)
                    if n == 0 and t == 0:
                        v.wait_ge(gate_sb, 9 * NB)
                    if t >= 4:
                        v.wait_ge(x_mid, T * n + t - 3)
                    elif n:
                        v.wait_ge(x_end, T * n)
                    v.tensor_tensor(delta[:, t % 4, :], ps[:, 7, 0:D], gates[:, n, t, 0, :],
                                    ALU.mult).then_inc(gated1, 1)

                def gate2(t):
                    v.wait_ge(m_ps, T * n + t + 1)
                    if t >= 4:
                        v.wait_ge(x_end, T * n + t - 3)
                    else:
                        v.wait_ge(x_mid, T * (n + 1))
                    v.tensor_tensor(delta[:, t % 4, :], ps[:, 6 + t % 2, 0:D], gates[:, n, t, 1, :],
                                    ALU.mult).then_inc(gated2, 1)

                if n:
                    spread_keys(0)
                for st in range(ATT):
                    if st < T:
                        shift_scores(st)
                    if n == 0 and 0 <= st - 1 < T:
                        weigh_heads(st - 1)
                    if n and st < T and st % 2 == 0 and st // 2 + 1 < T // 2:
                        spread_keys(st // 2 + 1)
                    if n and 0 <= st - 2 < T:
                        normalise(st - 2)
                    if 0 <= st - 4 < T:
                        gate1(st - 4)
                for h in range(2):
                    ln_stats(2 * n + 1, h)
                for h in range(2):
                    ln_apply(2 * n + 1, h)
                for h in range(2):
                    modulate(2 * n + 1, h)
                for t in range(T):
                    gate2(t)

        @block.scalar
        def _(a):
            for n in range(2):
                for w, src in ((wq, qkv_w), (wp, proj_w), (w1, fc1_w), (w2, fc2_w)):
                    a.dma_start(w[:, n], src[n]).then_inc(ld_w[n], 16)
                if n == 0:
                    a.dma_start(Pm[:], p_in).then_inc(ld_p, 16)
                    a.dma_start(PT[:], pt_in).then_inc(ld_p, 16)
            a.wait_ge(ld_cond, 16)
            a.wait_ge(dve, 1)
            a.activation(sT[0:C], cT[:], ACT.Silu).then_inc(silu_done, 1)
            for n in range(NB):
                a.wait_ge(gate_ps, 9 * n + 1)
                a.copy(gsb[:, n % 2, :], ps[0:SEQ, 1, 0:2 * D]).then_inc(gate_sb, 1)
                for t in range(T):
                    a.wait_ge(gate_ps, 9 * n + t + 2)
                    a.copy(gates[:, n, t].rearrange("p g f -> p (g f)"), ps[:, 2 + t % 2, 0:2 * D]).then_inc(gate_sb, 1)
            for r in range(2):
                a.wait_ge(v_ps, r + 1)
                a.copy(vsb[:, r, :], ps[:, 4 + r, :]).then_inc(v_sb, 1)

            def two_banks(b):
                return ps[:, b:b + 2, :].rearrange("p a (m r) -> p (a m) r", r=R)

            a.wait_ge(ex_ps, 1)
            a.mul(A2, two_banks(0), -1.0).then_inc(ex_act, 1)
            a.wait_ge(ex_ps, 2)
            a.copy(A3[:], two_banks(2)).then_inc(ex_act, 1)
            a.wait_ge(ex_ps, 5)
            a.copy(EF[:, 1], two_banks(0)).then_inc(ex_act, 1)
            for i in range(SQUARINGS - 1):
                dst = EG if i % 2 == 0 else EF
                a.wait_ge(ex_ps, 5 + 2 * i + 1)
                a.copy(dst[:, 0], two_banks(2 if i % 2 == 0 else 0))
                a.wait_ge(ex_ps, 5 + 2 * i + 2)
                a.copy(dst[:, 1], two_banks(4 if i % 2 == 0 else 6)).then_inc(ex_act, 1)

            for n in range(NB):
                if n == 2:
                    for h in range(2):
                        a.wait_ge(xT_ps, h + 1)
                        a.copy(xmT[0:C, :, HTOK * h:HTOK * (h + 1)], ps[0:C, 0:2, :]).then_inc(xT_sb, 1)
                        a.wait_ge(z_ps, h + 1)
                        a.copy(xn_z, ps[:, 2, :]).then_inc(z_sb, 1)
                        a.wait_ge(y_ps, h + 1)
                        if h == 1:
                            a.wait_ge(d_ps, HT)
                        ydst = xn_y[0:R].rearrange("p (i q t) -> p i q t", q=2, t=TOK)
                        for p in range(2):
                            ins = a.copy(ydst[:, :, p, :], ps[0:R, 4 + p, 0:HTOK // 2].rearrange("p (i t) -> p i t", t=TOK))
                        ins.then_inc(y_sb, 1)
                for t in range(T):
                    a.wait_ge(qkv_ps, T * n + t + 1)
                    if n == 2:
                        a.wait_ge(v_spread, 2)
                    a.copy(qkv[:, t, :], ps[:, 4 + t % 4, 0:QKV]).then_inc(qkv_sb, 1)
                    if n == 1 and t % HT == HT - 1:
                        h = t // HT
                        a.wait_ge(qk_xc, h + 1)
                        a.wait_ge(xnT_ps, 4 * n + 2)
                        if h == 1:
                            a.wait_ge(qk_ss, 1)
                        a.activation(xn[:].rearrange("p a b -> p (a b)").rearrange("p (t g) -> p t g", t=HT),
                                     qkv[:, HT * h:HT * h + HT, 0:2 * D], ACT.Square).then_inc(qk_sq, 1)

                na = n - 1

                def spread(p, part):
                    if part == 0:
                        a.wait_ge(qkT_ps, 4 * na + p + 1)
                        dst = qT[:, :, 2 * p * P:2 * (p + 1) * P]
                        src = ps[0:C, 4, :].rearrange("p (c t) -> p c t", c=2)
                        if n == 1:
                            a.activation(dst, src, ACT.Identity, bias=gb[:, 1:2], scale=gb[:, 0:1]).then_inc(q_sb, 1)
                        else:
                            a.copy(dst, src).then_inc(q_sb, 1)
                        if na or p:
                            a.wait_ge(k_dve, 4 * na + p)
                            a.wait_ge(k_act, 4 * na + p)
                        a.copy(kT[:], ps[0:C, 5, :]).then_inc(k_sb, 1)
                        a.wait_ge(k_sb, 4 * na + p + 1)
                        if na or p >= 2:
                            a.wait_ge(s_ps, T * n + 2 * p - 2)
                    for j in (range(0, 1) if part == 0 else range(1, K_ACT)):
                        dst = kexp[0:C, p % 2, :, :, j, :]
                        src = kT[:].rearrange("p (c b t) -> p c b t", c=2, t=TOK)
                        if n == 1:
                            ins = a.activation(dst, src, ACT.Identity, bias=kbias[:, j:j + 1], scale=kscale[:, j:j + 1])
                        else:
                            ins = a.activation(dst, src, ACT.Copy, scale=kmask[:, j:j + 1])
                    if part == 1:
                        ins.then_inc(k_act, 1)

                def exponential(t):
                    a.wait_ge(sub_done, T * n + t + 1)
                    p = probs[:, t % 2, 0:HEADS * (TOK if n else HEADS)]
                    a.activation(p, p, ACT.Exp, scale=DH ** -0.5).then_inc(exp_done, 1)

                def probs_out(t):
                    a.wait_ge(pT_ps, T * na + t + 1)
                    if na or t >= 2:
                        a.wait_ge(o_ps, T * na + t - 1)
                    a.copy(probsT[:, t % 2, :], ps[:, 2, :]).then_inc(pT_sb, 1)

                def o_out(t):
                    a.wait_ge(oT_ps, T * n + t + 1)
                    if n or t >= 2:
                        a.wait_ge(pr_ps, T * n + t - 1)
                    a.copy(oT[0:C, t % 2], ps[0:C, 3, 0:2 * P].rearrange("p (c t) -> p c t", c=2)).then_inc(oT_sb, 1)

                if n:
                    spread(0, 0)
                    spread(0, 1)
                for st in range(ATT):
                    if n and st // 2 + 1 < T // 2:
                        spread(st // 2 + 1, st % 2)
                    if n and 0 <= st - 1 < T:
                        probs_out(st - 1)
                    if st < T:
                        exponential(st)
                    if 0 <= st - 3 < T:
                        o_out(st - 3)

                for i in range(2 * MC):
                    h, m = divmod(i, MC)
                    a.wait_ge(h_ps, 2 * MC * n + i + 1)
                    if n:
                        a.wait_ge(m_ps, T * (n - 1) + HT * (h + 1))
                    rows = min(P, MLP - P * m)
                    a.activation(hT[0:rows, m, HTOK * h:HTOK * (h + 1)], ps[0:rows, 4 + i % 2, :],
                                 ACT.Gelu if n < 2 else ACT.Gelu_apprx_tanh).then_inc(gelu_done, 1)

        @block.gpsimd
        def _(g):
            own = [0]

            def link(ins):
                own[0] += 1
                ins.then_inc(pool_own, 1)
                g.wait_ge(pool_own, own[0])

            g.wait_ge(st_v, 16 * 2 * B)
            g.wait_ge(gate_ps, 9 * NB)
            link(g.memset(vexp[:], 0.0))
            for q in range(B):
                link(g.memset(vexp[32 * q:32 * q + 32].rearrange("p s g (h d) -> p (s g) h d", h=G4)[:, :, q, DH:VW], 1.0))
            g.wait_ge(gate_ps, 9 * (NB - 1) + 1)
            link(g.memset(hT[R:P, MC - 1, :], 1.0))
            g.wait_ge(ones_set, 1)
            g.wait_ge(diag_ready, 1)
            link(g.tensor_scalar(dg[:, 2:3], half_neg[0:R, 0:1], -1.0, None, ALU.mult))
            g.tensor_tensor(dg[:, 1:2], dg[:, 0:1], dg[:, 2:3], ALU.pow).then_inc(isd_ready, 1)

            def add_delta(n, t, gated, done):
                g.wait_ge(gated, T * n + t + 1)
                g.tensor_tensor(x[:, t, :], x[:, t, :], delta[:, t % 4, :], ALU.add).then_inc(done, 1)

            def ln_rstd(i, h):
                t = slice(HT * h, HT * h + HT)
                g.wait_ge(stats_ready, 2 * i + h + 1)
                link(g.tensor_scalar(veps[:, t], mv[:, t, 1], EPS, None, ALU.add))
                g.tensor_tensor(rstd[:, t], veps[:, t], half_neg[:].to_broadcast([P, HT]), ALU.pow).then_inc(rstd_ready, 1)

            for n in range(NB):
                for h in range(2):
                    ln_rstd(2 * n, h)
                if n == 0:
                    g.wait_ge(v_ps, 2)
                    for t in range(T):
                        g.wait_ge(qkv_sb, t + 1)
                        if t:
                            g.wait_ge(s_ps, t)
                        q_, k_ = (qkv[:, t, i * D:(i + 1) * D].rearrange("p (h d) -> p d h", h=HEADS) for i in range(2))
                        g.tensor_tensor(prod_qk.rearrange("p (d h k) -> p d h k", d=DH, h=HEADS),
                                        q_.unsqueeze(3).to_broadcast([P, DH, HEADS, HEADS]),
                                        k_.unsqueeze(2).to_broadcast([P, DH, HEADS, HEADS]),
                                        ALU.mult).then_inc(qk_prod, 1)
                        if t >= 4:
                            add_delta(n, t - 4, gated1, x_mid)
                    for t in range(T - 4, T):
                        add_delta(n, t, gated1, x_mid)
                for h in range(2 if n else 0):
                    if n == 1:
                        g.wait_ge(qk_ss, h + 1)
                        link(g.tensor_scalar(qk_mean[:], qk_sum[:], 1.0 / DH, QK_EPS, ALU.mult, ALU.add))
                        g.tensor_tensor(qk_rs[:], qk_mean[:], half_neg[:].to_broadcast([P, 4 * 2 * HEADS]), ALU.pow).then_inc(qk_rstd, 1)
                    g.wait_ge(qkv_sb, T * n + HT * (h + 1))
                    if n == 2:
                        g.wait_ge(o_ps, T)
                    for b in range(B):
                        for q in range(G4):
                            src = qkv[TOK * b:TOK * b + TOK, HT * h:HT * h + HT, 2 * D:].rearrange(
                                "p t (g s d) -> p t g s d", g=4, s=G4)[:, :, :, q, :]
                            dst = vexp[TOK * q:TOK * q + TOK].rearrange(
                                "p (t b) g (s d) -> p t b g s d", b=B, s=G4)[:, HT * h:HT * h + HT, b, :, q, 0:DH]
                            link(g.tensor_copy(dst, src))
                    g.sem_inc(v_spread, 1)
                for t in range(T if n else 0):
                    add_delta(n, t, gated1, x_mid)
                for h in range(2):
                    ln_rstd(2 * n + 1, h)
                for t in range(T):
                    add_delta(n, t, gated2, x_end)


def with_bias_row(w, b):
    n = w.shape[1]
    o = np.zeros((C + 1, 2, n), np.float32)
    o[0:C, 0], o[0:C, 1], o[C, 0] = w[0:C], w[C:D], b
    return o


def kernel(**inputs):
    import concourse.bacc as _bacc
    from concourse import mybir as _mybir
    from concourse.bass_utils import run_bass_kernel_spmd as _run

    a = {k: np.asarray(v) for k, v in inputs.items()}
    names = {"ada": ("L0_cond_ada_w", "L0_cond_ada_b", "L1_cond_w_ada", "L1_cond_b_ada", "L3_cond_W_ada", "L3_cond_b_ada"),
             "qkv": ("L0_cond_qkv_w", "L0_cond_qkv_b", "L1_cond_w_qkv", "L1_cond_b_qkv", "L3_cond_W_qkv", "L3_cond_b_qkv"),
             "proj": ("L0_cond_proj_w", "L0_cond_proj_b", "L1_cond_w_proj", "L1_cond_b_proj", "L3_cond_W_proj", "L3_cond_b_proj"),
             "fc1": ("L0_cond_fc1_w", "L0_cond_fc1_b", "L1_cond_w1", "L1_cond_b1", "L3_cond_W_fc1", "L3_cond_b_fc1"),
             "fc2": ("L0_cond_fc2_w", "L0_cond_fc2_b", "L1_cond_w2", "L1_cond_b2", "L3_cond_W_fc2", "L3_cond_b_fc2")}
    packed = {k: np.stack([with_bias_row(a[v[2 * i]], a[v[2 * i + 1]]) for i in range(NB)])
              for k, v in names.items() if k != "fc2"}
    fc2 = np.zeros((NB, MC * P, D), np.float32)
    for i in range(NB):
        fc2[i, 0:MLP], fc2[i, MLP] = a[names["fc2"][2 * i]], a[names["fc2"][2 * i + 1]]
    fc2 = np.ascontiguousarray(fc2.reshape(NB, MC, P, D).transpose(0, 2, 1, 3))
    cond = a["cond_1152"]
    cond_t = np.ascontiguousarray(cond.T.reshape(2, C, SEQ).transpose(1, 0, 2))
    gbs = np.stack([np.tile(a[k], HC) for k in ("L1_cond_qn_g", "L1_cond_qn_b", "L1_cond_kn_g", "L1_cond_kn_b")], 1)
    iu, ju = np.triu_indices(R, k=1)
    at = np.zeros((R, R), np.int64)
    at[iu, ju] = at[ju, iu] = np.arange(len(iu))
    rot = with_bias_row(a["L2_cond_W"][at.reshape(-1)].T, a["L2_cond_b"][at.reshape(-1)])
    pm = a["L2_cond_P"]
    f = np.float32
    scale = 2.0 ** -SQUARINGS
    ij = np.sign(np.arange(R)[None] - np.arange(R)[:, None])
    arrays = {
        "x_in": a["x"].reshape(SEQ * TOK, D), "cond_t": cond_t, "ada_w": packed["ada"], "qkv_w": packed["qkv"],
        "proj_w": packed["proj"], "fc1_w": packed["fc1"], "fc2_w": fc2, "qk_gb": gbs, "rot_w": rot,
        "p_in": np.ascontiguousarray(pm.reshape(2, C, R).transpose(1, 0, 2)), "pt_in": np.ascontiguousarray(pm.T),
        "eye": np.eye(P, dtype=f),
        "head_mask": (np.arange(C)[:, None] // DH == np.arange(HC)[None]).astype(f),
        "below": -(np.arange(R)[:, None] > np.arange(R)[None]).astype(f),
        "seq_mask": np.repeat(np.eye(SEQ, dtype=f), TOK, axis=1),
        "skew": (np.concatenate([ij, ij]) * scale).astype(f),
    }
    nc = _bacc.Bacc("TRN2", target_bir_lowering=False, num_devices=1)
    args, fed = [], {}
    for name, v in arrays.items():
        v = np.ascontiguousarray(v)
        fed[name + "_dram"] = v
        args.append(nc.dram_tensor(name + "_dram", v.shape, _mybir.dt.from_np(v.dtype), kind="ExternalInput").ap())
    args.append(nc.dram_tensor("out_dram", (SEQ * TOK, D), F32, kind="ExternalOutput").ap())
    fused_blocks(nc, *args)
    r = _run(nc, [fed], core_ids=[0])
    return r.results[0]["out_dram"].reshape(SEQ, TOK, D)
```

```python
from contextlib import ExitStack
from math import factorial

import numpy as np

import concourse.bass as bass
from concourse import mybir

F32 = mybir.dt.float32
ALU = mybir.AluOpType
ACT = mybir.ActivationFunctionType
AX = mybir.AxisListType

P = 128
SEQ, TOK, D = 32, 32, 144
T = SEQ * TOK // P
B = P // TOK
C = D // 2
HEADS, DH = 16, 9
HC = HEADS // 2
QKV = 3 * D
VW = DH + 1
G4 = 4
MLP = 4 * D
MC = 5
HT = T // 2
HTOK = HT * P
R = 64
PAIRS = SEQ // 2
SQUARINGS = 5
EPS, QK_EPS = 1e-6, 1e-5
NB = 3
CHAIN = 2 * R + 3
CH_START, CH_QKV, CH_GATES, CH_SUM, CH_EXPM, CH_L1 = 5, 2, 6, 2, 2, 2
CH_MOD = 6
ISD_TILE = 1 + (R + 1 - CH_START - 4 * CH_QKV - CH_MOD - CH_SUM - CH_GATES) // (CH_SUM + CH_EXPM) - 4
EXPM = 5 + SQUARINGS


def fused_blocks(nc, x_in, cond_t, ada_w, qkv_w, proj_w, fc1_w, fc2_w, qk_gb, rot_w, p_in, pt_in,
                 eye, head_mask, below, seq_mask, skew, out):
    with ExitStack() as ctx:
        def sb(name, shape):
            return ctx.enter_context(nc.sbuf_tensor(name, shape, F32))

        def sem(name):
            return ctx.enter_context(nc.semaphore(name))

        ps = ctx.enter_context(nc.psum_tensor("ps", [P, 8, 512], F32))

        x = sb("x", [P, T, D])
        xn = sb("xn", [P, T, D])
        xmT = sb("xmT", [P, 2, T * P])
        qkv = sb("qkv", [P, T, QKV])
        qT = sb("qT", [C, 2, T * P])
        kT = sb("kT", [C, 4 * P])
        kexp = sb("kexp", [P, 2, 2, 2 * B, HC, TOK])
        vexp = sb("vexp", [P, SEQ, 4, G4 * VW])
        probs = sb("probs", [P, 2, HEADS * TOK])
        probsT = sb("probsT", [P, 2, HEADS * TOK])
        rowmax = sb("rowmax", [P, 2, HEADS])
        rinv = sb("rinv", [P, 2, HEADS])
        o = sb("o", [P, 2, D])
        oT = sb("oT", [P, 2, 2, P])
        delta = sb("delta", [P, 4, D])
        hT = sb("hT", [P, MC, T * P])
        gates = sb("gates", [P, NB, T, 2, D])
        mod = sb("mod", [C, NB, 4, 2, SEQ])
        bn = sb("bn", [P, T, 6])
        mv = sb("mv", [P, T, 2])
        rstd = sb("rstd", [P, T])
        veps = sb("veps", [P, T])
        qk_sum = sb("qk_sum", [P, 4 * 2 * HEADS])
        qk_mean = sb("qk_mean", [P, 4 * 2 * HEADS])
        qk_rs = sb("qk_rs", [P, 4 * 2 * HEADS])
        wq = sb("wq", [P, 2, 2, QKV])
        wp = sb("wp", [P, 2, 2, D])
        w1 = sb("w1", [P, 2, 2, MLP])
        w2 = sb("w2", [P, 2, MC, D])
        ident = sb("ident", [P, P])
        kmask = sb("kmask", [C, HC])
        kscale = sb("kscale", [C, HC])
        kbias = sb("kbias", [C, HC])
        gb = sb("gb", [C, 4])
        half_neg = sb("half_neg", [P, 1])
        qk_eps = sb("qk_eps", [P, 1])
        cT = sb("cT", [C, 2, SEQ])
        sT = sb("sT", [P, 2, SEQ])
        neg_below = sb("neg_below", [R, R])
        W = sb("W", [R, R])
        M = sb("M", [R, R])
        fcol = sb("fcol", [R, R])
        RD = sb("RD", [R, R])
        SG = sb("SG", [R, R])
        piv = sb("piv", [R, 4])
        dg = sb("dg", [R, 4])
        LiT = sb("LiT", [R, R])
        PT = sb("PT", [R, D])
        Pm = sb("Pm", [C, 2, R])
        UT = sb("UT", [R, D])
        U = sb("U", [C, 2, 2, R])
        sgn = sb("sgn", [P, R])
        EG = sb("EG", [P, 2, PAIRS, R])
        A, A2 = EG[:, 0], EG[:, 1]
        A3 = sb("A3", [P, PAIRS, R])
        EF = sb("EF", [P, 2, PAIRS, R])
        pol = EF[:, 1]
        kexp_flat = kexp[:].rearrange("p a c b h k -> p (a c b h k)")
        rotw = kexp_flat[0:C + 1].rearrange("p (c n) -> p c n", c=2)
        NP = HEADS * HEADS * DH
        prod_qk = kexp_flat[:, 0:NP]
        prod_pv = kexp_flat[:, NP:2 * NP]
        o_heads = kexp_flat[:, 2 * NP:2 * NP + 2 * D].rearrange("p (i f) -> p i f", i=2)
        vsb = vexp[:].rearrange("p a b c -> p (a b c)")[:, 0:1024].rearrange("p (r n) -> p r n", r=2)
        spread_seq = vexp[:].rearrange("p a b c -> p (a b c)")[0:SEQ, 1024:1024 + T * P]
        gsb = vexp[:].rearrange("p a b c -> p (a b c)")[0:SEQ, 2048:2048 + 6 * D].rearrange("p (l n) -> p l n", l=NB)
        prod_slot = [prod_qk, hT[:].rearrange("p a b -> p (a b)")[:, 0:NP]]
        adaw = hT[:].rearrange("p a b -> p (a b)")[0:C + 1, 0:2 * 2 * 6 * D].rearrange(
            "p (l c n) -> p l c n", l=2, c=2)
        z_rot, y_rot = probs, probsT
        o_dram = nc.dram_tensor("o_scratch", (SEQ, HEADS, TOK, DH), F32, kind="Internal").ap()
        v_dram = nc.dram_tensor("v_scratch", (R, SEQ, R), F32, kind="Internal").ap()

        ld_const, ld_cond, ld_x, ld_p = sem("ld_const"), sem("ld_cond"), sem("ld_x"), sem("ld_p")
        ld_ada = [sem(f"ld_ada{n}") for n in range(NB)]
        ld_rot, ld_v, st_v = sem("ld_rot"), sem("ld_v"), sem("st_v")
        ld_id, pads_set = sem("ld_id"), sem("pads_set")
        ld_wq = [sem(f"ld_wq{n}") for n in range(NB)]
        ld_w = [sem(f"ld_w{n}") for n in range(NB)]
        silu_done, ones_set, ada_ps, ada_sb = sem("silu_done"), sem("ones_set"), sem("ada_ps"), sem("ada_sb")
        gseq_ps, gseq_sb, gate_ps, gate_sb = sem("gseq_ps"), sem("gseq_sb"), sem("gate_ps"), sem("gate_sb")
        v_ps, v_sb = sem("v_ps"), sem("v_sb")
        dve = sem("dve")
        act_own = sem("act_own")
        pool_own = sem("pool_own")
        gram_ps, w_ready, bc_ps, m_ready = sem("gram_ps"), sem("w_ready"), sem("bc_ps"), sem("m_ready")
        lit_in, lit_ps, lit_sb, ut_ps, ut_ready, u_ps, u_sb = (
            sem(s) for s in ("lit_in", "lit_ps", "lit_sb", "ut_ps", "ut_ready", "u_ps", "u_sb"))
        diag_ready, isd_ready = sem("diag_ready"), sem("isd_ready")
        a_ready, ex_ps, ex_act, ex_dve = sem("a_ready"), sem("ex_ps"), sem("ex_act"), sem("ex_dve")
        stats_ready, rstd_ready, xn_ready = sem("stats_ready"), sem("rstd_ready"), sem("xn_ready")
        xnT_ps, mod_done = sem("xnT_ps"), sem("mod_done")
        qkv_ps, qkv_sb = sem("qkv_ps"), sem("qkv_sb")
        qk_xc, qk_sq, qk_ss, qk_rstd, qk_norm = (sem(s) for s in ("qk_xc", "qk_sq", "qk_ss", "qk_rstd", "qk_norm"))
        v_spread = sem("v_spread")
        qkT_ps, q_sb, k_sb, k_act, k_dve = sem("qkT_ps"), sem("q_sb"), sem("k_sb"), sem("k_act"), sem("k_dve")
        s_ps, max_done, sub_done, exp_done = sem("s_ps"), sem("max_done"), sem("sub_done"), sem("exp_done")
        pT_ps, pT_sb, o_ps, o_sb = sem("pT_ps"), sem("pT_sb"), sem("o_ps"), sem("o_sb")
        oT_ps, oT_sb, pr_ps, gated1, x_mid = sem("oT_ps"), sem("oT_sb"), sem("pr_ps"), sem("gated1"), sem("x_mid")
        pv_prod = sem("pv_prod")
        qk_prod, heads_out, o_stored = sem("qk_prod"), sem("heads_out"), sem("o_stored")
        o_back = [sem("o_back0"), sem("o_back1")]
        h_ps, gelu_done, m_ps, gated2, x_end = sem("h_ps"), sem("gelu_done"), sem("m_ps"), sem("gated2"), sem("x_end")
        xT_ps, xT_sb, z_ps, z_sb, y_ps, y_sb, d_ps, x_rot = (
            sem(s) for s in ("xT_ps", "xT_sb", "z_ps", "z_sb", "y_ps", "y_sb", "d_ps", "x_rot"))
        stored = sem("stored")

        LNS = 2 * NB
        ATT = T + 4
        FC2_BANK = (6, 3)
        SPREAD_BANK = (2, 3, 4)
        O_BANK = (2, 3, 3)
        EX0, EX1 = (3, 4), (5, 6)
        K_ACT = 3

        def x_updates(n):
            return T * n

        block = ctx.enter_context(nc.Block())

        @block.sync
        def _(sp):
            sp.dma_start(cT[:], cond_t).then_inc(ld_cond, 16)
            sp.dma_start(ident[:], eye).then_inc(ld_id, 16)
            sp.dma_start(neg_below[:], below).then_inc(ld_id, 16)
            sp.dma_start(adaw[:, 0], ada_w[0]).then_inc(ld_ada[0], 16)
            sp.dma_start(x[:], x_in.rearrange("(t p) f -> p t f", p=P)).then_inc(ld_x, 16)
            sp.dma_start(adaw[:, 1], ada_w[1]).then_inc(ld_ada[1], 16)
            sp.dma_start(rotw[:], rot_w).then_inc(ld_rot, 16)
            sp.dma_start(kmask[:], head_mask).then_inc(ld_const, 16)
            sp.dma_start(sgn[:], skew).then_inc(ld_const, 16)
            sp.dma_start(spread_seq, seq_mask).then_inc(ld_const, 16)
            sp.dma_start(gb[:], qk_gb).then_inc(ld_const, 16)
            sp.wait_ge(ada_ps, 1)
            sp.wait_ge(gseq_ps, 1)
            sp.dma_start(adaw[:, 0], ada_w[2]).then_inc(ld_ada[2], 16)
            for r in range(2):
                sp.wait_ge(v_sb, r + 1)
                for q in range(B):
                    i0 = (r * B + q) * 8
                    sp.dma_start(v_dram[i0:i0 + 8].rearrange("i b j -> b i j"),
                                 vsb[32 * q:32 * q + 32, r].rearrange("b (i j) -> b i j", i=8)).then_inc(st_v, 16)
            sp.wait_ge(st_v, 16 * 2 * B)
            for p in range(2):
                sp.dma_start(EG[R * p:R * p + R, 1], v_dram[:, p:SEQ:2, :]).then_inc(ld_v, 16)
            for t in range(T):
                sp.wait_ge(heads_out, t + 1)
                for b in range(B):
                    sp.dma_start(o_dram[B * t + b].rearrange("h t d -> t h d"),
                                 o_heads[TOK * b:TOK * b + TOK, t % 2].rearrange("p (h d) -> p h d", h=HEADS)
                                 ).then_inc(o_stored, 16)
                sp.wait_ge(o_stored, 16 * B * (t + 1))
                if t >= 2:
                    sp.wait_ge(oT_ps, t - 1)
                sp.dma_start(o[:, t % 2, :], o_dram.rearrange("n h t d -> (n h t d)").rearrange(
                    "(i p f) -> i p f", p=P, f=D)[t]).then_inc(o_back[t % 2], 16)
            sp.wait_ge(m_ps, T)
            sp.dma_start(wq[0:C + 1, 0], qkv_w[2]).then_inc(ld_wq[2], 16)
            for w, src in ((wp[0:C + 1], proj_w), (w1[0:C + 1], fc1_w), (w2, fc2_w)):
                sp.dma_start(w[:, 0], src[2]).then_inc(ld_w[2], 16)
            for h in range(2):
                sp.wait_ge(x_end, T * (NB - 1) + HT * (h + 1))
                sp.dma_start(out.rearrange("(t p) f -> p t f", p=P)[:, HT * h:HT * h + HT],
                             x[:, HT * h:HT * h + HT]).then_inc(stored, 16)
            sp.wait_ge(stored, 32)

        @block.tensor
        def _(pe):
            def chunked(dst, lhs, rhs, padded=True):
                k0, k1 = (P, P) if padded else (C + 1, C)
                pe.matmul(dst, lhs(0, k0), rhs(0, k0), start=True, stop=False)
                return pe.matmul(dst, lhs(1, k1), rhs(1, k1), start=False, stop=True)

            pe.wait_ge(ld_id, 32)
            pe.wait_ge(ld_p, 32)
            for kc in range(2):
                mm = pe.matmul(ps[0:R, 7, 0:R], Pm[:, kc, :], Pm[:, kc, :], start=kc == 0, stop=kc == 1)
            mm.then_inc(gram_ps, 1)

            def bcast_row(src, k):
                pe.matmul(ps[0:R, 7, 0:R], ident[0:R, k:k + 1].to_broadcast([R, R]), src[:, :],
                          start=True, stop=True).then_inc(bc_ps, 1)

            def chain_step(j):
                if j < R:
                    pe.wait_ge(w_ready, j + 1)
                    bcast_row(W, j)
                elif j == R:
                    pe.wait_ge(lit_in, 1)
                    pe.transpose(ps[0:R, 7, 0:R], W[:, :], ident[0:R, 0:R]).then_inc(lit_ps, 1)
                elif j == R + 1:
                    pe.wait_ge(lit_sb, 1)
                    pe.matmul(ps[0:R, 7, 0:D], LiT[:, :], PT[:, :], start=True, stop=True).then_inc(ut_ps, 1)
                elif j < CHAIN - 1:
                    pe.wait_ge(m_ready, j - R - 1)
                    bcast_row(M, j - R - 2)
                else:
                    pe.wait_ge(ut_ready, 1)
                    for c in range(2):
                        mm = pe.transpose(ps[0:C, 7, c * R:(c + 1) * R], UT[:, c * C:(c + 1) * C], ident[0:R, 0:R])
                    mm.then_inc(u_ps, 1)

            chain_at = [0]

            def chain(steps):
                first, chain_at[0] = chain_at[0], min(chain_at[0] + steps, CHAIN)
                for j in range(first, chain_at[0]):
                    chain_step(j)

            def modulation(n):
                pe.wait_ge(ld_ada[n], 16)
                if n >= 1:
                    pe.wait_ge(ada_sb, n)
                w = adaw[:, n % 2]
                for i, kind in enumerate((0, 1, 3, 4)):
                    for c in range(2):
                        col = kind * D + c * C
                        mm = chunked(ps[0:C, 6, (2 * i + c) * SEQ:(2 * i + c + 1) * SEQ],
                                     lambda kc, k: w[0:k, kc, col:col + C], lambda kc, k: sT[0:k, kc, :],
                                     padded=False)
                mm.then_inc(ada_ps, 1)
                if n >= 1:
                    chain(1)

            def gates_by_sequence(n):
                if n >= 1:
                    pe.wait_ge(gseq_sb, n)
                w = adaw[:, n % 2]
                for i, kind in enumerate((2, 5)):
                    mm = chunked(ps[0:SEQ, 5, i * D:(i + 1) * D], lambda kc, k: sT[0:k, kc, :],
                                 lambda kc, k: w[0:k, kc, kind * D:(kind + 1) * D], padded=False)
                mm.then_inc(gseq_ps, 1)
                if n >= 1:
                    chain(1)

            def spread_gates(i):
                pe.wait_ge(gseq_sb, i // T + 1)
                if i >= 3:
                    pe.wait_ge(gate_sb, i - 2)
                t = i % T
                pe.matmul(ps[:, SPREAD_BANK[i % 3], 0:2 * D], spread_seq[:, t * P:(t + 1) * P],
                          gsb[:, i // T, :], start=True, stop=True).then_inc(gate_ps, 1)

            def rotation_generators():
                pe.wait_ge(ld_rot, 16)
                for r in range(2):
                    for kc in range(2):
                        k = C + 1 - kc
                        for q in range(B):
                            col = (r * B + q) * 512
                            mm = pe.matmul(ps[32 * q:32 * q + 32, r, :], sT[0:k, kc, :], rotw[0:k, kc, col:col + 512],
                                           start=kc == 0, stop=kc == 1)
                    mm.then_inc(v_ps, 1)
                    chain(1)

            def pair_products(banks, lhs, rhs, every):
                for first in range(2):
                    for i in range(8):
                        for p in range(2):
                            m = (first ^ p) * 8 + i
                            row = slice(R * p, R * p + R)
                            mm = pe.matmul(ps[row, banks[m // 8], (m % 8) * R:(m % 8 + 1) * R],
                                           lhs(row, m), rhs(row, m), start=True, stop=True)
                        if (first * 8 + i + 1) % every == 0 and (first, i) != (1, 7):
                            chain(1)
                mm.then_inc(ex_ps, 1)
                chain(1)

            def mat(buf):
                return lambda row, m: buf[row, m, :]

            def half_of(buf, i):
                return lambda row, m: buf[row, i, m, :]

            def expm(e):
                if e == 0:
                    pe.wait_ge(gate_sb, NB * T)
                    pe.wait_ge(gseq_sb, NB)
                    pe.wait_ge(ada_sb, NB)
                    pe.wait_ge(a_ready, 1)
                    pair_products(EX0, mat(A), mat(A), 8)
                elif e == 1:
                    pe.wait_ge(ex_act, 1)
                    pair_products(EX1, mat(A2), mat(A), 8)
                elif e == 2:
                    pe.wait_ge(ex_act, 2)
                    pe.wait_ge(ex_dve, 1)
                    pair_products(EX0, mat(A3), mat(pol), 8)
                elif e == 3:
                    pe.wait_ge(ex_dve, 2)
                    pair_products(EX1, mat(A3), mat(pol), 8)
                elif e == 4:
                    pe.wait_ge(ex_dve, 3)
                    pair_products(EX0, half_of(EF, 0), lambda row, m: ident[row, row], 8)
                else:
                    i = e - 5
                    src = EF if i % 2 == 0 else EG
                    pe.wait_ge(ex_act, 3 + i)
                    every = 16 if i < SQUARINGS - 1 else 8
                    pair_products(EX0, half_of(src, 1), half_of(src, 0), every)
                    if i < SQUARINGS - 1:
                        pair_products(EX1, half_of(src, 0), half_of(src, 1), every)

            def ln_transpose(i, h):
                pe.wait_ge(xn_ready, 2 * i + h + 1)
                if i >= 1:
                    pe.wait_ge(mod_done, 2 * i + h - 1)
                if i == 1:
                    pe.wait_ge(ex_act, 2 + SQUARINGS)
                    pe.wait_ge(sub_done, T)
                for t in range(HT * h, HT * h + HT):
                    for c in range(2):
                        mm = pe.transpose(ps[0:C, 2 * h + c, (t % HT) * P:(t % HT + 1) * P],
                                          xn[:, t, c * C:(c + 1) * C], ident[:, :])
                mm.then_inc(xnT_ps, 1)

            def rotate():
                for h in range(2):
                    pe.wait_ge(x_end, T + HT * (h + 1))
                    for t in range(HT * h, HT * h + HT):
                        for c in range(2):
                            mm = pe.transpose(ps[0:C, 2 * h + c, (t % HT) * P:(t % HT + 1) * P], x[:, t, c * C:(c + 1) * C],
                                              ident[:, :])
                    mm.then_inc(xT_ps, 1)
                chain(CHAIN)
                pe.wait_ge(u_sb, 1)
                for h in range(2):
                    pe.wait_ge(xT_sb, h + 1)
                    for c in range(2):
                        mm = pe.matmul(ps[:, 4 + h, :], U[:, c].rearrange("p i r -> p (i r)"),
                                       xmT[0:C, c, HTOK * h:HTOK * (h + 1)], start=c == 0, stop=c == 1)
                    mm.then_inc(z_ps, 1)
                for h in range(2):
                    pe.wait_ge(z_sb, h + 1)
                    for i in range(HT * B // 2):
                        for p in range(2):
                            b = HT * B * h + 2 * i + p
                            row = slice(R * p, R * p + R)
                            mm = pe.matmul(ps[0:R, 2 * h + p, i * TOK:(i + 1) * TOK], A3[row, b // 2, :],
                                           z_rot[row, h, (b % (HT * B)) * TOK:(b % (HT * B) + 1) * TOK],
                                           start=True, stop=True)
                    mm.then_inc(y_ps, 1)
                for h in range(2):
                    pe.wait_ge(y_sb, h + 1)
                    for t in range(HT * h, HT * h + HT):
                        if t >= 2:
                            pe.wait_ge(x_rot, t - 1)
                        pe.matmul(ps[:, 6 + t % 2, 0:D], y_rot[0:R, h, (t % HT) * P:(t % HT + 1) * P], UT[:, :],
                                  start=True, stop=True).then_inc(d_ps, 1)

            for n in range(NB):
                s = n % 2
                if n == 0:
                    chain(CH_START)
                    pe.wait_ge(silu_done, 1)
                    modulation(0)
                if n == 2:
                    rotate()
                ln_transpose(2 * n, 0)
                pe.wait_ge(ld_wq[n], 16)
                for t in range(T):
                    if t == 2:
                        ln_transpose(2 * n, 1)
                    pe.wait_ge(mod_done, 4 * n + t // HT + 1)
                    if t >= 3:
                        pe.wait_ge(qkv_sb, T * n + t - 2)
                    elif n >= 1:
                        pe.wait_ge(gelu_done, 2 * MC * n)
                        pe.wait_ge(gated2, T * n)
                        if n == 2:
                            pe.wait_ge(x_rot, T)
                    chunked(ps[:, 4 + t % 3, 0:QKV], lambda kc, k: xmT[0:k, kc, t * P:(t + 1) * P],
                            lambda kc, k: wq[0:k, s, kc, :]).then_inc(qkv_ps, 1)
                    if n == 0 and t >= HT:
                        chain(CH_QKV)
                if n == 0:
                    pe.wait_ge(ld_const, 16 * 4)
                    pe.wait_ge(qkv_sb, T)
                    gates_by_sequence(0)
                    modulation(1)
                    gates_by_sequence(1)
                    rotation_generators()
                    modulation(2)
                    gates_by_sequence(2)

                na = n - 1

                def sum_products(t):
                    pe.wait_ge(qk_prod, t + 1)
                    if t < 2:
                        pe.wait_ge(v_sb, 2)
                    else:
                        pe.wait_ge(sub_done, t - 1)
                    for d in range(DH):
                        mm = pe.matmul(ps[:, t % 2, 0:HEADS * HEADS], ident[:, :],
                                       prod_slot[t % 2][:, d * HEADS * HEADS:(d + 1) * HEADS * HEADS],
                                       start=d == 0, stop=d == DH - 1)
                        if d % 4 == 3:
                            chain(CH_SUM // 2)
                    mm.then_inc(s_ps, 1)

                def qk_transpose(p):
                    pe.wait_ge(qkv_sb, T * n + (T if p == 0 else 2 * p + 2))
                    if n == 1:
                        pe.wait_ge(qk_norm, p // 2 + 1)
                    if p >= 1:
                        pe.wait_ge(k_sb, 4 * na + p)
                    for i in range(2):
                        for c in range(2):
                            for j in range(2):
                                mm = pe.transpose(ps[0:C, 4 + i, (2 * c + j) * P:(2 * c + j + 1) * P],
                                                  qkv[:, 2 * p + j, i * D + c * C:i * D + (c + 1) * C], ident[:, :])
                    mm.then_inc(qkT_ps, 1)

                def scores(t):
                    p = t // 2
                    pe.wait_ge(q_sb, 4 * na + p + 1)
                    pe.wait_ge(k_act, 4 * na + p + 1)
                    pe.wait_ge(k_dve, 4 * na + p + 1)
                    if t >= 2:
                        pe.wait_ge(sub_done, T * n + t - 1)
                    for c in range(2):
                        for b in range(B):
                            mm = pe.matmul(ps[TOK * b:TOK * b + TOK, t % 2, c * 256:(c + 1) * 256],
                                           qT[:, c, t * P + b * TOK:t * P + (b + 1) * TOK],
                                           kexp[0:C, p % 2, c, (t % 2) * B + b, :, :],
                                           start=True, stop=True)
                    mm.then_inc(s_ps, 1)

                def probs_transpose(t):
                    pe.wait_ge(exp_done, T * n + t + 1)
                    if na or t:
                        pe.wait_ge(pT_sb, T * na + t)
                    for g in range(4):
                        mm = pe.transpose(ps[:, 2, g * P:(g + 1) * P], probs[:, t % 2, g * P:(g + 1) * P], ident[:, :])
                    mm.then_inc(pT_ps, 1)

                def values(t):
                    pe.wait_ge(pT_sb, T * na + t + 1)
                    pe.wait_ge(v_spread, 2 * na + t // HT + 1)
                    if na or t:
                        pe.wait_ge(o_sb, T * na + t)
                    if t == 0:
                        pe.wait_ge(qkv_sb, T * (n + 1))
                    for g in range(4):
                        for b in range(B):
                            mm = pe.matmul(ps[TOK * b:TOK * b + TOK, 6, g * G4 * VW:(g + 1) * G4 * VW],
                                           probsT[:, t % 2, g * P + TOK * b:g * P + TOK * b + TOK],
                                           vexp[:, B * t + b, g, :], start=True, stop=True)
                    mm.then_inc(o_ps, 1)

                def o_transpose(t):
                    if n == 0:
                        pe.wait_ge(o_back[t % 2], 16 * (t // 2 + 1))
                    else:
                        pe.wait_ge(o_sb, T * na + t + 1)
                    if n or t:
                        pe.wait_ge(gated1, T * n + t)
                    for c in range(2):
                        mm = pe.transpose(ps[0:C, O_BANK[n], c * P:(c + 1) * P], o[:, t % 2, c * C:(c + 1) * C], ident[:, :])
                    mm.then_inc(oT_ps, 1)

                def project(t):
                    pe.wait_ge(oT_sb, T * n + t + 1)
                    if t == 0:
                        pe.wait_ge(ld_w[n], 16 * 3)
                    chunked(ps[:, O_BANK[n], 0:D], lambda kc, k: oT[0:k, t % 2, kc, :],
                            lambda kc, k: wp[0:k, s, kc, :]).then_inc(pr_ps, 1)

                for st in range(0 if n else ATT):
                    if 0 <= st - 4 < T:
                        project(st - 4)
                    if st < T:
                        sum_products(st)
                    else:
                        chain(CH_SUM)
                    if st == 0:
                        for i in range(NB * T):
                            spread_gates(i)
                            if i % (NB * T // CH_GATES) == 1:
                                chain(1)
                    elif st <= EXPM:
                        expm(st - 1)
                    else:
                        chain(CH_EXPM)
                    if 0 <= st - 3 < T:
                        o_transpose(st - 3)
                    if st == ATT - 2:
                        ln_transpose(2 * n + 1, 0)
                if n:
                    qk_transpose(0)
                for st in range(ATT if n else 0):
                    if st < T and st % 2 == 0 and st // 2 + 1 < T // 2:
                        qk_transpose(st // 2 + 1)
                    if st < T:
                        scores(st)
                    if 0 <= st - 4 < T:
                        project(st - 4)
                    chain(CH_L1 // 2)
                    if 0 <= st - 1 < T:
                        probs_transpose(st - 1)
                    if 0 <= st - 2 < T:
                        values(st - 2)
                    if 0 <= st - 3 < T:
                        o_transpose(st - 3)
                    chain((CH_L1 + 1) // 2)
                    if st == ATT - 2:
                        ln_transpose(2 * n + 1, 0)

                def fc1(h):
                    pe.wait_ge(mod_done, 4 * n + 2 + h + 1)
                    for m in range(MC):
                        i = MC * h + m
                        if i == 3:
                            ln_transpose(2 * n + 1, 1)
                        if i >= 2:
                            pe.wait_ge(gelu_done, 2 * MC * n + i - 1)
                        rows = min(P, MLP - P * m)
                        chunked(ps[0:rows, 4 + i % 2, :], lambda kc, k: w1[0:k, s, kc, m * P:m * P + rows],
                                lambda kc, k: xmT[0:k, kc, HTOK * h:HTOK * (h + 1)]).then_inc(h_ps, 1)
                        if i < 2 or i >= MC:
                            chain(1)

                def fc2(t):
                    pe.wait_ge(gelu_done, 2 * MC * n + MC * (t // HT + 1))
                    if t >= 2:
                        pe.wait_ge(gated2, T * n + t - 1)
                    else:
                        pe.wait_ge(gated1, T * (n + 1))
                    for m in range(MC):
                        rows = P if m < MC - 1 else R + 1
                        mm = pe.matmul(ps[:, FC2_BANK[t % 2], 0:D], hT[0:rows, m, t * P:(t + 1) * P], w2[0:rows, s, m, :],
                                       start=m == 0, stop=m == MC - 1)
                    mm.then_inc(m_ps, 1)
                    chain(1)

                fc1(0)
                fc1(1)
                for t in range(T):
                    fc2(t)

        @block.vector
        def _(v):
            own = [0]

            def link(ins):
                own[0] += 1
                ins.then_inc(dve, 1)
                v.wait_ge(dve, own[0])

            link(v.memset(sT[64:P, :, :], 1.0))
            v.memset(xmT[64:P, :, :], 1.0)
            v.memset(oT[64:P, :, :, :], 1.0)
            v.memset(qk_eps[:], QK_EPS)
            v.memset(half_neg[:], -0.5).then_inc(ones_set, 1)

            def modulation(n):
                v.wait_ge(ada_ps, n + 1)
                src = ps[0:C, 6, 0:8 * SEQ].rearrange("p (k m) -> p k m", k=4)
                dst = mod[:, n].rearrange("p k c b -> p k (c b)")
                v.tensor_copy(dst[:, 0:4:2], src[:, 0:4:2])
                v.tensor_scalar(dst[:, 1:4:2], src[:, 1:4:2], 1.0, None, ALU.add).then_inc(ada_sb, 1)

            def chain_step(j):
                if j < R:
                    k = j
                    v.wait_ge(bc_ps, k + 1)
                    link(v.reciprocal(RD[:, k:k + 1], ps[0:R, 7, k:k + 1]))
                    link(v.scalar_tensor_tensor(out=fcol[:, k:k + 1], in0=W[:, k:k + 1], scalar=RD[:, k:k + 1],
                                                in1=neg_below[:, k:k + 1], op0=ALU.mult, op1=ALU.mult))
                    link(v.scalar_tensor_tensor(out=W[:], in0=ps[0:R, 7, 0:R], scalar=fcol[:, k:k + 1], in1=W[:],
                                                op0=ALU.mult, op1=ALU.add))
                    v.tensor_copy(W[:, k:k + 1], fcol[:, k:k + 1]).then_inc(w_ready, 1)
                    if k == R - 1:
                        v.wait_ge(w_ready, R + 1)
                        v.tensor_tensor(W[:], W[:], ident[0:R, 0:R], ALU.add).then_inc(lit_in, 1)
                        link(v.tensor_tensor(SG[:], RD[:], ident[0:R, 0:R], ALU.mult))
                        v.tensor_reduce(dg[:, 0:1], SG[:], AX.X, ALU.add).then_inc(diag_ready, 1)
                elif j == R:
                    v.wait_ge(lit_ps, 1)
                    v.tensor_copy(LiT[:], ps[0:R, 7, 0:R]).then_inc(lit_sb, 1)
                elif j == R + 1:
                    v.wait_ge(ut_ps, 1)
                    v.wait_ge(isd_ready, 1)
                    link(v.tensor_scalar(UT[:], ps[0:R, 7, 0:D], dg[:, 1:2], None, ALU.mult))
                    v.tensor_copy(M[:], UT[:, 0:R]).then_inc(m_ready, 1)
                elif j < CHAIN - 1:
                    k = j - R - 2
                    v.wait_ge(bc_ps, R + k + 1)
                    alpha = ps[0:R, 7, k:k + 1]
                    link(v.tensor_scalar(SG[:, k:k + 1], alpha, 0.0, 2.0, ALU.is_ge, ALU.mult))
                    link(v.scalar_tensor_tensor(out=piv[:, 0:1], in0=SG[:, k:k + 1], scalar=-1.0, in1=alpha,
                                                op0=ALU.add, op1=ALU.add))
                    link(v.reciprocal(piv[:, 1:2], piv[:, 0:1]))
                    link(v.scalar_tensor_tensor(out=piv[:, 2:3], in0=M[:, k:k + 1], scalar=piv[:, 1:2],
                                                in1=neg_below[:, k:k + 1], op0=ALU.mult, op1=ALU.mult))
                    v.scalar_tensor_tensor(out=M[:], in0=ps[0:R, 7, 0:R], scalar=piv[:, 2:3], in1=M[:],
                                           op0=ALU.mult, op1=ALU.add).then_inc(m_ready, 1)
                    v.wait_ge(m_ready, k + 2)
                    if k == R - 1:
                        link(v.tensor_tensor(RD[:], SG[:], ident[0:R, 0:R], ALU.mult))
                        link(v.tensor_reduce(dg[:, 2:3], RD[:], AX.X, ALU.add))
                        link(v.tensor_scalar(dg[:, 3:4], dg[:, 2:3], -1.0, 1.0, ALU.mult, ALU.add))
                        v.tensor_scalar(UT[:], UT[:], dg[:, 3:4], None, ALU.mult).then_inc(ut_ready, 1)
                else:
                    v.wait_ge(u_ps, 1)
                    for i in range(2):
                        ins = v.tensor_copy(U[:, :, i, :], ps[0:C, 7, 0:2 * R].rearrange("p (c r) -> p c r", c=2))
                    ins.then_inc(u_sb, 1)

            chain_at = [0]

            def chain(steps):
                first, chain_at[0] = chain_at[0], min(chain_at[0] + steps, CHAIN)
                for j in range(first, chain_at[0]):
                    chain_step(j)

            cf = [1.0 / factorial(i) for i in range(9)]

            def pair_banks(banks):
                return ps[:, banks[0]:banks[1] + 1, :].rearrange("p a (m r) -> p a m r", r=R)

            def halves(buf):
                return buf.rearrange("p (a m) r -> p a m r", a=2)

            eye_p = [ident[R * p:R * p + R, R * p:R * p + R].unsqueeze(1).to_broadcast([R, PAIRS, R]) for p in range(2)]

            def add_eye(buf, c):
                for p in range(2):
                    ins = v.scalar_tensor_tensor(out=buf[R * p:R * p + R], in0=eye_p[p], scalar=c,
                                                 in1=buf[R * p:R * p + R], op0=ALU.mult, op1=ALU.add)
                return ins

            def expm(e):
                if e == 1:
                    v.wait_ge(ex_act, 1)
                    link(v.tensor_scalar(pol, A2, cf[8], None, ALU.mult))
                    link(v.scalar_tensor_tensor(out=pol, in0=A, scalar=cf[7], in1=pol, op0=ALU.mult, op1=ALU.add))
                    add_eye(pol, cf[6]).then_inc(ex_dve, 1)
                elif e == 2:
                    link(v.tensor_scalar(EF[:, 0], A2, cf[5], None, ALU.mult))
                    link(v.scalar_tensor_tensor(out=EF[:, 0], in0=A, scalar=cf[4], in1=EF[:, 0], op0=ALU.mult, op1=ALU.add))
                    link(add_eye(EF[:, 0], cf[3]))
                    v.wait_ge(ex_ps, 3)
                    v.scalar_tensor_tensor(out=halves(pol), in0=pair_banks(EX0), scalar=-1.0, in1=halves(EF[:, 0]),
                                           op0=ALU.mult, op1=ALU.add).then_inc(ex_dve, 1)
                elif e == 3:
                    v.wait_ge(ex_dve, 2)
                    link(v.scalar_tensor_tensor(out=EF[:, 0], in0=A2, scalar=cf[2], in1=A, op0=ALU.mult, op1=ALU.add))
                    link(add_eye(EF[:, 0], 1.0))
                    v.wait_ge(ex_ps, 4)
                    v.scalar_tensor_tensor(out=halves(EF[:, 0]), in0=pair_banks(EX1), scalar=-1.0, in1=halves(EF[:, 0]),
                                           op0=ALU.mult, op1=ALU.add).then_inc(ex_dve, 1)
                elif e == EXPM - 1:
                    v.wait_ge(ex_ps, 5 + 2 * SQUARINGS - 1)
                    link(v.tensor_copy(halves(A3[:]), pair_banks(EX0)))
                    add_eye(A3, -1.0).then_inc(ex_dve, 1)

            def ln_stats(i, h):
                if i == 0:
                    v.wait_ge(ld_x, 16)
                elif i == 4:
                    v.wait_ge(x_rot, HT * (h + 1))
                elif i % 2 == 0:
                    v.wait_ge(x_end, x_updates(i // 2) - HT * (1 - h))
                else:
                    v.wait_ge(x_mid, T * (i // 2) + HT * (h + 1))
                for t in range(HT * h, HT * h + HT):
                    ins = v.bn_stats(bn[:, t, :], x[:, t, :])
                link(ins)
                for t in range(HT * h, HT * h + HT):
                    ins = v.bn_aggr(mv[:, t, :], bn[:, t, :])
                ins.then_inc(stats_ready, 1)

            def ln_apply(i, h):
                v.wait_ge(rstd_ready, 2 * i + h + 1)
                if i >= 1:
                    v.wait_ge(xnT_ps, 2 * i + h - 1)
                for t in range(HT * h, HT * h + HT):
                    ins = v.tensor_scalar(xn[:, t, :], x[:, t, :], mv[:, t, 0:1], rstd[:, t:t + 1],
                                          ALU.subtract, ALU.mult)
                ins.then_inc(xn_ready, 1)

            def modulate(i, h):
                n, k = i // 2, 2 * (i % 2)
                if i == 0:
                    v.wait_ge(ada_sb, 1)
                v.wait_ge(xnT_ps, 2 * i + h + 1)
                b0 = HT * B * h
                dst = xmT[0:C, :, HTOK * h:HTOK * (h + 1)].rearrange("p c (b t) -> p c b t", t=TOK)
                scale = mod[:, n, k + 1, :, b0:b0 + HT * B].unsqueeze(3).to_broadcast([C, 2, HT * B, TOK])
                shift = mod[:, n, k, :, b0:b0 + HT * B].unsqueeze(3).to_broadcast([C, 2, HT * B, TOK])
                link(v.tensor_tensor(dst, ps[0:C, 2 * h:2 * h + 2, :].rearrange("p c (b t) -> p c b t", t=TOK),
                                     scale, ALU.mult))
                v.tensor_tensor(dst, dst, shift, ALU.add).then_inc(mod_done, 1)

            for n in range(NB):
                if n == 0:
                    v.wait_ge(gram_ps, 1)
                    v.tensor_copy(W[:], ps[0:R, 7, 0:R]).then_inc(w_ready, 1)
                    v.wait_ge(ld_id, 32)
                    chain(CH_START)
                if n == 2:
                    chain(CHAIN)
                    for t in range(T):
                        v.wait_ge(d_ps, t + 1)
                        v.tensor_tensor(x[:, t, :], x[:, t, :], ps[:, 6 + t % 2, 0:D], ALU.add).then_inc(x_rot, 1)
                if n != 1:
                    ln_stats(2 * n, 0)
                    ln_stats(2 * n, 1)
                    ln_apply(2 * n, 0)
                    if n == 0:
                        modulation(0)
                    modulate(2 * n, 0)
                else:
                    ln_stats(2 * n, 1)
                ln_apply(2 * n, 1)
                modulate(2 * n, 1)

                if n == 0:
                    chain(CH_QKV * HT)
                    v.wait_ge(ld_const, 16 * 4)
                    v.tensor_scalar(kscale[:], kmask[:], gb[:, 2:3], None, ALU.mult)
                    v.tensor_scalar(kbias[:], kmask[:], gb[:, 3:4], None, ALU.mult)
                    modulation(1)
                    chain(4)
                    modulation(2)
                    chain(CH_MOD - 4)

                na = n - 1

                def spread_keys(p):
                    v.wait_ge(k_sb, 4 * na + p + 1)
                    if na or p >= 2:
                        v.wait_ge(s_ps, T * n + 2 * p - 2)
                    for j in range(K_ACT, HC):
                        dst = kexp[0:C, p % 2, :, :, j, :]
                        src = kT[:].rearrange("p (c b t) -> p c b t", c=2, t=TOK)
                        if n == 1:
                            ins = v.tensor_scalar(dst, src, kscale[:, j:j + 1], kbias[:, j:j + 1], ALU.mult, ALU.add)
                        else:
                            ins = v.tensor_scalar(dst, src, kmask[:, j:j + 1], None, ALU.mult)
                    ins.then_inc(k_dve, 1)

                if n == 1:
                    for h in range(2):
                        qk = qkv[:, HT * h:HT * h + HT, 0:2 * D].rearrange("p t (g d) -> p t g d", d=DH)

                        def by_head(stat):
                            return stat[:].rearrange("p (t g) -> p t g", t=HT)

                        def over_head(stat):
                            return by_head(stat).unsqueeze(3).to_broadcast([P, HT, 2 * HEADS, DH])

                        v.wait_ge(qkv_sb, T * n + HT * (h + 1))
                        link(v.tensor_reduce(by_head(qk_sum), qk, AX.X, ALU.add))
                        link(v.tensor_scalar(qk_mean[:], qk_sum[:], 1.0 / DH, None, ALU.mult))
                        v.tensor_tensor(qk, qk, over_head(qk_mean), ALU.subtract).then_inc(qk_xc, 1)
                        if h == 1:
                            spread_keys(0)
                        v.wait_ge(qk_sq, h + 1)
                        v.tensor_reduce(by_head(qk_sum), xn[:].rearrange("p a (g d) -> p (a g) d", d=DH).rearrange(
                            "p (t g) d -> p t g d", t=HT), AX.X, ALU.add).then_inc(qk_ss, 1)
                        v.wait_ge(qk_rstd, h + 1)
                        link(v.reciprocal(qk_rs[:], qk_mean[:]))
                        v.tensor_tensor(qk, qk, over_head(qk_rs), ALU.mult).then_inc(qk_norm, 1)

                keys = TOK if n else HEADS

                def by_head(buf):
                    return buf[:, 0:HEADS * keys].rearrange("p (h k) -> p h k", h=HEADS)

                def shift_scores(t):
                    v.wait_ge(s_ps, T * n + t + 1)
                    s = by_head(ps[:, t % 2, :])
                    v.tensor_reduce(rowmax[:, t % 2, :], s, AX.X, ALU.max).then_inc(max_done, 1)
                    v.wait_ge(max_done, T * n + t + 1)
                    if na >= 0 and (na or t >= 2):
                        v.wait_ge(pT_ps, T * na + t - 1)
                    v.tensor_tensor(by_head(probs[:, t % 2, :]), s,
                                    rowmax[:, t % 2, :].unsqueeze(2).to_broadcast([P, HEADS, keys]),
                                    ALU.subtract).then_inc(sub_done, 1)

                def normalise(t):
                    v.wait_ge(o_ps, T * na + t + 1)
                    acc = ps[:, 6, 0:HEADS * VW].rearrange("p (h d) -> p h d", h=HEADS)
                    link(v.reciprocal(rinv[:, t % 2, :], acc[:, :, DH]))
                    if n or t >= 2:
                        v.wait_ge(oT_ps, T * n + t - 1)
                    v.tensor_tensor(o[:, t % 2, :].rearrange("p (h d) -> p h d", h=HEADS), acc[:, :, 0:DH],
                                    rinv[:, t % 2, :].unsqueeze(2).to_broadcast([P, HEADS, DH]),
                                    ALU.mult).then_inc(o_sb, 1)

                def sum_probs(t):
                    v.wait_ge(exp_done, t + 1)
                    link(v.tensor_reduce(rowmax[:, t % 2, :], by_head(probs[:, t % 2, :]), AX.X, ALU.add))
                    link(v.reciprocal(rinv[:, t % 2, :], rowmax[:, t % 2, :]))

                def weigh_heads(t):
                    prod = prod_pv.rearrange("p (h d k) -> p h d k", h=HEADS, d=DH)
                    if t >= 2:
                        v.wait_ge(o_stored, 16 * B * (t - 1))
                    v.wait_ge(pv_prod, t + 1)
                    dst = o_heads[:, t % 2].rearrange("p (h d) -> p h d", h=HEADS)
                    for hs in (slice(0, HC), slice(HC, HEADS)):
                        link(v.tensor_reduce(dst[:, hs], prod[:, hs], AX.X, ALU.add))
                        chain(CH_EXPM // 2)
                    v.tensor_tensor(dst, dst, rinv[:, t % 2, :].unsqueeze(2).to_broadcast([P, HEADS, DH]),
                                    ALU.mult).then_inc(heads_out, 1)

                def gate1(t):
                    v.wait_ge(pr_ps, T * n + t + 1)
                    if n == 0 and t == 0:
                        v.wait_ge(gate_sb, T * NB)
                    if t >= 4:
                        v.wait_ge(x_mid, T * n + t - 3)
                    elif n:
                        v.wait_ge(x_end, T * n)
                    v.tensor_tensor(delta[:, t % 4, :], ps[:, O_BANK[n], 0:D], gates[:, n, t, 0, :],
                                    ALU.mult).then_inc(gated1, 1)

                def gate2(t):
                    v.wait_ge(m_ps, T * n + t + 1)
                    if t >= 4:
                        v.wait_ge(x_end, T * n + t - 3)
                    else:
                        v.wait_ge(x_mid, T * (n + 1))
                    v.tensor_tensor(delta[:, t % 4, :], ps[:, FC2_BANK[t % 2], 0:D], gates[:, n, t, 1, :],
                                    ALU.mult).then_inc(gated2, 1)

                def mlp_norm(st):
                    if st == T:
                        ln_stats(2 * n + 1, 0)
                    if st == T + 1:
                        ln_apply(2 * n + 1, 0)
                    if st == ATT - 1:
                        modulate(2 * n + 1, 0)

                for st in range(0 if n else ATT):
                    if 0 <= st - 4 < T:
                        gate1(st - 4)
                    if 1 <= st <= T:
                        sum_probs(st - 1)
                    chain(CH_SUM)
                    if st < T:
                        shift_scores(st)
                    if 1 <= st <= T:
                        weigh_heads(st - 1)
                    elif st == 0:
                        chain(CH_GATES)
                    else:
                        chain(CH_EXPM)
                    if st == 0:
                        v.wait_ge(ld_v, 32)
                        v.tensor_tensor(A, A2, sgn[:].unsqueeze(1).to_broadcast([P, PAIRS, R]), ALU.mult).then_inc(a_ready, 1)
                        v.wait_ge(a_ready, 1)
                    elif st <= EXPM:
                        expm(st - 1)
                    mlp_norm(st)
                if n == 2:
                    spread_keys(0)
                for st in range(ATT if n else 0):
                    if st < T:
                        shift_scores(st)
                    if 0 <= st - 4 < T:
                        gate1(st - 4)
                    chain(CH_L1 // 2)
                    if st < T and st % 2 == 0 and st // 2 + 1 < T // 2:
                        spread_keys(st // 2 + 1)
                    if 0 <= st - 2 < T:
                        normalise(st - 2)
                    chain((CH_L1 + 1) // 2)
                    mlp_norm(st)
                ln_stats(2 * n + 1, 1)
                chain(2)
                ln_apply(2 * n + 1, 1)
                modulate(2 * n + 1, 1)
                chain(MC)
                for t in range(T):
                    gate2(t)
                    chain(1)
                    if n == 0 and t == HT:
                        ln_stats(2, 0)
                    if n == 0 and t == HT + 2:
                        ln_apply(2, 0)
                if n == 0:
                    modulate(2, 0)

        @block.scalar
        def _(a):
            a.dma_start(Pm[:], p_in).then_inc(ld_p, 16)
            a.dma_start(PT[:], pt_in).then_inc(ld_p, 16)
            a.wait_ge(ld_cond, 16)
            a.wait_ge(dve, 1)
            a.activation(sT[0:C], cT[:], ACT.Silu).then_inc(silu_done, 1)
            a.wait_ge(pads_set, 1)
            a.dma_start(wq[0:C + 1, 0], qkv_w[0]).then_inc(ld_wq[0], 16)
            for w, src in ((wp[0:C + 1], proj_w), (w1[0:C + 1], fc1_w), (w2, fc2_w)):
                a.dma_start(w[:, 0], src[0]).then_inc(ld_w[0], 16)
            a.dma_start(wq[0:C + 1, 1], qkv_w[1]).then_inc(ld_wq[1], 16)
            for w, src in ((wp[0:C + 1], proj_w), (w1[0:C + 1], fc1_w), (w2, fc2_w)):
                a.dma_start(w[:, 1], src[1]).then_inc(ld_w[1], 16)

            def gates_by_sequence(n):
                a.wait_ge(gseq_ps, n + 1)
                a.copy(gsb[:, n, :], ps[0:SEQ, 5, 0:2 * D]).then_inc(gseq_sb, 1)

            def pair_banks(banks):
                return ps[:, banks[0]:banks[1] + 1, :].rearrange("p a (m r) -> p a m r", r=R)

            def halves(buf):
                return buf.rearrange("p (a m) r -> p a m r", a=2)

            def expm(e):
                if e == 0:
                    a.wait_ge(ex_ps, 1)
                    a.mul(halves(A2), pair_banks(EX0), -1.0).then_inc(ex_act, 1)
                elif e == 1:
                    a.wait_ge(ex_ps, 2)
                    a.copy(halves(A3[:]), pair_banks(EX1)).then_inc(ex_act, 1)
                elif e == 4:
                    a.wait_ge(ex_ps, 5)
                    a.copy(halves(EF[:, 1]), pair_banks(EX0)).then_inc(ex_act, 1)
                elif 5 <= e < EXPM - 1:
                    i = e - 5
                    dst = EG if i % 2 == 0 else EF
                    a.wait_ge(ex_ps, 5 + 2 * i + 1)
                    a.copy(halves(dst[:, 0]), pair_banks(EX0))
                    a.wait_ge(ex_ps, 5 + 2 * i + 2)
                    a.copy(halves(dst[:, 1]), pair_banks(EX1)).then_inc(ex_act, 1)

            for n in range(NB):
                if n == 2:
                    for h in range(2):
                        a.wait_ge(xT_ps, h + 1)
                        a.copy(xmT[0:C, :, HTOK * h:HTOK * (h + 1)], ps[0:C, 2 * h:2 * h + 2, :]).then_inc(xT_sb, 1)
                    for h in range(2):
                        a.wait_ge(z_ps, h + 1)
                        a.copy(z_rot[:, h, :], ps[:, 4 + h, :]).then_inc(z_sb, 1)
                    for h in range(2):
                        a.wait_ge(y_ps, h + 1)
                        ydst = y_rot[0:R, h, :].rearrange("p (i q t) -> p i q t", q=2, t=TOK)
                        for p in range(2):
                            ins = a.copy(ydst[:, :, p, :], ps[0:R, 2 * h + p, 0:HTOK // 2].rearrange("p (i t) -> p i t", t=TOK))
                        ins.then_inc(y_sb, 1)

                def deviation(h):
                    a.wait_ge(qk_ss, h + 1)
                    a.activation(qk_mean[:], qk_sum[:], ACT.Sqrt, bias=qk_eps[:, 0:1], scale=1.0 / DH).then_inc(qk_rstd, 1)

                for t in range(T):
                    a.wait_ge(qkv_ps, T * n + t + 1)
                    if n == 2:
                        a.wait_ge(v_spread, 2)
                    a.copy(qkv[:, t, :], ps[:, 4 + t % 3, 0:QKV]).then_inc(qkv_sb, 1)
                    if n == 1 and t % HT == HT - 1:
                        h = t // HT
                        a.wait_ge(qk_xc, h + 1)
                        a.wait_ge(xnT_ps, 4 * n + 2)
                        a.activation(xn[:].rearrange("p a b -> p (a b)").rearrange("p (t g) -> p t g", t=HT),
                                     qkv[:, HT * h:HT * h + HT, 0:2 * D], ACT.Square).then_inc(qk_sq, 1)
                    if n == 1 and t == HT + 1:
                        deviation(0)
                if n == 0:
                    gates_by_sequence(0)
                    gates_by_sequence(1)
                    for r in range(2):
                        a.wait_ge(v_ps, r + 1)
                        a.copy(vsb[:, r, :], ps[:, r, :]).then_inc(v_sb, 1)
                    gates_by_sequence(2)

                na = n - 1

                def spread(p, part):
                    if part == 0:
                        a.wait_ge(qkT_ps, 4 * na + p + 1)
                        dst = qT[:, :, 2 * p * P:2 * (p + 1) * P]
                        src = ps[0:C, 4, :].rearrange("p (c t) -> p c t", c=2)
                        if n == 1:
                            a.activation(dst, src, ACT.Identity, bias=gb[:, 1:2], scale=gb[:, 0:1]).then_inc(q_sb, 1)
                        else:
                            a.copy(dst, src).then_inc(q_sb, 1)
                        if na or p:
                            a.wait_ge(k_dve, 4 * na + p)
                            a.wait_ge(k_act, 4 * na + p)
                        a.copy(kT[:], ps[0:C, 5, :]).then_inc(k_sb, 1)
                        a.wait_ge(k_sb, 4 * na + p + 1)
                        if na or p >= 2:
                            a.wait_ge(s_ps, T * n + 2 * p - 2)
                    for j in (range(0, 1) if part == 0 else range(1, K_ACT)):
                        dst = kexp[0:C, p % 2, :, :, j, :]
                        src = kT[:].rearrange("p (c b t) -> p c b t", c=2, t=TOK)
                        if n == 1:
                            ins = a.activation(dst, src, ACT.Identity, bias=kbias[:, j:j + 1], scale=kscale[:, j:j + 1])
                        else:
                            ins = a.activation(dst, src, ACT.Copy, scale=kmask[:, j:j + 1])
                    if part == 1:
                        ins.then_inc(k_act, 1)

                def exponential(t):
                    a.wait_ge(sub_done, T * n + t + 1)
                    p = probs[:, t % 2, 0:HEADS * (TOK if n else HEADS)]
                    a.activation(p, p, ACT.Exp, scale=DH ** -0.5).then_inc(exp_done, 1)

                def probs_out(t):
                    a.wait_ge(pT_ps, T * na + t + 1)
                    if na or t >= 2:
                        a.wait_ge(o_ps, T * na + t - 1)
                    a.copy(probsT[:, t % 2, :], ps[:, 2, :]).then_inc(pT_sb, 1)

                def o_out(t):
                    a.wait_ge(oT_ps, T * n + t + 1)
                    if n or t >= 2:
                        a.wait_ge(pr_ps, T * n + t - 1)
                    a.copy(oT[0:C, t % 2], ps[0:C, O_BANK[n], 0:2 * P].rearrange("p (c t) -> p c t", c=2)).then_inc(oT_sb, 1)

                if n:
                    spread(0, 0)
                    if n == 1:
                        deviation(1)
                    spread(0, 1)
                for st in range(0 if n else ATT):
                    if st == 0:
                        for i in range(NB * T):
                            a.wait_ge(gate_ps, i + 1)
                            a.copy(gates[:, i // T, i % T].rearrange("p g f -> p (g f)"),
                                   ps[:, SPREAD_BANK[i % 3], 0:2 * D]).then_inc(gate_sb, 1)
                            if i == 5:
                                exponential(0)
                    elif st < T:
                        exponential(st)
                    if 1 <= st <= EXPM:
                        expm(st - 1)
                    if 0 <= st - 3 < T:
                        o_out(st - 3)
                for st in range(ATT if n else 0):
                    if st // 2 + 1 < T // 2:
                        spread(st // 2 + 1, st % 2)
                    if 0 <= st - 1 < T:
                        probs_out(st - 1)
                    if st < T:
                        exponential(st)
                    if 0 <= st - 3 < T:
                        o_out(st - 3)

                for i in range(2 * MC):
                    h, m = divmod(i, MC)
                    a.wait_ge(h_ps, 2 * MC * n + i + 1)
                    if n:
                        a.wait_ge(m_ps, T * (n - 1) + HT * (h + 1))
                    rows = min(P, MLP - P * m)
                    a.activation(hT[0:rows, m, HTOK * h:HTOK * (h + 1)], ps[0:rows, 4 + i % 2, :],
                                 ACT.Gelu if n < 2 else ACT.Gelu_apprx_tanh).then_inc(gelu_done, 1)

        @block.gpsimd
        def _(g):
            own = [0]

            def link(ins):
                own[0] += 1
                ins.then_inc(pool_own, 1)
                g.wait_ge(pool_own, own[0])

            for w in (wq, wp, w1):
                ins = g.memset(w[64:P], 0.0)
            link(ins)
            g.sem_inc(pads_set, 1)
            g.wait_ge(ones_set, 1)
            link(g.tensor_scalar(dg[:, 2:3], half_neg[0:R, 0:1], -1.0, None, ALU.mult))

            def add_delta(n, t, gated, done):
                g.wait_ge(gated, T * n + t + 1)
                g.tensor_tensor(x[:, t, :], x[:, t, :], delta[:, t % 4, :], ALU.add).then_inc(done, 1)

            def ln_rstd(i, h):
                t = slice(HT * h, HT * h + HT)
                g.wait_ge(stats_ready, 2 * i + h + 1)
                link(g.tensor_scalar(veps[:, t], mv[:, t, 1], EPS, None, ALU.add))
                g.tensor_tensor(rstd[:, t], veps[:, t], half_neg[:].to_broadcast([P, HT]), ALU.pow).then_inc(rstd_ready, 1)

            for n in range(NB):
                if n != 1:
                    ln_rstd(2 * n, 0)
                ln_rstd(2 * n, 1)
                if n == 0:
                    def weigh_values(t):
                        g.wait_ge(exp_done, t + 1)
                        if t:
                            g.wait_ge(heads_out, t)
                        pr = probs[:, t % 2, 0:HEADS * HEADS].rearrange("p (h k) -> p h k", h=HEADS)
                        values = qkv[:, t, 2 * D:].rearrange("p (k d) -> p d k", k=HEADS)
                        g.tensor_tensor(prod_pv.rearrange("p (h d k) -> p h d k", h=HEADS, d=DH),
                                        pr.unsqueeze(2).to_broadcast([P, HEADS, DH, HEADS]),
                                        values.unsqueeze(1).to_broadcast([P, HEADS, DH, HEADS]),
                                        ALU.mult).then_inc(pv_prod, 1)

                    g.wait_ge(v_ps, 2)
                    for t in range(T):
                        g.wait_ge(qkv_sb, t + 1)
                        if t == 1:
                            g.wait_ge(gseq_ps, NB)
                        if t >= 2:
                            g.wait_ge(s_ps, t - 1)
                        q_, k_ = (qkv[:, t, i * D:(i + 1) * D].rearrange("p (h d) -> p d h", h=HEADS) for i in range(2))
                        g.tensor_tensor(prod_slot[t % 2].rearrange("p (d h k) -> p d h k", d=DH, h=HEADS),
                                        q_.unsqueeze(3).to_broadcast([P, DH, HEADS, HEADS]),
                                        k_.unsqueeze(2).to_broadcast([P, DH, HEADS, HEADS]),
                                        ALU.mult).then_inc(qk_prod, 1)
                        if t >= 1:
                            weigh_values(t - 1)
                        if t >= 6:
                            add_delta(n, t - 6, gated1, x_mid)
                    weigh_values(T - 1)
                for h in range(2 if n else 0):
                    g.wait_ge(qkv_sb, T * n + HT * (h + 1))
                    if n == 2:
                        g.wait_ge(o_ps, T)
                    for b in range(B):
                        for q in range(G4):
                            src = qkv[TOK * b:TOK * b + TOK, HT * h:HT * h + HT, 2 * D:].rearrange(
                                "p t (g s d) -> p t g s d", g=4, s=G4)[:, :, :, q, :]
                            dst = vexp[TOK * q:TOK * q + TOK].rearrange(
                                "p (t b) g (s d) -> p t b g s d", b=B, s=G4)[:, HT * h:HT * h + HT, b, :, q, 0:DH]
                            link(g.tensor_copy(dst, src))
                    g.sem_inc(v_spread, 1)
                for t in range(0 if n else 2, T):
                    if n == 0 and t == ISD_TILE:
                        g.wait_ge(diag_ready, 1)
                        g.tensor_tensor(dg[:, 1:2], dg[:, 0:1], dg[:, 2:3], ALU.pow).then_inc(isd_ready, 1)
                    add_delta(n, t, gated1, x_mid)
                    if t == HT:
                        if n == 0:
                            g.wait_ge(x_mid, HT + 1)
                            link(g.memset(hT[R:P, MC - 1, :], 1.0))
                        ln_rstd(2 * n + 1, 0)
                ln_rstd(2 * n + 1, 1)
                if n == 0:
                    g.wait_ge(st_v, 16 * 2 * B)
                    g.wait_ge(gate_ps, T * NB)
                    g.wait_ge(rstd_ready, 4)
                    link(g.memset(vexp[:], 0.0))
                    for q in range(B):
                        link(g.memset(vexp[32 * q:32 * q + 32].rearrange(
                            "p s g (h d) -> p (s g) h d", h=G4)[:, :, q, DH:VW], 1.0))
                for t in range(T):
                    add_delta(n, t, gated2, x_end)
                    if n == 0 and t == HT:
                        ln_rstd(2, 0)


def with_bias_row(w, b):
    n = w.shape[1]
    o = np.zeros((C + 1, 2, n), np.float32)
    o[0:C, 0], o[0:C, 1], o[C, 0] = w[0:C], w[C:D], b
    return o


def kernel(**inputs):
    import concourse.bacc as _bacc
    from concourse import mybir as _mybir
    from concourse.bass_utils import run_bass_kernel_spmd as _run

    a = {k: np.asarray(v) for k, v in inputs.items()}
    names = {"ada": ("L0_cond_ada_w", "L0_cond_ada_b", "L1_cond_w_ada", "L1_cond_b_ada", "L3_cond_W_ada", "L3_cond_b_ada"),
             "qkv": ("L0_cond_qkv_w", "L0_cond_qkv_b", "L1_cond_w_qkv", "L1_cond_b_qkv", "L3_cond_W_qkv", "L3_cond_b_qkv"),
             "proj": ("L0_cond_proj_w", "L0_cond_proj_b", "L1_cond_w_proj", "L1_cond_b_proj", "L3_cond_W_proj", "L3_cond_b_proj"),
             "fc1": ("L0_cond_fc1_w", "L0_cond_fc1_b", "L1_cond_w1", "L1_cond_b1", "L3_cond_W_fc1", "L3_cond_b_fc1"),
             "fc2": ("L0_cond_fc2_w", "L0_cond_fc2_b", "L1_cond_w2", "L1_cond_b2", "L3_cond_W_fc2", "L3_cond_b_fc2")}
    packed = {k: np.stack([with_bias_row(a[v[2 * i]], a[v[2 * i + 1]]) for i in range(NB)])
              for k, v in names.items() if k != "fc2"}
    fc2 = np.zeros((NB, MC * P, D), np.float32)
    for i in range(NB):
        fc2[i, 0:MLP], fc2[i, MLP] = a[names["fc2"][2 * i]], a[names["fc2"][2 * i + 1]]
    fc2 = np.ascontiguousarray(fc2.reshape(NB, MC, P, D).transpose(0, 2, 1, 3))
    cond = a["cond_1152"]
    cond_t = np.ascontiguousarray(cond.T.reshape(2, C, SEQ).transpose(1, 0, 2))
    gbs = np.stack([np.tile(a[k], HC) for k in ("L1_cond_qn_g", "L1_cond_qn_b", "L1_cond_kn_g", "L1_cond_kn_b")], 1)
    iu, ju = np.triu_indices(R, k=1)
    at = np.zeros((R, R), np.int64)
    at[iu, ju] = at[ju, iu] = np.arange(len(iu))
    rot = with_bias_row(a["L2_cond_W"][at.reshape(-1)].T, a["L2_cond_b"][at.reshape(-1)])
    pm = a["L2_cond_P"]
    f = np.float32
    scale = 2.0 ** -SQUARINGS
    ij = np.sign(np.arange(R)[None] - np.arange(R)[:, None])
    arrays = {
        "x_in": a["x"].reshape(SEQ * TOK, D), "cond_t": cond_t, "ada_w": packed["ada"], "qkv_w": packed["qkv"],
        "proj_w": packed["proj"], "fc1_w": packed["fc1"], "fc2_w": fc2, "qk_gb": gbs, "rot_w": rot,
        "p_in": np.ascontiguousarray(pm.reshape(2, C, R).transpose(1, 0, 2)), "pt_in": np.ascontiguousarray(pm.T),
        "eye": np.eye(P, dtype=f),
        "head_mask": (np.arange(C)[:, None] // DH == np.arange(HC)[None]).astype(f),
        "below": -(np.arange(R)[:, None] > np.arange(R)[None]).astype(f),
        "seq_mask": np.repeat(np.eye(SEQ, dtype=f), TOK, axis=1),
        "skew": (np.concatenate([ij, ij]) * scale).astype(f),
    }
    nc = _bacc.Bacc("TRN2", target_bir_lowering=False, num_devices=1)
    args, fed = [], {}
    for name, v in arrays.items():
        v = np.ascontiguousarray(v)
        fed[name + "_dram"] = v
        args.append(nc.dram_tensor(name + "_dram", v.shape, _mybir.dt.from_np(v.dtype), kind="ExternalInput").ap())
    args.append(nc.dram_tensor("out_dram", (SEQ * TOK, D), F32, kind="ExternalOutput").ap())
    fused_blocks(nc, *args)
    r = _run(nc, [fed], core_ids=[0])
    return r.results[0]["out_dram"].reshape(SEQ, TOK, D)
```

```python
from contextlib import ExitStack
from math import factorial

import numpy as np

import concourse.bass as bass
from concourse import mybir

F32 = mybir.dt.float32
ALU = mybir.AluOpType
ACT = mybir.ActivationFunctionType
AX = mybir.AxisListType

P = 128
SEQ, TOK, D = 32, 32, 144
T = SEQ * TOK // P
B = P // TOK
C = D // 2
HEADS, DH = 16, 9
HC = HEADS // 2
QKV = 3 * D
VW = DH + 1
G4 = 4
MLP = 4 * D
MC = 5
HT = T // 2
HTOK = HT * P
R = 64
PAIRS = SEQ // 2
SQUARINGS = 5
EPS, QK_EPS = 1e-6, 1e-5
NB = 3
PAIR_STEPS = R // 2
CHAIN = 2 * PAIR_STEPS + 3
ROW2 = P
CH_START, CH_QKV, CH_MOD, CH_GATES = 3, 1, 3, 1
CH_SUM, CH_EXPM, CH_TAIL, CH_L1 = 2, 2, 0, 0
ISD_STEP = 1 + (PAIR_STEPS + 1 - CH_START - 4 * CH_QKV - CH_MOD - CH_SUM - CH_GATES) // (CH_SUM + CH_EXPM)
assert ISD_STEP <= T
EXPM = 5 + SQUARINGS
EXPM_AT = [()] + [(0, 1)] + [(e,) for e in range(2, EXPM)]


def share(steps, i, places):
    return steps * (i + 1) // places - steps * i // places


def fused_blocks(nc, x_in, cond_t, ada_w, qkv_w, proj_w, fc1_w, fc2_w, qk_gb, rot_w, p_in, pt_in,
                 eye, head_mask, below, seq_mask, skew, out):
    with ExitStack() as ctx:
        def sb(name, shape):
            return ctx.enter_context(nc.sbuf_tensor(name, shape, F32))

        def sem(name):
            return ctx.enter_context(nc.semaphore(name))

        ps = ctx.enter_context(nc.psum_tensor("ps", [P, 8, 512], F32))

        x = sb("x", [P, T, D])
        xn = sb("xn", [P, T, D])
        xmT = sb("xmT", [P, 2, T * P])
        qkv = sb("qkv", [P, T, QKV])
        qT = sb("qT", [C, 2, T * P])
        kT = sb("kT", [C, 4 * P])
        kexp = sb("kexp", [P, 2, 2, 2 * B, HC, TOK])
        vexp = sb("vexp", [P, SEQ, 4, G4 * VW])
        probs = sb("probs", [P, 2, HEADS * TOK])
        probsT = sb("probsT", [P, 2, HEADS * TOK])
        rowmax = sb("rowmax", [P, 2, HEADS])
        rinv = sb("rinv", [P, 2, HEADS])
        o = sb("o", [P, 2, D])
        oT = sb("oT", [P, 2, 2, P])
        delta = sb("delta", [P, 4, D])
        hT = sb("hT", [P, MC, T * P])
        gates = sb("gates", [P, NB, T, 2, D])
        mod = sb("mod", [C, NB, 4, 2, SEQ])
        bn = sb("bn", [P, T, 6])
        mv = sb("mv", [P, T, 2])
        rstd = sb("rstd", [P, T])
        veps = sb("veps", [P, T])
        qk_sum = sb("qk_sum", [P, 4 * 2 * HEADS])
        qk_mean = sb("qk_mean", [P, 4 * 2 * HEADS])
        qk_rs = sb("qk_rs", [P, 4 * 2 * HEADS])
        wq = sb("wq", [P, 2, 2, QKV])
        wp = sb("wp", [P, 2, 2, D])
        w1 = sb("w1", [P, 2, 2, MLP])
        w2 = sb("w2", [P, 2, MC, D])
        ident = sb("ident", [P, P])
        kmask = sb("kmask", [C, HC])
        kscale = sb("kscale", [C, HC])
        kbias = sb("kbias", [C, HC])
        gb = sb("gb", [C, 4])
        half_neg = sb("half_neg", [P, 1])
        qk_eps = sb("qk_eps", [P, 1])
        cT = sb("cT", [C, 2, SEQ])
        sT = sb("sT", [P, 2, SEQ])
        neg_below = sb("neg_below", [R, R])
        W = sb("W", [R, 2 * R])
        M = sb("M", [R, R])
        fcol = sb("fcol", [R, R])
        RD = sb("RD", [R, R])
        SG = sb("SG", [R, R])
        piv = sb("piv", [R, 3])
        dg = sb("dg", [R, 4])
        LiT = sb("LiT", [R, R])
        PT = sb("PT", [R, D])
        Pm = sb("Pm", [C, 2, R])
        row2 = Pm[0:R].rearrange("p c r -> p (c r)")
        UT = sb("UT", [R, D])
        U = sb("U", [C, 2, 2, R])
        sgn = sb("sgn", [P, R])
        eye_pair = sgn
        EG = sb("EG", [P, 2, PAIRS, R])
        A, A2 = EG[:, 0], EG[:, 1]
        A3 = sb("A3", [P, PAIRS, R])
        EF = sb("EF", [P, 2, PAIRS, R])
        pol = EF[:, 1]
        kexp_flat = kexp[:].rearrange("p a c b h k -> p (a c b h k)")
        rotw = kexp_flat[0:C + 1].rearrange("p (c n) -> p c n", c=2)
        NP = HEADS * HEADS * DH
        prod_qk = kexp_flat[:, 0:NP]
        o_heads = kexp_flat[:, 2 * NP:2 * NP + 2 * D].rearrange("p (i f) -> p i f", i=2)
        vsb = vexp[:].rearrange("p a b c -> p (a b c)")[:, 0:1024].rearrange("p (r n) -> p r n", r=2)
        spread_seq = vexp[:].rearrange("p a b c -> p (a b c)")[0:SEQ, 1024:1024 + T * P]
        gsb = vexp[:].rearrange("p a b c -> p (a b c)")[0:SEQ, 2048:2048 + 6 * D].rearrange("p (l n) -> p l n", l=NB)
        hT_flat = hT[:].rearrange("p a b -> p (a b)")
        prod_slot = [prod_qk, hT_flat[:, 0:NP]]
        prod_pv = [hT_flat[:, NP:2 * NP], kexp_flat[:, NP:2 * NP]]
        adaw = hT[:].rearrange("p a b -> p (a b)")[0:C + 1, 0:2 * 2 * 6 * D].rearrange(
            "p (l c n) -> p l c n", l=2, c=2)
        z_rot, y_rot = probs, probsT
        o_dram = nc.dram_tensor("o_scratch", (SEQ, HEADS, TOK, DH), F32, kind="Internal").ap()
        v_dram = nc.dram_tensor("v_scratch", (R, SEQ, R), F32, kind="Internal").ap()

        ld_const, ld_cond, ld_x, ld_p = sem("ld_const"), sem("ld_cond"), sem("ld_x"), sem("ld_p")
        ld_ada = [sem(f"ld_ada{n}") for n in range(NB)]
        ld_rot, ld_v, st_v = sem("ld_rot"), sem("ld_v"), sem("st_v")
        ld_id, pads_set = sem("ld_id"), sem("pads_set")
        ld_wq = [sem(f"ld_wq{n}") for n in range(NB)]
        ld_w = [sem(f"ld_w{n}") for n in range(NB)]
        silu_done, ones_set, ada_ps, ada_sb = sem("silu_done"), sem("ones_set"), sem("ada_ps"), sem("ada_sb")
        gseq_ps, gseq_sb, gate_ps, gate_sb = sem("gseq_ps"), sem("gseq_sb"), sem("gate_ps"), sem("gate_sb")
        v_ps, v_sb = sem("v_ps"), sem("v_sb")
        dve = sem("dve")
        act_own = sem("act_own")
        pool_own = sem("pool_own")
        gram_ps, w_ready, bc_ps, m_ready = sem("gram_ps"), sem("w_ready"), sem("bc_ps"), sem("m_ready")
        lit_in, lit_ps, lit_sb, ut_ps, ut_ready, u_ps, u_sb = (
            sem(s) for s in ("lit_in", "lit_ps", "lit_sb", "ut_ps", "ut_ready", "u_ps", "u_sb"))
        diag_ready, isd_ready = sem("diag_ready"), sem("isd_ready")
        a_ready, ex_ps, ex_act, ex_dve, ex_pol = (sem(s) for s in ("a_ready", "ex_ps", "ex_act", "ex_dve", "ex_pol"))
        stats_ready, rstd_ready, xn_ready = sem("stats_ready"), sem("rstd_ready"), sem("xn_ready")
        xnT_ps, mod_done = sem("xnT_ps"), sem("mod_done")
        qkv_ps, qkv_sb = sem("qkv_ps"), sem("qkv_sb")
        qk_xc, qk_sq, qk_ss, qk_rstd, qk_norm = (sem(s) for s in ("qk_xc", "qk_sq", "qk_ss", "qk_rstd", "qk_norm"))
        v_spread = sem("v_spread")
        qkT_ps, q_sb, k_sb, k_act, k_dve = sem("qkT_ps"), sem("q_sb"), sem("k_sb"), sem("k_act"), sem("k_dve")
        s_ps, max_done, sub_done, exp_done = sem("s_ps"), sem("max_done"), sem("sub_done"), sem("exp_done")
        pT_ps, pT_sb, o_ps, o_sb = sem("pT_ps"), sem("pT_sb"), sem("o_ps"), sem("o_sb")
        oT_ps, oT_sb, pr_ps, gated1, x_mid = sem("oT_ps"), sem("oT_sb"), sem("pr_ps"), sem("gated1"), sem("x_mid")
        pv_prod = sem("pv_prod")
        qk_prod, heads_out, o_stored = sem("qk_prod"), sem("heads_out"), sem("o_stored")
        o_back = [sem("o_back0"), sem("o_back1")]
        h_ps, gelu_done, m_ps, gated2, x_end = sem("h_ps"), sem("gelu_done"), sem("m_ps"), sem("gated2"), sem("x_end")
        xT_ps, xT_sb, z_ps, z_sb, y_ps, y_sb, d_ps, x_rot = (
            sem(s) for s in ("xT_ps", "xT_sb", "z_ps", "z_sb", "y_ps", "y_sb", "d_ps", "x_rot"))
        stored = sem("stored")

        LNS = 2 * NB
        ATT = T + 4
        ATT0 = T + 3
        FC2_BANK = (6, 3)
        QKV_FIRST = (T, T, HT)
        QKV_BANK = [[4 + t % 3 if t < QKV_FIRST[n] else 7 for t in range(T)] for n in range(NB)]
        SPREAD_BANK = [2 + i % 3 if i < T else i % 2 for i in range(NB * T)]
        O_BANK = (2, 3, 3)
        cf = [1.0 / factorial(i) for i in range(9)]
        EX0, EX1 = (3, 4), (5, 6)
        K_ACT = 3

        def x_updates(n):
            return T * n

        block = ctx.enter_context(nc.Block())

        @block.sync
        def _(sp):
            sp.dma_start(cT[:], cond_t).then_inc(ld_cond, 16)
            sp.dma_start(ident[:], eye).then_inc(ld_id, 16)
            sp.dma_start(neg_below[:], below).then_inc(ld_id, 16)
            sp.dma_start(adaw[:, 0], ada_w[0]).then_inc(ld_ada[0], 16)
            sp.dma_start(x[:], x_in.rearrange("(t p) f -> p t f", p=P)).then_inc(ld_x, 16)
            sp.dma_start(adaw[:, 1], ada_w[1]).then_inc(ld_ada[1], 16)
            sp.dma_start(rotw[:], rot_w).then_inc(ld_rot, 16)
            sp.dma_start(kmask[:], head_mask).then_inc(ld_const, 16)
            sp.dma_start(sgn[:], skew).then_inc(ld_const, 16)
            sp.dma_start(spread_seq, seq_mask).then_inc(ld_const, 16)
            sp.dma_start(gb[:], qk_gb).then_inc(ld_const, 16)
            sp.wait_ge(ada_ps, 1)
            sp.wait_ge(gseq_ps, 1)
            sp.dma_start(adaw[:, 0], ada_w[2]).then_inc(ld_ada[2], 16)
            for r in range(2):
                sp.wait_ge(v_sb, r + 1)
                for q in range(B):
                    i0 = (r * B + q) * 8
                    sp.dma_start(v_dram[i0:i0 + 8].rearrange("i b j -> b i j"),
                                 vsb[32 * q:32 * q + 32, r].rearrange("b (i j) -> b i j", i=8)).then_inc(st_v, 16)
            sp.wait_ge(st_v, 16 * 2 * B)
            for p in range(2):
                sp.dma_start(EG[R * p:R * p + R, 1], v_dram[:, p:SEQ:2, :]).then_inc(ld_v, 16)
            for t in range(T):
                sp.wait_ge(heads_out, t + 1)
                for b in range(B):
                    sp.dma_start(o_dram[B * t + b].rearrange("h t d -> t h d"),
                                 o_heads[TOK * b:TOK * b + TOK, t % 2].rearrange("p (h d) -> p h d", h=HEADS)
                                 ).then_inc(o_stored, 16)
                sp.wait_ge(o_stored, 16 * B * (t + 1))
                if t >= 2:
                    sp.wait_ge(oT_ps, t - 1)
                sp.dma_start(o[:, t % 2, :], o_dram.rearrange("n h t d -> (n h t d)").rearrange(
                    "(i p f) -> i p f", p=P, f=D)[t]).then_inc(o_back[t % 2], 16)
            sp.wait_ge(m_ps, T)
            sp.dma_start(wq[0:C + 1, 0], qkv_w[2]).then_inc(ld_wq[2], 16)
            for w, src in ((wp[0:C + 1], proj_w), (w1[0:C + 1], fc1_w), (w2, fc2_w)):
                sp.dma_start(w[:, 0], src[2]).then_inc(ld_w[2], 16)
            for h in range(2):
                sp.wait_ge(x_end, T * (NB - 1) + HT * (h + 1))
                sp.dma_start(out.rearrange("(t p) f -> p t f", p=P)[:, HT * h:HT * h + HT],
                             x[:, HT * h:HT * h + HT]).then_inc(stored, 16)
            sp.wait_ge(stored, 32)

        @block.tensor
        def _(pe):
            def chunked(dst, lhs, rhs, padded=True):
                k0, k1 = (P, P) if padded else (C + 1, C)
                pe.matmul(dst, lhs(0, k0), rhs(0, k0), start=True, stop=False)
                return pe.matmul(dst, lhs(1, k1), rhs(1, k1), start=False, stop=True)

            pe.wait_ge(ld_id, 32)
            pe.wait_ge(ld_p, 32)
            for kc in range(2):
                mm = pe.matmul(ps[0:R, 7, 0:R], Pm[:, kc, :], Pm[:, kc, :], start=kc == 0, stop=kc == 1)
            mm.then_inc(gram_ps, 1)

            def bcast_rows(src, k, stop):
                for i in range(2):
                    mm = pe.matmul(ps[0:R, 7, ROW2 * i:ROW2 * i + stop - k], ident[0:R, k + i:k + i + 1].to_broadcast([R, R]),
                                   src[:, k:stop], start=True, stop=True)
                mm.then_inc(bc_ps, 1)

            def chain_step(j):
                if j < PAIR_STEPS:
                    pe.wait_ge(w_ready, j + 1)
                    bcast_rows(W, 2 * j, R + 2 * j + 2)
                elif j == PAIR_STEPS:
                    pe.wait_ge(lit_in, 1)
                    pe.transpose(ps[0:R, 7, 0:R], W[:, R:2 * R], ident[0:R, 0:R]).then_inc(lit_ps, 1)
                elif j == PAIR_STEPS + 1:
                    pe.wait_ge(lit_sb, 1)
                    pe.matmul(ps[0:R, 7, 0:D], LiT[:, :], PT[:, :], start=True, stop=True).then_inc(ut_ps, 1)
                elif j < CHAIN - 1:
                    pe.wait_ge(m_ready, j - PAIR_STEPS - 1)
                    bcast_rows(M, 2 * (j - PAIR_STEPS - 2), R)
                else:
                    pe.wait_ge(ut_ready, 1)
                    for c in range(2):
                        mm = pe.transpose(ps[0:C, 7, c * R:(c + 1) * R], UT[:, c * C:(c + 1) * C], ident[0:R, 0:R])
                    mm.then_inc(u_ps, 1)

            chain_at = [0]

            def chain(steps):
                first, chain_at[0] = chain_at[0], min(chain_at[0] + steps, CHAIN)
                for j in range(first, chain_at[0]):
                    chain_step(j)

            def modulation(n):
                pe.wait_ge(ld_ada[n], 16)
                if n >= 1:
                    pe.wait_ge(ada_sb, n)
                w = adaw[:, n % 2]
                for i, kind in enumerate((0, 1, 3, 4)):
                    for c in range(2):
                        col = kind * D + c * C
                        mm = chunked(ps[0:C, 6, (2 * i + c) * SEQ:(2 * i + c + 1) * SEQ],
                                     lambda kc, k: w[0:k, kc, col:col + C], lambda kc, k: sT[0:k, kc, :],
                                     padded=False)
                mm.then_inc(ada_ps, 1)
                if n >= 1:
                    chain(1)

            def gates_by_sequence(n):
                if n >= 1:
                    pe.wait_ge(gseq_sb, n)
                w = adaw[:, n % 2]
                for i, kind in enumerate((2, 5)):
                    mm = chunked(ps[0:SEQ, 5, i * D:(i + 1) * D], lambda kc, k: sT[0:k, kc, :],
                                 lambda kc, k: w[0:k, kc, kind * D:(kind + 1) * D], padded=False)
                mm.then_inc(gseq_ps, 1)

            def spread_gates(i):
                pe.wait_ge(gseq_sb, i // T + 1)
                if i >= T + 2:
                    pe.wait_ge(gate_sb, i - 1)
                elif 3 <= i < T:
                    pe.wait_ge(gate_sb, i - 2)
                t = i % T
                pe.matmul(ps[:, SPREAD_BANK[i], 0:2 * D], spread_seq[:, t * P:(t + 1) * P],
                          gsb[:, i // T, :], start=True, stop=True).then_inc(gate_ps, 1)

            def rotation_generators():
                pe.wait_ge(ld_rot, 16)
                for r in range(2):
                    for kc in range(2):
                        k = C + 1 - kc
                        for q in range(B):
                            col = (r * B + q) * 512
                            mm = pe.matmul(ps[32 * q:32 * q + 32, r, :], sT[0:k, kc, :], rotw[0:k, kc, col:col + 512],
                                           start=kc == 0, stop=kc == 1)
                    mm.then_inc(v_ps, 1)
                    if r == 0:
                        chain(1)

            def pair_products(banks, lhs, rhs, steps):
                for first in range(2):
                    for i in range(8):
                        for p in range(2):
                            m = (first ^ p) * 8 + i
                            row = slice(R * p, R * p + R)
                            mm = pe.matmul(ps[row, banks[m // 8], (m % 8) * R:(m % 8 + 1) * R],
                                           lhs(row, m), rhs(row, m), start=True, stop=True)
                        if (first, i) != (1, 7):
                            chain(share(steps, first * 8 + i, 16))
                mm.then_inc(ex_ps, 1)
                chain(share(steps, 15, 16))

            def mat(buf):
                return lambda row, m: buf[row, m, :]

            def half_of(buf, i):
                return lambda row, m: buf[row, i, m, :]

            def expm(e, steps):
                if e == 0:
                    pe.wait_ge(gate_sb, T)
                    pe.wait_ge(gseq_sb, NB)
                    pe.wait_ge(ada_sb, NB)
                    pe.wait_ge(a_ready, 1)
                    pair_products(EX0, mat(A), mat(A), steps)
                elif e == 1:
                    pe.wait_ge(ex_act, 1)
                    pair_products(EX1, mat(A2), mat(A), steps)
                elif e == 2:
                    pe.wait_ge(ex_act, 2)
                    pe.wait_ge(ex_dve, 1)
                    pair_products(EX0, mat(A3), mat(pol), steps)
                elif e == 3:
                    pe.wait_ge(ex_dve, 2)
                    pair_products(EX1, mat(A3), mat(pol), steps)
                elif e == 4:
                    pe.wait_ge(ex_dve, 3)
                    pair_products(EX0, half_of(EF, 0), lambda row, m: ident[row, row], steps)
                else:
                    i = e - 5
                    src = EF if i % 2 == 0 else EG
                    pe.wait_ge(ex_act, 3 + i)
                    two = i < SQUARINGS - 1
                    pair_products(EX0, half_of(src, 1), half_of(src, 0), steps // 2 if two else steps)
                    if two:
                        pair_products(EX1, half_of(src, 0), half_of(src, 1), steps - steps // 2)

            def ln_transpose(i, h):
                pe.wait_ge(xn_ready, 2 * i + h + 1)
                if i >= 1:
                    pe.wait_ge(mod_done, 2 * i + h - 1)
                if i == 2:
                    pe.wait_ge(gate_sb, NB * T)
                if i == 1:
                    pe.wait_ge(ex_act, 2 + SQUARINGS + h)
                    pe.wait_ge(sub_done, T)
                for t in range(HT * h, HT * h + HT):
                    for c in range(2):
                        mm = pe.transpose(ps[0:C, 2 * h + c, (t % HT) * P:(t % HT + 1) * P],
                                          xn[:, t, c * C:(c + 1) * C], ident[:, :])
                mm.then_inc(xnT_ps, 1)

            def rotate():
                for h in range(2):
                    pe.wait_ge(x_end, T + HT * (h + 1))
                    for t in range(HT * h, HT * h + HT):
                        for c in range(2):
                            mm = pe.transpose(ps[0:C, 2 * h + c, (t % HT) * P:(t % HT + 1) * P], x[:, t, c * C:(c + 1) * C],
                                              ident[:, :])
                    mm.then_inc(xT_ps, 1)
                chain(CHAIN)
                pe.wait_ge(u_sb, 1)
                for h in range(2):
                    pe.wait_ge(xT_sb, h + 1)
                    for c in range(2):
                        mm = pe.matmul(ps[:, 4 + h, :], U[:, c].rearrange("p i r -> p (i r)"),
                                       xmT[0:C, c, HTOK * h:HTOK * (h + 1)], start=c == 0, stop=c == 1)
                    mm.then_inc(z_ps, 1)
                for h in range(2):
                    pe.wait_ge(z_sb, h + 1)
                    for i in range(HT * B // 2):
                        for p in range(2):
                            b = HT * B * h + 2 * i + p
                            row = slice(R * p, R * p + R)
                            mm = pe.matmul(ps[0:R, 2 * h + p, i * TOK:(i + 1) * TOK], A3[row, b // 2, :],
                                           z_rot[row, h, (b % (HT * B)) * TOK:(b % (HT * B) + 1) * TOK],
                                           start=True, stop=True)
                    mm.then_inc(y_ps, 1)
                for h in range(2):
                    pe.wait_ge(y_sb, h + 1)
                    for t in range(HT * h, HT * h + HT):
                        if t >= 2:
                            pe.wait_ge(x_rot, t - 1)
                        pe.matmul(ps[:, 6 + t % 2, 0:D], y_rot[0:R, h, (t % HT) * P:(t % HT + 1) * P], UT[:, :],
                                  start=True, stop=True).then_inc(d_ps, 1)

            for n in range(NB):
                s = n % 2
                if n == 0:
                    chain(CH_START)
                    pe.wait_ge(silu_done, 1)
                    modulation(0)
                if n == 2:
                    rotate()
                ln_transpose(2 * n, 0)
                pe.wait_ge(ld_wq[n], 16)

                def project_qkv(t):
                    pe.wait_ge(mod_done, 4 * n + t // HT + 1)
                    if t > QKV_FIRST[n]:
                        pe.wait_ge(qkv_sb, T * n + t)
                    elif 3 <= t < QKV_FIRST[n]:
                        pe.wait_ge(qkv_sb, T * n + t - 2)
                    elif n >= 1 and t < 3:
                        pe.wait_ge(gelu_done, 2 * MC * n)
                        pe.wait_ge(gated2, T * n)
                        if n == 2:
                            pe.wait_ge(x_rot, T)
                    chunked(ps[:, QKV_BANK[n][t], 0:QKV], lambda kc, k: xmT[0:k, kc, t * P:(t + 1) * P],
                            lambda kc, k: wq[0:k, s, kc, :]).then_inc(qkv_ps, 1)

                for t in range(QKV_FIRST[n]):
                    if t == (1 if n == 1 else 0):
                        ln_transpose(2 * n, 1)
                    project_qkv(t)
                    if n == 0 and t >= HT:
                        chain(CH_QKV)
                if n == 0:
                    pe.wait_ge(ld_const, 16 * 4)
                    pe.wait_ge(qkv_sb, T)
                    gates_by_sequence(0)
                    modulation(1)
                    gates_by_sequence(1)
                    rotation_generators()
                    modulation(2)
                    gates_by_sequence(2)

                na = n - 1

                def sum_products(t):
                    pe.wait_ge(qk_prod, t + 1)
                    if t < 2:
                        pe.wait_ge(v_sb, 2)
                    else:
                        pe.wait_ge(sub_done, t - 1)
                    for d in range(DH):
                        mm = pe.matmul(ps[:, t % 2, 0:HEADS * HEADS], ident[:, :],
                                       prod_slot[t % 2][:, d * HEADS * HEADS:(d + 1) * HEADS * HEADS],
                                       start=d == 0, stop=d == DH - 1)
                        chain(share(CH_SUM, d, DH))
                    mm.then_inc(s_ps, 1)

                def qk_transpose(p):
                    pe.wait_ge(qkv_sb, T * n + (QKV_FIRST[n] if p == 0 else 2 * p + 2))
                    if n == 1:
                        pe.wait_ge(qk_norm, p // 2 + 1)
                    if p >= 1:
                        pe.wait_ge(k_sb, 4 * na + p)
                    for i in range(2):
                        for c in range(2):
                            for j in range(2):
                                mm = pe.transpose(ps[0:C, 4 + i, (2 * c + j) * P:(2 * c + j + 1) * P],
                                                  qkv[:, 2 * p + j, i * D + c * C:i * D + (c + 1) * C], ident[:, :])
                    mm.then_inc(qkT_ps, 1)

                def scores(t):
                    p = t // 2
                    pe.wait_ge(q_sb, 4 * na + p + 1)
                    pe.wait_ge(k_act, 4 * na + p + 1)
                    pe.wait_ge(k_dve, 4 * na + p + 1)
                    if t >= 2:
                        pe.wait_ge(sub_done, T * n + t - 1)
                    for c in range(2):
                        for b in range(B):
                            mm = pe.matmul(ps[TOK * b:TOK * b + TOK, t % 2, c * 256:(c + 1) * 256],
                                           qT[:, c, t * P + b * TOK:t * P + (b + 1) * TOK],
                                           kexp[0:C, p % 2, c, (t % 2) * B + b, :, :],
                                           start=True, stop=True)
                    mm.then_inc(s_ps, 1)

                def probs_transpose(t):
                    pe.wait_ge(exp_done, T * n + t + 1)
                    if na or t:
                        pe.wait_ge(pT_sb, T * na + t)
                    for g in range(4):
                        mm = pe.transpose(ps[:, 2, g * P:(g + 1) * P], probs[:, t % 2, g * P:(g + 1) * P], ident[:, :])
                    mm.then_inc(pT_ps, 1)

                def values(t):
                    pe.wait_ge(pT_sb, T * na + t + 1)
                    pe.wait_ge(v_spread, 2 * na + t // HT + 1)
                    if na or t:
                        pe.wait_ge(o_sb, T * na + t)
                    if t == 0:
                        pe.wait_ge(qkv_sb, T * n + QKV_FIRST[n])
                    for g in range(4):
                        for b in range(B):
                            mm = pe.matmul(ps[TOK * b:TOK * b + TOK, 6, g * G4 * VW:(g + 1) * G4 * VW],
                                           probsT[:, t % 2, g * P + TOK * b:g * P + TOK * b + TOK],
                                           vexp[:, B * t + b, g, :], start=True, stop=True)
                    mm.then_inc(o_ps, 1)

                def o_transpose(t):
                    if n == 0:
                        pe.wait_ge(o_back[t % 2], 16 * (t // 2 + 1))
                    else:
                        pe.wait_ge(o_sb, T * na + t + 1)
                    if n or t:
                        pe.wait_ge(gated1, T * n + t)
                    for c in range(2):
                        mm = pe.transpose(ps[0:C, O_BANK[n], c * P:(c + 1) * P], o[:, t % 2, c * C:(c + 1) * C], ident[:, :])
                    mm.then_inc(oT_ps, 1)

                def project(t):
                    pe.wait_ge(oT_sb, T * n + t + 1)
                    if t == 0:
                        pe.wait_ge(ld_w[n], 16 * 3)
                    chunked(ps[:, O_BANK[n], 0:D], lambda kc, k: oT[0:k, t % 2, kc, :],
                            lambda kc, k: wp[0:k, s, kc, :]).then_inc(pr_ps, 1)

                for st in range(0 if n else ATT0):
                    if 0 <= st - 3 < T:
                        o_transpose(st - 3)
                    if st < T:
                        sum_products(st)
                    if 0 <= st - 3 < T:
                        project(st - 3)
                    if st == 0:
                        for i in range(T):
                            spread_gates(i)
                            chain(share(CH_GATES, i, T))
                    elif st < EXPM:
                        for i, e in enumerate(EXPM_AT[st]):
                            expm(e, share(CH_EXPM, i, len(EXPM_AT[st])))
                    else:
                        chain(CH_TAIL)
                    if st == ATT0 - 2:
                        ln_transpose(2 * n + 1, 0)
                if n:
                    qk_transpose(0)
                for st in range(ATT if n else 0):
                    if st < T and st % 2 == 0 and st // 2 + 1 < T // 2:
                        qk_transpose(st // 2 + 1)
                    if st < T:
                        scores(st)
                    if QKV_FIRST[n] + st < T:
                        project_qkv(QKV_FIRST[n] + st)
                    if 0 <= st - 4 < T:
                        project(st - 4)
                    chain(CH_L1 // 2)
                    if 0 <= st - 1 < T:
                        probs_transpose(st - 1)
                    if 0 <= st - 2 < T:
                        values(st - 2)
                    if 0 <= st - 3 < T:
                        o_transpose(st - 3)
                    chain((CH_L1 + 1) // 2)
                    if st == ATT - 2:
                        ln_transpose(2 * n + 1, 0)

                def fc1(h):
                    pe.wait_ge(mod_done, 4 * n + 2 + h + 1)
                    for m in range(MC):
                        i = MC * h + m
                        if i == 3:
                            ln_transpose(2 * n + 1, 1)
                        if i >= 2:
                            pe.wait_ge(gelu_done, 2 * MC * n + i - 1)
                        rows = min(P, MLP - P * m)
                        chunked(ps[0:rows, 4 + i % 2, :], lambda kc, k: w1[0:k, s, kc, m * P:m * P + rows],
                                lambda kc, k: xmT[0:k, kc, HTOK * h:HTOK * (h + 1)]).then_inc(h_ps, 1)
                        if i < 2 or i >= MC:
                            chain(1)
                        if n == 0:
                            for j in range(2 * T * i // (2 * MC), 2 * T * (i + 1) // (2 * MC)):
                                spread_gates(T + j)

                def fc2(t):
                    pe.wait_ge(gelu_done, 2 * MC * n + MC * (t // HT + 1))
                    if t >= 2:
                        pe.wait_ge(gated2, T * n + t - 1)
                    else:
                        pe.wait_ge(gated1, T * (n + 1))
                    for m in range(MC):
                        rows = P if m < MC - 1 else R + 1
                        mm = pe.matmul(ps[:, FC2_BANK[t % 2], 0:D], hT[0:rows, m, t * P:(t + 1) * P], w2[0:rows, s, m, :],
                                       start=m == 0, stop=m == MC - 1)
                    mm.then_inc(m_ps, 1)
                    chain(1)

                fc1(0)
                fc1(1)
                for t in range(T):
                    fc2(t)

        @block.vector
        def _(v):
            own = [0]

            def link(ins):
                own[0] += 1
                ins.then_inc(dve, 1)
                v.wait_ge(dve, own[0])

            link(v.memset(sT[64:P, :, :], 1.0))
            v.memset(xmT[64:P, :, :], 1.0)
            v.memset(oT[64:P, :, :, :], 1.0)
            v.memset(qk_eps[:], QK_EPS)
            v.memset(half_neg[:], -0.5).then_inc(ones_set, 1)

            def modulation(n):
                v.wait_ge(ada_ps, n + 1)
                src = ps[0:C, 6, 0:8 * SEQ].rearrange("p (k m) -> p k m", k=4)
                dst = mod[:, n].rearrange("p k c b -> p k (c b)")
                v.tensor_copy(dst[:, 0:4:2], src[:, 0:4:2])
                v.tensor_scalar(dst[:, 1:4:2], src[:, 1:4:2], 1.0, None, ALU.add).then_inc(ada_sb, 1)

            def mark(ins):
                own[0] += 1
                ins.then_inc(dve, 1)
                return own[0]

            def two_rows(step, X, k, n1, n2, invert):
                r1, r2 = ps[0:R, 7, 0:n1], ps[0:R, 7, ROW2:ROW2 + n1]
                v.wait_ge(bc_ps, step + 1)
                invert(r1[:, 0:1], k, lambda: mark(v.tensor_copy(row2[:, 0:n1], r2)))
                last = k + 2 == R
                u = mark(v.tensor_scalar(piv[:, 1:2], r2[:, 0:1], RD[:, k:k + 1], -1.0, ALU.mult, ALU.mult))
                f = mark(v.scalar_tensor_tensor(out=fcol[:, k:k + 1], in0=X[:, k:k + 1], scalar=RD[:, k:k + 1],
                                                in1=neg_below[:, k:k + 1], op0=ALU.mult, op1=ALU.mult))
                v.wait_ge(dve, u)
                row = mark(v.scalar_tensor_tensor(out=row2[:, 1:n1], in0=r1[:, 1:n1], scalar=piv[:, 1:2],
                                                  in1=row2[:, 1:n1], op0=ALU.mult, op1=ALU.add))
                v.wait_ge(dve, f)
                live = X[:, k + 1:k + n1]
                v.scalar_tensor_tensor(out=live, in0=r1[:, 1:n1], scalar=fcol[:, k:k + 1], in1=live,
                                       op0=ALU.mult, op1=ALU.add).then_inc(dve, 1)
                own[0] += 1
                v.wait_ge(dve, row)
                invert(row2[:, 1:2], k + 1)
                if last:
                    v.wait_ge(dve, own[0])
                    return None
                link(v.scalar_tensor_tensor(out=fcol[:, k + 1:k + 2], in0=X[:, k + 1:k + 2], scalar=RD[:, k + 1:k + 2],
                                            in1=neg_below[:, k + 1:k + 2], op0=ALU.mult, op1=ALU.mult))
                live = X[:, k + 2:k + 2 + n2]
                return v.scalar_tensor_tensor(out=live, in0=row2[:, 2:2 + n2], scalar=fcol[:, k + 1:k + 2], in1=live,
                                              op0=ALU.mult, op1=ALU.add)

            def inverse(pivot, k, meanwhile=lambda: None):
                at = mark(v.reciprocal(RD[:, k:k + 1], pivot))
                meanwhile()
                v.wait_ge(dve, at)

            def signed_inverse(alpha, k, meanwhile=lambda: None):
                at = mark(v.tensor_scalar(SG[:, k:k + 1], alpha, 0.0, 2.0, ALU.is_ge, ALU.mult))
                meanwhile()
                v.wait_ge(dve, at)
                link(v.scalar_tensor_tensor(out=piv[:, 0:1], in0=SG[:, k:k + 1], scalar=-1.0, in1=alpha,
                                            op0=ALU.add, op1=ALU.add))
                link(v.reciprocal(RD[:, k:k + 1], piv[:, 0:1]))

            def chain_step(j):
                if j < PAIR_STEPS:
                    ins = two_rows(j, W, 2 * j, R + 2, R, inverse)
                    if ins is not None:
                        ins.then_inc(w_ready, 1)
                        v.wait_ge(w_ready, j + 2)
                    else:
                        v.tensor_tensor(SG[:], RD[:], ident[0:R, 0:R], ALU.mult).then_inc(lit_in, 1)
                        v.wait_ge(lit_in, 1)
                        v.tensor_reduce(dg[:, 0:1], SG[:], AX.X, ALU.add).then_inc(diag_ready, 1)
                elif j == PAIR_STEPS:
                    v.wait_ge(lit_ps, 1)
                    v.tensor_copy(LiT[:], ps[0:R, 7, 0:R]).then_inc(lit_sb, 1)
                elif j == PAIR_STEPS + 1:
                    v.wait_ge(ut_ps, 1)
                    v.wait_ge(isd_ready, 1)
                    link(v.tensor_scalar(UT[:], ps[0:R, 7, 0:D], dg[:, 1:2], None, ALU.mult))
                    v.tensor_copy(M[:], UT[:, 0:R]).then_inc(m_ready, 1)
                elif j < CHAIN - 1:
                    k = 2 * (j - PAIR_STEPS - 2)
                    ins = two_rows(j - 2, M, k, R - k, R - k - 2, signed_inverse)
                    if ins is not None:
                        ins.then_inc(m_ready, 1)
                        v.wait_ge(m_ready, k // 2 + 2)
                    else:
                        link(v.tensor_tensor(RD[:], SG[:], ident[0:R, 0:R], ALU.mult))
                        link(v.tensor_reduce(dg[:, 2:3], RD[:], AX.X, ALU.add))
                        link(v.tensor_scalar(dg[:, 3:4], dg[:, 2:3], -1.0, 1.0, ALU.mult, ALU.add))
                        v.tensor_scalar(UT[:], UT[:], dg[:, 3:4], None, ALU.mult).then_inc(ut_ready, 1)
                else:
                    v.wait_ge(u_ps, 1)
                    for i in range(2):
                        ins = v.tensor_copy(U[:, :, i, :], ps[0:C, 7, 0:2 * R].rearrange("p (c r) -> p c r", c=2))
                    ins.then_inc(u_sb, 1)

            chain_at = [0]

            def chain(steps):
                first, chain_at[0] = chain_at[0], min(chain_at[0] + steps, CHAIN)
                for j in range(first, chain_at[0]):
                    chain_step(j)

            def pair_banks(banks):
                return ps[:, banks[0]:banks[1] + 1, :].rearrange("p a (m r) -> p a m r", r=R)

            def halves(buf):
                return buf.rearrange("p (a m) r -> p a m r", a=2)

            def add_eye(buf, c):
                return v.scalar_tensor_tensor(out=buf, in0=eye_pair[:].unsqueeze(1).to_broadcast([P, PAIRS, R]), scalar=c,
                                              in1=buf, op0=ALU.mult, op1=ALU.add)

            def expm(e):
                if e == 1:
                    v.wait_ge(ex_pol, 1)
                    link(v.scalar_tensor_tensor(out=pol, in0=A, scalar=cf[7], in1=pol, op0=ALU.mult, op1=ALU.add))
                    add_eye(pol, cf[6]).then_inc(ex_dve, 1)
                elif e == 2:
                    v.wait_ge(ex_pol, 2)
                    link(v.scalar_tensor_tensor(out=EF[:, 0], in0=A, scalar=cf[4], in1=EF[:, 0], op0=ALU.mult, op1=ALU.add))
                    link(add_eye(EF[:, 0], cf[3]))
                    v.wait_ge(ex_ps, 3)
                    v.scalar_tensor_tensor(out=halves(pol), in0=pair_banks(EX0), scalar=-1.0, in1=halves(EF[:, 0]),
                                           op0=ALU.mult, op1=ALU.add).then_inc(ex_dve, 1)
                elif e == 3:
                    v.wait_ge(ex_dve, 2)
                    link(v.scalar_tensor_tensor(out=EF[:, 0], in0=A2, scalar=cf[2], in1=A, op0=ALU.mult, op1=ALU.add))
                    link(add_eye(EF[:, 0], 1.0))
                    v.wait_ge(ex_ps, 4)
                    v.scalar_tensor_tensor(out=halves(EF[:, 0]), in0=pair_banks(EX1), scalar=-1.0, in1=halves(EF[:, 0]),
                                           op0=ALU.mult, op1=ALU.add).then_inc(ex_dve, 1)
                elif e == EXPM - 1:
                    v.wait_ge(ex_act, 3 + SQUARINGS)
                    add_eye(A3[:], -1.0).then_inc(ex_dve, 1)

            def ln_stats(i, h):
                if i == 0:
                    v.wait_ge(ld_x, 16)
                elif i == 4:
                    v.wait_ge(x_rot, HT * (h + 1))
                elif i % 2 == 0:
                    v.wait_ge(x_end, x_updates(i // 2) - HT * (1 - h))
                else:
                    v.wait_ge(x_mid, T * (i // 2) + HT * (h + 1))
                for t in range(HT * h, HT * h + HT):
                    ins = v.bn_stats(bn[:, t, :], x[:, t, :])
                link(ins)
                for t in range(HT * h, HT * h + HT):
                    ins = v.bn_aggr(mv[:, t, :], bn[:, t, :])
                ins.then_inc(stats_ready, 1)

            def ln_apply(i, h):
                v.wait_ge(rstd_ready, 2 * i + h + 1)
                if i >= 1:
                    v.wait_ge(xnT_ps, 2 * i + h - 1)
                for t in range(HT * h, HT * h + HT):
                    ins = v.tensor_scalar(xn[:, t, :], x[:, t, :], mv[:, t, 0:1], rstd[:, t:t + 1],
                                          ALU.subtract, ALU.mult)
                ins.then_inc(xn_ready, 1)

            def modulate(i, h):
                n, k = i // 2, 2 * (i % 2)
                if i == 0:
                    v.wait_ge(ada_sb, 1)
                v.wait_ge(xnT_ps, 2 * i + h + 1)
                b0 = HT * B * h
                dst = xmT[0:C, :, HTOK * h:HTOK * (h + 1)].rearrange("p c (b t) -> p c b t", t=TOK)
                scale = mod[:, n, k + 1, :, b0:b0 + HT * B].unsqueeze(3).to_broadcast([C, 2, HT * B, TOK])
                shift = mod[:, n, k, :, b0:b0 + HT * B].unsqueeze(3).to_broadcast([C, 2, HT * B, TOK])
                link(v.tensor_tensor(dst, ps[0:C, 2 * h:2 * h + 2, :].rearrange("p c (b t) -> p c b t", t=TOK),
                                     scale, ALU.mult))
                v.tensor_tensor(dst, dst, shift, ALU.add).then_inc(mod_done, 1)

            for n in range(NB):
                if n == 0:
                    v.wait_ge(ld_id, 32)
                    v.tensor_copy(W[:, R:2 * R], ident[0:R, 0:R])
                    v.wait_ge(gram_ps, 1)
                    v.tensor_copy(W[:, 0:R], ps[0:R, 7, 0:R]).then_inc(w_ready, 1)
                    v.wait_ge(w_ready, 1)
                    chain(CH_START)
                if n == 2:
                    chain(CHAIN)
                    for t in range(T):
                        v.wait_ge(d_ps, t + 1)
                        v.tensor_tensor(x[:, t, :], x[:, t, :], ps[:, 6 + t % 2, 0:D], ALU.add).then_inc(x_rot, 1)
                if n != 1:
                    ln_stats(2 * n, 0)
                    ln_stats(2 * n, 1)
                    ln_apply(2 * n, 0)
                    if n == 0:
                        modulation(0)
                    modulate(2 * n, 0)
                else:
                    ln_stats(2 * n, 1)
                ln_apply(2 * n, 1)
                modulate(2 * n, 1)

                if n == 0:
                    chain(CH_QKV * HT)
                    v.wait_ge(ld_const, 16 * 4)
                    v.tensor_scalar(kscale[:], kmask[:], gb[:, 2:3], None, ALU.mult)
                    v.tensor_scalar(kbias[:], kmask[:], gb[:, 3:4], None, ALU.mult)
                    modulation(1)
                    chain(CH_MOD - 1)
                    modulation(2)
                    chain(1)

                na = n - 1

                def spread_keys(p):
                    v.wait_ge(k_sb, 4 * na + p + 1)
                    if na or p >= 2:
                        v.wait_ge(s_ps, T * n + 2 * p - 2)
                    for j in range(K_ACT, HC):
                        dst = kexp[0:C, p % 2, :, :, j, :]
                        src = kT[:].rearrange("p (c b t) -> p c b t", c=2, t=TOK)
                        if n == 1:
                            ins = v.tensor_scalar(dst, src, kscale[:, j:j + 1], kbias[:, j:j + 1], ALU.mult, ALU.add)
                        else:
                            ins = v.tensor_scalar(dst, src, kmask[:, j:j + 1], None, ALU.mult)
                    ins.then_inc(k_dve, 1)

                def by_qk_head(stat):
                    return stat[:].rearrange("p (t g) -> p t g", t=HT)

                def over_head(stat):
                    return by_qk_head(stat).unsqueeze(3).to_broadcast([P, HT, 2 * HEADS, DH])

                def qk_of(h):
                    return qkv[:, HT * h:HT * h + HT, 0:2 * D].rearrange("p t (g d) -> p t g d", d=DH)

                def qk_centre(h):
                    v.wait_ge(qkv_sb, T * n + HT * (h + 1))
                    link(v.tensor_reduce(by_qk_head(qk_sum), qk_of(h), AX.X, ALU.add))
                    link(v.tensor_scalar(qk_mean[:], qk_sum[:], 1.0 / DH, None, ALU.mult))
                    v.tensor_tensor(qk_of(h), qk_of(h), over_head(qk_mean), ALU.subtract).then_inc(qk_xc, 1)

                def qk_scale(h):
                    v.wait_ge(qk_sq, h + 1)
                    v.tensor_reduce(by_qk_head(qk_sum), xn[:].rearrange("p a (g d) -> p (a g) d", d=DH).rearrange(
                        "p (t g) d -> p t g d", t=HT), AX.X, ALU.add).then_inc(qk_ss, 1)
                    v.wait_ge(qk_rstd, h + 1)
                    link(v.reciprocal(qk_rs[:], qk_mean[:]))
                    v.tensor_tensor(qk_of(h), qk_of(h), over_head(qk_rs), ALU.mult).then_inc(qk_norm, 1)

                keys = TOK if n else HEADS

                def by_head(buf):
                    return buf[:, 0:HEADS * keys].rearrange("p (h k) -> p h k", h=HEADS)

                def shift_scores(t):
                    v.wait_ge(s_ps, T * n + t + 1)
                    s = by_head(ps[:, t % 2, :])
                    v.tensor_reduce(rowmax[:, t % 2, :], s, AX.X, ALU.max).then_inc(max_done, 1)
                    v.wait_ge(max_done, T * n + t + 1)
                    if na >= 0 and (na or t >= 2):
                        v.wait_ge(pT_ps, T * na + t - 1)
                    v.tensor_tensor(by_head(probs[:, t % 2, :]), s,
                                    rowmax[:, t % 2, :].unsqueeze(2).to_broadcast([P, HEADS, keys]),
                                    ALU.subtract).then_inc(sub_done, 1)

                def normalise(t):
                    v.wait_ge(o_ps, T * na + t + 1)
                    acc = ps[:, 6, 0:HEADS * VW].rearrange("p (h d) -> p h d", h=HEADS)
                    link(v.reciprocal(rinv[:, t % 2, :], acc[:, :, DH]))
                    if n or t >= 2:
                        v.wait_ge(oT_ps, T * n + t - 1)
                    v.tensor_tensor(o[:, t % 2, :].rearrange("p (h d) -> p h d", h=HEADS), acc[:, :, 0:DH],
                                    rinv[:, t % 2, :].unsqueeze(2).to_broadcast([P, HEADS, DH]),
                                    ALU.mult).then_inc(o_sb, 1)

                def sum_probs(t):
                    v.wait_ge(exp_done, t + 1)
                    link(v.tensor_reduce(rowmax[:, t % 2, :], by_head(probs[:, t % 2, :]), AX.X, ALU.add))
                    link(v.reciprocal(rinv[:, t % 2, :], rowmax[:, t % 2, :]))

                def weigh_heads(t):
                    prod = prod_pv[t % 2].rearrange("p (h d k) -> p h d k", h=HEADS, d=DH)
                    if t >= 2:
                        v.wait_ge(o_stored, 16 * B * (t - 1))
                    v.wait_ge(pv_prod, t + 1)
                    dst = o_heads[:, t % 2].rearrange("p (h d) -> p h d", h=HEADS)
                    for i in range(2):
                        hs = slice(HC * i, HC * i + HC)
                        link(v.tensor_reduce(dst[:, hs], prod[:, hs], AX.X, ALU.add))
                        chain(share(CH_EXPM, i, 2))
                    v.tensor_tensor(dst, dst, rinv[:, t % 2, :].unsqueeze(2).to_broadcast([P, HEADS, DH]),
                                    ALU.mult).then_inc(heads_out, 1)

                def gate1(t):
                    v.wait_ge(pr_ps, T * n + t + 1)
                    if n == 0 and t == 0:
                        v.wait_ge(gate_sb, T)
                    if t >= 4:
                        v.wait_ge(x_mid, T * n + t - 3)
                    elif n:
                        v.wait_ge(x_end, T * n)
                    if n == 1 and t == 0:
                        v.wait_ge(gate_sb, T * NB)
                    v.tensor_tensor(delta[:, t % 4, :], ps[:, O_BANK[n], 0:D], gates[:, n, t, 0, :],
                                    ALU.mult).then_inc(gated1, 1)

                def gate2(t):
                    v.wait_ge(m_ps, T * n + t + 1)
                    if t >= 4:
                        v.wait_ge(x_end, T * n + t - 3)
                    else:
                        v.wait_ge(x_mid, T * (n + 1))
                    v.tensor_tensor(delta[:, t % 4, :], ps[:, FC2_BANK[t % 2], 0:D], gates[:, n, t, 1, :],
                                    ALU.mult).then_inc(gated2, 1)

                def mlp_norm(st):
                    if st == T:
                        ln_stats(2 * n + 1, 0)
                    if st == T + 1:
                        ln_apply(2 * n + 1, 0)
                    if st == (ATT if n else ATT0) - 1:
                        modulate(2 * n + 1, 0)

                for st in range(0 if n else ATT0):
                    if 1 <= st <= T:
                        sum_probs(st - 1)
                    if st < T:
                        chain(CH_SUM)
                        shift_scores(st)
                    if 0 <= st - 3 < T:
                        gate1(st - 3)
                    if 1 <= st <= T:
                        weigh_heads(st - 1)
                    elif st == 0:
                        chain(CH_GATES)
                    elif st < EXPM:
                        chain(CH_EXPM)
                    else:
                        chain(CH_TAIL)
                    if st == 0:
                        v.wait_ge(ld_v, 32)
                        v.tensor_tensor(A, A2, sgn[:].unsqueeze(1).to_broadcast([P, PAIRS, R]), ALU.mult).then_inc(a_ready, 1)
                        v.wait_ge(a_ready, 1)
                        for p in range(2):
                            ins = v.tensor_copy(eye_pair[R * p:R * p + R, :], ident[R * p:R * p + R, R * p:R * p + R])
                        link(ins)
                    elif st < EXPM:
                        for e in EXPM_AT[st]:
                            expm(e)
                    mlp_norm(st)
                if n == 1:
                    qk_centre(0)
                    qk_scale(0)
                if n:
                    if n == 1:
                        qk_centre(1)
                    spread_keys(0)
                    if n == 1:
                        qk_scale(1)
                for st in range(ATT if n else 0):
                    if st < T:
                        shift_scores(st)
                    if 0 <= st - 4 < T:
                        gate1(st - 4)
                    chain(CH_L1 // 2)
                    if st < T and st % 2 == 0 and st // 2 + 1 < T // 2:
                        spread_keys(st // 2 + 1)
                    if 0 <= st - 2 < T:
                        normalise(st - 2)
                    chain((CH_L1 + 1) // 2)
                    mlp_norm(st)
                ln_stats(2 * n + 1, 1)
                chain(2)
                ln_apply(2 * n + 1, 1)
                modulate(2 * n + 1, 1)
                chain(MC)
                for t in range(T):
                    gate2(t)
                    chain(1)
                    if n == 0 and t == HT:
                        ln_stats(2, 0)
                    if n == 0 and t == HT + 2:
                        ln_apply(2, 0)
                if n == 0:
                    modulate(2, 0)

        @block.scalar
        def _(a):
            a.dma_start(Pm[:], p_in).then_inc(ld_p, 16)
            a.dma_start(PT[:], pt_in).then_inc(ld_p, 16)
            a.wait_ge(ld_cond, 16)
            a.wait_ge(dve, 1)
            a.activation(sT[0:C], cT[:], ACT.Silu).then_inc(silu_done, 1)
            a.wait_ge(pads_set, 1)
            a.dma_start(wq[0:C + 1, 0], qkv_w[0]).then_inc(ld_wq[0], 16)
            for w, src in ((wp[0:C + 1], proj_w), (w1[0:C + 1], fc1_w), (w2, fc2_w)):
                a.dma_start(w[:, 0], src[0]).then_inc(ld_w[0], 16)
            a.dma_start(wq[0:C + 1, 1], qkv_w[1]).then_inc(ld_wq[1], 16)
            for w, src in ((wp[0:C + 1], proj_w), (w1[0:C + 1], fc1_w), (w2, fc2_w)):
                a.dma_start(w[:, 1], src[1]).then_inc(ld_w[1], 16)

            def gates_by_sequence(n):
                a.wait_ge(gseq_ps, n + 1)
                a.copy(gsb[:, n, :], ps[0:SEQ, 5, 0:2 * D]).then_inc(gseq_sb, 1)

            def pair_banks(banks):
                return ps[:, banks[0]:banks[1] + 1, :].rearrange("p a (m r) -> p a m r", r=R)

            def halves(buf):
                return buf.rearrange("p (a m) r -> p a m r", a=2)

            def expm(e):
                if e == 0:
                    a.wait_ge(ex_ps, 1)
                    a.mul(halves(A2), pair_banks(EX0), -1.0).then_inc(ex_act, 1)
                    a.mul(halves(pol), pair_banks(EX0), -cf[8]).then_inc(ex_pol, 1)
                    a.mul(halves(EF[:, 0]), pair_banks(EX0), -cf[5]).then_inc(ex_pol, 1)
                elif e == 1:
                    a.wait_ge(ex_ps, 2)
                    a.copy(halves(A3[:]), pair_banks(EX1)).then_inc(ex_act, 1)
                elif e == 4:
                    a.wait_ge(ex_ps, 5)
                    a.copy(halves(EF[:, 1]), pair_banks(EX0)).then_inc(ex_act, 1)
                elif 5 <= e < EXPM - 1:
                    i = e - 5
                    dst = EG if i % 2 == 0 else EF
                    a.wait_ge(ex_ps, 5 + 2 * i + 1)
                    a.copy(halves(dst[:, 0]), pair_banks(EX0))
                    a.wait_ge(ex_ps, 5 + 2 * i + 2)
                    a.copy(halves(dst[:, 1]), pair_banks(EX1)).then_inc(ex_act, 1)
                elif e == EXPM - 1:
                    a.wait_ge(ex_ps, 5 + 2 * SQUARINGS - 1)
                    a.copy(halves(A3[:]), pair_banks(EX0)).then_inc(ex_act, 1)

            for n in range(NB):
                if n == 2:
                    for h in range(2):
                        a.wait_ge(xT_ps, h + 1)
                        a.copy(xmT[0:C, :, HTOK * h:HTOK * (h + 1)], ps[0:C, 2 * h:2 * h + 2, :]).then_inc(xT_sb, 1)
                    for h in range(2):
                        a.wait_ge(z_ps, h + 1)
                        a.copy(z_rot[:, h, :], ps[:, 4 + h, :]).then_inc(z_sb, 1)
                    for h in range(2):
                        a.wait_ge(y_ps, h + 1)
                        ydst = y_rot[0:R, h, :].rearrange("p (i q t) -> p i q t", q=2, t=TOK)
                        for p in range(2):
                            ins = a.copy(ydst[:, :, p, :], ps[0:R, 2 * h + p, 0:HTOK // 2].rearrange("p (i t) -> p i t", t=TOK))
                        ins.then_inc(y_sb, 1)

                def squares(h):
                    a.wait_ge(qk_xc, h + 1)
                    a.wait_ge(xnT_ps, 4 * n + 2)
                    a.activation(xn[:].rearrange("p a b -> p (a b)").rearrange("p (t g) -> p t g", t=HT),
                                 qkv[:, HT * h:HT * h + HT, 0:2 * D], ACT.Square).then_inc(qk_sq, 1)

                def deviation(h):
                    a.wait_ge(qk_ss, h + 1)
                    a.activation(qk_mean[:], qk_sum[:], ACT.Sqrt, bias=qk_eps[:, 0:1], scale=1.0 / DH).then_inc(qk_rstd, 1)

                def qkv_out(t):
                    a.wait_ge(qkv_ps, T * n + t + 1)
                    if n == 2:
                        a.wait_ge(v_spread, 2)
                    a.copy(qkv[:, t, :], ps[:, QKV_BANK[n][t], 0:QKV]).then_inc(qkv_sb, 1)

                for t in range(QKV_FIRST[n]):
                    qkv_out(t)
                    if n == 1 and t == HT - 1:
                        squares(0)
                    if n == 1 and t == HT + 1:
                        deviation(0)
                if n == 0:
                    gates_by_sequence(0)
                    gates_by_sequence(1)
                    for r in range(2):
                        a.wait_ge(v_ps, r + 1)
                        a.copy(vsb[:, r, :], ps[:, r, :]).then_inc(v_sb, 1)
                    gates_by_sequence(2)

                na = n - 1

                def spread(p, part):
                    if part == 0:
                        a.wait_ge(qkT_ps, 4 * na + p + 1)
                        dst = qT[:, :, 2 * p * P:2 * (p + 1) * P]
                        src = ps[0:C, 4, :].rearrange("p (c t) -> p c t", c=2)
                        if n == 1:
                            a.activation(dst, src, ACT.Identity, bias=gb[:, 1:2], scale=gb[:, 0:1]).then_inc(q_sb, 1)
                        else:
                            a.copy(dst, src).then_inc(q_sb, 1)
                        if na or p:
                            a.wait_ge(k_dve, 4 * na + p)
                            a.wait_ge(k_act, 4 * na + p)
                        a.copy(kT[:], ps[0:C, 5, :]).then_inc(k_sb, 1)
                        a.wait_ge(k_sb, 4 * na + p + 1)
                        if na or p >= 2:
                            a.wait_ge(s_ps, T * n + 2 * p - 2)
                    for j in (range(0, 1) if part == 0 else range(1, K_ACT)):
                        dst = kexp[0:C, p % 2, :, :, j, :]
                        src = kT[:].rearrange("p (c b t) -> p c b t", c=2, t=TOK)
                        if n == 1:
                            ins = a.activation(dst, src, ACT.Identity, bias=kbias[:, j:j + 1], scale=kscale[:, j:j + 1])
                        else:
                            ins = a.activation(dst, src, ACT.Copy, scale=kmask[:, j:j + 1])
                    if part == 1:
                        ins.then_inc(k_act, 1)

                def exponential(t):
                    a.wait_ge(sub_done, T * n + t + 1)
                    p = probs[:, t % 2, 0:HEADS * (TOK if n else HEADS)]
                    a.activation(p, p, ACT.Exp, scale=DH ** -0.5).then_inc(exp_done, 1)

                def probs_out(t):
                    a.wait_ge(pT_ps, T * na + t + 1)
                    if na or t >= 2:
                        a.wait_ge(o_ps, T * na + t - 1)
                    a.copy(probsT[:, t % 2, :], ps[:, 2, :]).then_inc(pT_sb, 1)

                def o_out(t):
                    a.wait_ge(oT_ps, T * n + t + 1)
                    if n or t >= 2:
                        a.wait_ge(pr_ps, T * n + t - 1)
                    a.copy(oT[0:C, t % 2], ps[0:C, O_BANK[n], 0:2 * P].rearrange("p (c t) -> p c t", c=2)).then_inc(oT_sb, 1)

                if n:
                    spread(0, 0)
                    spread(0, 1)
                    if n == 1:
                        squares(1)
                        deviation(1)

                def gates_by_token(i):
                    a.wait_ge(gate_ps, i + 1)
                    a.copy(gates[:, i // T, i % T].rearrange("p g f -> p (g f)"),
                           ps[:, SPREAD_BANK[i], 0:2 * D]).then_inc(gate_sb, 1)

                for st in range(0 if n else ATT0):
                    if 0 <= st - 3 < T:
                        o_out(st - 3)
                    if st < T:
                        exponential(st)
                    if st == 0:
                        for i in range(T):
                            gates_by_token(i)
                    elif st < EXPM:
                        for e in EXPM_AT[st]:
                            expm(e)
                for st in range(ATT if n else 0):
                    if st // 2 + 1 < T // 2:
                        spread(st // 2 + 1, st % 2)
                    if 0 <= st - 1 < T:
                        probs_out(st - 1)
                    if QKV_FIRST[n] + st < T:
                        qkv_out(QKV_FIRST[n] + st)
                    if st < T:
                        exponential(st)
                    if 0 <= st - 3 < T:
                        o_out(st - 3)

                for i in range(2 * MC):
                    h, m = divmod(i, MC)
                    a.wait_ge(h_ps, 2 * MC * n + i + 1)
                    if n:
                        a.wait_ge(m_ps, T * (n - 1) + HT * (h + 1))
                    rows = min(P, MLP - P * m)
                    a.activation(hT[0:rows, m, HTOK * h:HTOK * (h + 1)], ps[0:rows, 4 + i % 2, :],
                                 ACT.Gelu if n < 2 else ACT.Gelu_apprx_tanh).then_inc(gelu_done, 1)
                    if n == 0:
                        for j in range(2 * T * i // (2 * MC), 2 * T * (i + 1) // (2 * MC)):
                            gates_by_token(T + j)

        @block.gpsimd
        def _(g):
            own = [0]

            def link(ins):
                own[0] += 1
                ins.then_inc(pool_own, 1)
                g.wait_ge(pool_own, own[0])

            for w in (wq, wp, w1):
                ins = g.memset(w[64:P], 0.0)
            link(ins)
            g.sem_inc(pads_set, 1)
            g.wait_ge(ones_set, 1)
            link(g.tensor_scalar(dg[:, 2:3], half_neg[0:R, 0:1], -1.0, None, ALU.mult))

            def add_delta(n, t, gated, done):
                g.wait_ge(gated, T * n + t + 1)
                g.tensor_tensor(x[:, t, :], x[:, t, :], delta[:, t % 4, :], ALU.add).then_inc(done, 1)

            def ln_rstd(i, h):
                t = slice(HT * h, HT * h + HT)
                g.wait_ge(stats_ready, 2 * i + h + 1)
                link(g.tensor_scalar(veps[:, t], mv[:, t, 1], EPS, None, ALU.add))
                g.tensor_tensor(rstd[:, t], veps[:, t], half_neg[:].to_broadcast([P, HT]), ALU.pow).then_inc(rstd_ready, 1)

            for n in range(NB):
                if n != 1:
                    ln_rstd(2 * n, 0)
                ln_rstd(2 * n, 1)
                if n == 0:
                    def pivot_powers():
                        g.wait_ge(diag_ready, 1)
                        g.tensor_tensor(dg[:, 1:2], dg[:, 0:1], dg[:, 2:3], ALU.pow).then_inc(isd_ready, 1)

                    def weigh_values(t):
                        g.wait_ge(exp_done, t + 1)
                        if t >= 2:
                            g.wait_ge(heads_out, t - 1)
                        pr = probs[:, t % 2, 0:HEADS * HEADS].rearrange("p (h k) -> p h k", h=HEADS)
                        values = qkv[:, t, 2 * D:].rearrange("p (k d) -> p d k", k=HEADS)
                        g.tensor_tensor(prod_pv[t % 2].rearrange("p (h d k) -> p h d k", h=HEADS, d=DH),
                                        pr.unsqueeze(2).to_broadcast([P, HEADS, DH, HEADS]),
                                        values.unsqueeze(1).to_broadcast([P, HEADS, DH, HEADS]),
                                        ALU.mult).then_inc(pv_prod, 1)

                    g.wait_ge(v_ps, 2)
                    for t in range(T):
                        g.wait_ge(qkv_sb, t + 1)
                        if t == 1:
                            g.wait_ge(gseq_ps, NB)
                        if t >= 2:
                            g.wait_ge(s_ps, t - 1)
                        q_, k_ = (qkv[:, t, i * D:(i + 1) * D].rearrange("p (h d) -> p d h", h=HEADS) for i in range(2))
                        g.tensor_tensor(prod_slot[t % 2].rearrange("p (d h k) -> p d h k", d=DH, h=HEADS),
                                        q_.unsqueeze(3).to_broadcast([P, DH, HEADS, HEADS]),
                                        k_.unsqueeze(2).to_broadcast([P, DH, HEADS, HEADS]),
                                        ALU.mult).then_inc(qk_prod, 1)
                        if t >= 1:
                            weigh_values(t - 1)
                        if t >= 5:
                            add_delta(n, t - 5, gated1, x_mid)
                        if t == ISD_STEP:
                            pivot_powers()
                    weigh_values(T - 1)
                    if ISD_STEP == T:
                        pivot_powers()
                for h in range(2 if n else 0):
                    g.wait_ge(qkv_sb, T * n + HT * (h + 1))
                    if n == 2:
                        g.wait_ge(o_ps, T)
                    for b in range(B):
                        for q in range(G4):
                            src = qkv[TOK * b:TOK * b + TOK, HT * h:HT * h + HT, 2 * D:].rearrange(
                                "p t (g s d) -> p t g s d", g=4, s=G4)[:, :, :, q, :]
                            dst = vexp[TOK * q:TOK * q + TOK].rearrange(
                                "p (t b) g (s d) -> p t b g s d", b=B, s=G4)[:, HT * h:HT * h + HT, b, :, q, 0:DH]
                            link(g.tensor_copy(dst, src))
                    g.sem_inc(v_spread, 1)
                for t in range(0 if n else T - 5, T):
                    add_delta(n, t, gated1, x_mid)
                    if t == HT:
                        if n == 0:
                            g.wait_ge(x_mid, HT + 1)
                            g.wait_ge(heads_out, T - 1)
                            link(g.memset(hT[R:P, MC - 1, :], 1.0))
                        ln_rstd(2 * n + 1, 0)
                ln_rstd(2 * n + 1, 1)
                if n == 0:
                    g.wait_ge(st_v, 16 * 2 * B)
                    g.wait_ge(gate_ps, T * NB)
                    g.wait_ge(rstd_ready, 4)
                    link(g.memset(vexp[:], 0.0))
                    for q in range(B):
                        link(g.memset(vexp[32 * q:32 * q + 32].rearrange(
                            "p s g (h d) -> p (s g) h d", h=G4)[:, :, q, DH:VW], 1.0))
                for t in range(T):
                    add_delta(n, t, gated2, x_end)
                    if n == 0 and t == HT:
                        ln_rstd(2, 0)


def with_bias_row(w, b):
    n = w.shape[1]
    o = np.zeros((C + 1, 2, n), np.float32)
    o[0:C, 0], o[0:C, 1], o[C, 0] = w[0:C], w[C:D], b
    return o


def kernel(**inputs):
    import concourse.bacc as _bacc
    from concourse import mybir as _mybir
    from concourse.bass_utils import run_bass_kernel_spmd as _run

    a = {k: np.asarray(v) for k, v in inputs.items()}
    names = {"ada": ("L0_cond_ada_w", "L0_cond_ada_b", "L1_cond_w_ada", "L1_cond_b_ada", "L3_cond_W_ada", "L3_cond_b_ada"),
             "qkv": ("L0_cond_qkv_w", "L0_cond_qkv_b", "L1_cond_w_qkv", "L1_cond_b_qkv", "L3_cond_W_qkv", "L3_cond_b_qkv"),
             "proj": ("L0_cond_proj_w", "L0_cond_proj_b", "L1_cond_w_proj", "L1_cond_b_proj", "L3_cond_W_proj", "L3_cond_b_proj"),
             "fc1": ("L0_cond_fc1_w", "L0_cond_fc1_b", "L1_cond_w1", "L1_cond_b1", "L3_cond_W_fc1", "L3_cond_b_fc1"),
             "fc2": ("L0_cond_fc2_w", "L0_cond_fc2_b", "L1_cond_w2", "L1_cond_b2", "L3_cond_W_fc2", "L3_cond_b_fc2")}
    packed = {k: np.stack([with_bias_row(a[v[2 * i]], a[v[2 * i + 1]]) for i in range(NB)])
              for k, v in names.items() if k != "fc2"}
    fc2 = np.zeros((NB, MC * P, D), np.float32)
    for i in range(NB):
        fc2[i, 0:MLP], fc2[i, MLP] = a[names["fc2"][2 * i]], a[names["fc2"][2 * i + 1]]
    fc2 = np.ascontiguousarray(fc2.reshape(NB, MC, P, D).transpose(0, 2, 1, 3))
    cond = a["cond_1152"]
    cond_t = np.ascontiguousarray(cond.T.reshape(2, C, SEQ).transpose(1, 0, 2))
    gbs = np.stack([np.tile(a[k], HC) for k in ("L1_cond_qn_g", "L1_cond_qn_b", "L1_cond_kn_g", "L1_cond_kn_b")], 1)
    iu, ju = np.triu_indices(R, k=1)
    at = np.zeros((R, R), np.int64)
    at[iu, ju] = at[ju, iu] = np.arange(len(iu))
    rot = with_bias_row(a["L2_cond_W"][at.reshape(-1)].T, a["L2_cond_b"][at.reshape(-1)])
    pm = a["L2_cond_P"]
    f = np.float32
    scale = 2.0 ** -SQUARINGS
    ij = np.sign(np.arange(R)[None] - np.arange(R)[:, None])
    arrays = {
        "x_in": a["x"].reshape(SEQ * TOK, D), "cond_t": cond_t, "ada_w": packed["ada"], "qkv_w": packed["qkv"],
        "proj_w": packed["proj"], "fc1_w": packed["fc1"], "fc2_w": fc2, "qk_gb": gbs, "rot_w": rot,
        "p_in": np.ascontiguousarray(pm.reshape(2, C, R).transpose(1, 0, 2)), "pt_in": np.ascontiguousarray(pm.T),
        "eye": np.eye(P, dtype=f),
        "head_mask": (np.arange(C)[:, None] // DH == np.arange(HC)[None]).astype(f),
        "below": -(np.arange(R)[:, None] > np.arange(R)[None]).astype(f),
        "seq_mask": np.repeat(np.eye(SEQ, dtype=f), TOK, axis=1),
        "skew": (np.concatenate([ij, ij]) * scale).astype(f),
    }
    nc = _bacc.Bacc("TRN2", target_bir_lowering=False, num_devices=1)
    args, fed = [], {}
    for name, v in arrays.items():
        v = np.ascontiguousarray(v)
        fed[name + "_dram"] = v
        args.append(nc.dram_tensor(name + "_dram", v.shape, _mybir.dt.from_np(v.dtype), kind="ExternalInput").ap())
    args.append(nc.dram_tensor("out_dram", (SEQ * TOK, D), F32, kind="ExternalOutput").ap())
    fused_blocks(nc, *args)
    r = _run(nc, [fed], core_ids=[0])
    return r.results[0]["out_dram"].reshape(SEQ, TOK, D)
```
